# Optimizing a Trainium2 kernel written in Bass

```python
import numpy as np
import jax
import jax.numpy as jnp

def _softmax(x, axis=-1):
    return jax.nn.softmax(x, axis=axis)

def _gelu(x):
    return jax.nn.gelu(x, approximate=True)

def _silu(x):
    return jax.nn.silu(x)

def _sigmoid(x):
    return jax.nn.sigmoid(x)

def _layernorm(x, axis=-1, eps=1e-05):
    m = jnp.mean(x, axis=axis, keepdims=True)
    v = jnp.var(x, axis=axis, keepdims=True)
    return (x - m) / jnp.sqrt(v + eps)

def _scatter_add(tgt, idx, src, axis=0):
    return tgt.at[idx].add(src)

def _segment_sum(src, seg, n):
    return jax.ops.segment_sum(src, seg, n)
kernel_name = 'mk_seq_preln_d1_jaxref_r8_f6f91c'

def setup_inputs(seed: int=0):
    np.random.seed(seed)
    _w = jnp.asarray

    def _L0_attn_setup():
        import jax, jax.numpy as jnp
        import numpy as np
        NUM_HEAD = 16
        D_Q = 64
        D_KV = 64
        ROPE_BASE = 10000.0

        def _cos_sin(seq_len, dim):
            pos = jnp.arange(seq_len, dtype=jnp.float32)[:, None]
            ids = jnp.arange(dim // 2, dtype=jnp.float32)
            theta = ROPE_BASE ** (-2.0 * ids) / (dim // 2)
            r = pos * theta[None, :]
            return (jnp.cos(r), jnp.sin(r))

        def _rope(x, cos, sin):
            b, s, d = x.shape
            xv = x.reshape(b, s, d // 2, 2)
            x0, x1 = (xv[..., 0], xv[..., 1])
            out = jnp.stack([x0 * cos - x1 * sin, x1 * cos + x0 * sin], axis=-1)
            return out.reshape(b, s, d)
        key = jax.random.key(seed)
        ks = jax.random.split(key, 10)
        d_model, d_q, d_kv = (128, D_Q, D_KV)
        b, s = (2, 256)
        w = lambda k, i, o: jax.random.normal(k, (i, o), dtype=jnp.float32) * 0.02
        return {'x': jax.random.normal(ks[0], (b, s, d_model), dtype=jnp.float32), 'Wd_q_w': w(ks[1], d_model, d_q), 'Wd_q_b': jnp.zeros((d_q,), jnp.float32), 'Wu_q_w': w(ks[2], d_q, d_model), 'Wu_q_b': jnp.zeros((d_model,), jnp.float32), 'Wq_r_w': w(ks[3], d_q, d_model), 'Wq_r_b': jnp.zeros((d_model,), jnp.float32), 'Wk_r_w': w(ks[4], d_model, d_model), 'Wk_r_b': jnp.zeros((d_model,), jnp.float32), 'Wd_kv_w': w(ks[5], d_model, d_kv), 'Wd_kv_b': jnp.zeros((d_kv,), jnp.float32), 'Wu_k_w': w(ks[6], d_kv, d_model), 'Wu_k_b': jnp.zeros((d_model,), jnp.float32), 'Wu_v_w': w(ks[7], d_kv, d_model), 'Wu_v_b': jnp.zeros((d_model,), jnp.float32), 'Wo_w': w(ks[8], d_model, d_model), 'Wo_b': jnp.zeros((d_model,), jnp.float32)}
    _L0_attn_in = _L0_attn_setup()

    def _L0_ffn_setup():
        import jax, jax.numpy as jnp
        import numpy as np
        B, S, D_MODEL, D_FF, N_EXPERTS, TOP_K = (4, 128, 128, 512, 24, 2)
        key = jax.random.key(seed)
        ks = jax.random.split(key, 7)
        sd = 1.0 / np.sqrt(D_MODEL)
        sf = 1.0 / np.sqrt(D_FF)
        return {'x': jax.random.normal(ks[0], (B, S, D_MODEL), jnp.float32), 'gate_w': jax.random.uniform(ks[1], (D_MODEL, N_EXPERTS), jnp.float32, -sd, sd), 'gate_b': jax.random.uniform(ks[2], (N_EXPERTS,), jnp.float32, -sd, sd), 'w1': jax.random.uniform(ks[3], (N_EXPERTS, D_MODEL, D_FF), jnp.float32, -sd, sd), 'b1': jax.random.uniform(ks[4], (N_EXPERTS, D_FF), jnp.float32, -sd, sd), 'w2': jax.random.uniform(ks[5], (N_EXPERTS, D_FF, D_MODEL), jnp.float32, -sf, sf), 'b2': jax.random.uniform(ks[6], (N_EXPERTS, D_MODEL), jnp.float32, -sf, sf)}
    _L0_ffn_in = _L0_ffn_setup()
    _d = {'L0_attn_x': _L0_attn_in['x'], 'L0_attn_Wd_q_w': _L0_attn_in['Wd_q_w'], 'L0_attn_Wd_q_b': _L0_attn_in['Wd_q_b'], 'L0_attn_Wu_q_w': _L0_attn_in['Wu_q_w'], 'L0_attn_Wu_q_b': _L0_attn_in['Wu_q_b'], 'L0_attn_Wq_r_w': _L0_attn_in['Wq_r_w'], 'L0_attn_Wq_r_b': _L0_attn_in['Wq_r_b'], 'L0_attn_Wk_r_w': _L0_attn_in['Wk_r_w'], 'L0_attn_Wk_r_b': _L0_attn_in['Wk_r_b'], 'L0_attn_Wd_kv_w': _L0_attn_in['Wd_kv_w'], 'L0_attn_Wd_kv_b': _L0_attn_in['Wd_kv_b'], 'L0_attn_Wu_k_w': _L0_attn_in['Wu_k_w'], 'L0_attn_Wu_k_b': _L0_attn_in['Wu_k_b'], 'L0_attn_Wu_v_w': _L0_attn_in['Wu_v_w'], 'L0_attn_Wu_v_b': _L0_attn_in['Wu_v_b'], 'L0_attn_Wo_w': _L0_attn_in['Wo_w'], 'L0_attn_Wo_b': _L0_attn_in['Wo_b'], 'L0_ffn_gate_w': _L0_ffn_in['gate_w'], 'L0_ffn_gate_b': _L0_ffn_in['gate_b'], 'L0_ffn_w1': _L0_ffn_in['w1'], 'L0_ffn_b1': _L0_ffn_in['b1'], 'L0_ffn_w2': _L0_ffn_in['w2'], 'L0_ffn_b2': _L0_ffn_in['b2']}
    _x0 = _d['L0_attn_x']
    _d['L0_attn_x'] = jax.random.normal(jax.random.fold_in(jax.random.key(seed), 1), (16, 256, 128), dtype=_x0.dtype)
    del _x0
    return _d

def reference(L0_attn_x, L0_attn_Wd_q_w, L0_attn_Wd_q_b, L0_attn_Wu_q_w, L0_attn_Wu_q_b, L0_attn_Wq_r_w, L0_attn_Wq_r_b, L0_attn_Wk_r_w, L0_attn_Wk_r_b, L0_attn_Wd_kv_w, L0_attn_Wd_kv_b, L0_attn_Wu_k_w, L0_attn_Wu_k_b, L0_attn_Wu_v_w, L0_attn_Wu_v_b, L0_attn_Wo_w, L0_attn_Wo_b, L0_ffn_gate_w, L0_ffn_gate_b, L0_ffn_w1, L0_ffn_b1, L0_ffn_w2, L0_ffn_b2):

    def _L0_attn_ref(x, Wd_q_w, Wd_q_b, Wu_q_w, Wu_q_b, Wq_r_w, Wq_r_b, Wk_r_w, Wk_r_b, Wd_kv_w, Wd_kv_b, Wu_k_w, Wu_k_b, Wu_v_w, Wu_v_b, Wo_w, Wo_b):
        import jax, jax.numpy as jnp
        import numpy as np
        NUM_HEAD = 16
        D_Q = 64
        D_KV = 64
        ROPE_BASE = 10000.0

        def _cos_sin(seq_len, dim):
            pos = jnp.arange(seq_len, dtype=jnp.float32)[:, None]
            ids = jnp.arange(dim // 2, dtype=jnp.float32)
            theta = ROPE_BASE ** (-2.0 * ids) / (dim // 2)
            r = pos * theta[None, :]
            return (jnp.cos(r), jnp.sin(r))

        def _rope(x, cos, sin):
            b, s, d = x.shape
            xv = x.reshape(b, s, d // 2, 2)
            x0, x1 = (xv[..., 0], xv[..., 1])
            out = jnp.stack([x0 * cos - x1 * sin, x1 * cos + x0 * sin], axis=-1)
            return out.reshape(b, s, d)
        b, s, d_model = x.shape
        h = NUM_HEAD
        hd = d_model // h
        scale = jnp.sqrt(jnp.float32(h + D_KV + D_Q))

        def heads(t):
            return t.reshape(b, s, h, hd).transpose(0, 2, 1, 3)
        cos, sin = _cos_sin(s, d_model)
        ct_q = x @ Wd_q_w + Wd_q_b
        qt_c = heads(ct_q @ Wu_q_w + Wu_q_b)
        qt_r = heads(_rope(ct_q @ Wq_r_w + Wq_r_b, cos, sin))
        query = qt_c + qt_r
        ct_kv = x @ Wd_kv_w + Wd_kv_b
        kt_c = heads(ct_kv @ Wu_k_w + Wu_k_b)
        kt_r = heads(_rope(x @ Wk_r_w + Wk_r_b, cos, sin))
        key = kt_c + kt_r
        value = heads(ct_kv @ Wu_v_w + Wu_v_b)
        attn = jnp.einsum('bhqd,bhkd->bhqk', query, key) / scale
        attn = jax.nn.softmax(attn, axis=-1)
        out = jnp.einsum('bhqk,bhkd->bhqd', attn, value)
        out = out.transpose(0, 2, 1, 3).reshape(b, s, d_model)
        return out @ Wo_w + Wo_b

    def _L0_ffn_ref(x, gate_w, gate_b, w1, b1, w2, b2):
        import jax, jax.numpy as jnp
        import numpy as np
        B, S, D_MODEL, D_FF, N_EXPERTS, TOP_K = (4, 128, 128, 512, 24, 2)
        b, s, d = x.shape
        xt = x.reshape(-1, d)
        t = xt.shape[0]
        scores = xt @ gate_w + gate_b
        topv, topi = jax.lax.top_k(scores, TOP_K)
        gates = jax.nn.softmax(topv, axis=-1)
        cw = jnp.zeros((t, N_EXPERTS), x.dtype).at[jnp.arange(t)[:, None], topi].add(gates)
        out = jnp.zeros_like(xt)
        for e in range(N_EXPERTS):
            h = jax.nn.gelu(xt @ w1[e] + b1[e], approximate=False)
            y = h @ w2[e] + b2[e]
            out = out + cw[:, e:e + 1] * y
        return out.reshape(b, s, d)
    x = L0_attn_x
    x = x + _L0_attn_ref(_layernorm(x, axis=-1), L0_attn_Wd_q_w, L0_attn_Wd_q_b, L0_attn_Wu_q_w, L0_attn_Wu_q_b, L0_attn_Wq_r_w, L0_attn_Wq_r_b, L0_attn_Wk_r_w, L0_attn_Wk_r_b, L0_attn_Wd_kv_w, L0_attn_Wd_kv_b, L0_attn_Wu_k_w, L0_attn_Wu_k_b, L0_attn_Wu_v_w, L0_attn_Wu_v_b, L0_attn_Wo_w, L0_attn_Wo_b)
    x = x + _L0_ffn_ref(_layernorm(x, axis=-1), L0_ffn_gate_w, L0_ffn_gate_b, L0_ffn_w1, L0_ffn_b1, L0_ffn_w2, L0_ffn_b2)
    return x

_drawn_inputs = setup_inputs


def setup_inputs(seed=0):
    import zlib

    import numpy as np

    out = dict(_drawn_inputs(seed))
    spreads = {'L0_attn_Wd_q_b': (0.0, 0.8),
     'L0_attn_Wu_q_b': (0.0, 0.8),
     'L0_attn_Wq_r_b': (0.0, 0.8),
     'L0_attn_Wk_r_b': (0.0, 0.8),
     'L0_attn_Wd_kv_b': (0.0, 0.768),
     'L0_attn_Wu_k_b': (0.0, 0.8),
     'L0_attn_Wu_v_b': (0.0, 0.1),
     'L0_attn_Wo_b': (0.0, 0.1)}
    factors = {'L0_attn_Wd_q_w': 8.0,
     'L0_attn_Wu_q_w': 8.0,
     'L0_attn_Wq_r_w': 8.0,
     'L0_attn_Wk_r_w': 8.0,
     'L0_attn_Wd_kv_w': 8.0,
     'L0_attn_Wu_k_w': 8.0,
     'L0_attn_Wu_v_w': 6.039,
     'L0_ffn_b1': 4.377,
     'L0_ffn_b2': 3.14}
    for name, (base, spread) in spreads.items():
        noise = np.random.default_rng([zlib.crc32(name.encode()), seed]).standard_normal(out[name].shape)
        drawn = base * np.exp(spread * noise) if base else spread * noise
        out[name] = jnp.asarray(drawn.astype(out[name].dtype))
    for name, factor in factors.items():
        out[name] = (out[name] * factor).astype(out[name].dtype)
    return out
```

```python
from contextlib import ExitStack

import numpy as np
import concourse.bass as bass
from concourse import mybir

F32 = mybir.dt.float32
BF16 = mybir.dt.bfloat16
U32 = mybir.dt.uint32
I32 = mybir.dt.int32
ALU = mybir.AluOpType
ACT = mybir.ActivationFunctionType
AX = mybir.AxisListType

P = 128
NB, S, D = 16, 256, 128
H, HD = 16, 8
DQ = 64
NE, DF, TOPK = 24, 512, 2
FC = DF // P
QT = S // P
T = NB * S
NT = T // P
NG = 4
NQ = H // NG
NP = 3
QW = NG * HD
KR = NP * NP * HD
SCALE = float(H + 2 * DQ) ** -0.5
EPS = 1e-5
REG = T + P
ROWW = D + 4
TILES = (TOPK * T + NE * (P - 1)) // P
UNROLL = 4
TILES = -(-TILES // UNROLL) * UNROLL
CHUNK = 4
PADT, PLAN = 2, 15

C_ID, C_TRI, C_ONE = 0, P, 2 * P
C_COS = 3 * P
C_SIN = C_COS + 2 * S
C_EXP = C_SIN + 2 * S
C_BASE = C_EXP + NE
C_PART = C_BASE + NE
C_PAD = C_PART + 1
NCONST = C_PAD + 1

W_D = 0
W_U = W_D + P
W_KR = W_U + 5 * P
W_O = W_KR + 2 * P
W_G = W_O + P
W_B1 = W_G + NE
W_B = W_B1 + NE * FC
NW = W_B + 7
R_V, R_O, R_G, R_B2 = 0, P, 2 * P, 2 * P + NE
NR = R_B2 + NE * D


def by_dimension():
    return np.arange(D).reshape(H, HD).T.reshape(-1)


def shape_constants():
    c = np.zeros((P, NCONST), np.float32)
    p = np.arange(P)
    c[:, C_ID:C_ID + P] = np.eye(P)
    c[:, C_TRI:C_TRI + P] = p[:, None] < p[None, :]
    c[:, C_ONE:C_ONE + P] = 1.0
    ids = np.arange(D // 2, dtype=np.float32)
    theta = (np.float32(10000.0) ** (np.float32(-2.0) * ids) / np.float32(D // 2)).astype(np.float32)
    angle = (np.arange(S, dtype=np.float32)[:, None] * theta[None, :]).astype(np.float32)
    cos = np.repeat(np.cos(angle).astype(np.float32).T, 2, axis=0)
    sin = np.repeat(np.sin(angle).astype(np.float32).T, 2, axis=0)
    sin[0::2] *= -1.0
    cos, sin = cos[by_dimension()], sin[by_dimension()]
    for i in range(2):
        c[:, C_COS + i * S:C_COS + (i + 1) * S] = cos
        c[:, C_SIN + i * S:C_SIN + (i + 1) * S] = sin
    c[:, C_EXP:C_EXP + NE] = np.arange(NE)
    c[:, C_BASE:C_BASE + NE] = np.arange(NE) * REG
    c[:, C_PART] = p
    c[:, C_PAD] = TOPK * T
    return c


def result_rows():
    p, t, k = np.ogrid[0:P, 0:NT, 0:TOPK]
    return (TOPK * (P * t + p) + k).astype(np.uint32).reshape(P, NT * TOPK)


def build(nc, x_in, w_in, r_in, w1_in, w2_in, c_in, rows_in, out):
    with ExitStack() as ctx:
        def sb(name, shape, dt=F32):
            return ctx.enter_context(nc.sbuf_tensor(name, shape, dt))

        def ps(name, shape):
            return ctx.enter_context(nc.psum_tensor(name, shape, F32))

        def sem(name):
            return ctx.enter_context(nc.semaphore(name))

        dispatched = nc.dram_tensor("dispatched", ((NE + 1) * REG, ROWW), F32, kind="Internal").ap()
        parts_out = nc.dram_tensor("parts_out", (2, NP, D * S), BF16, kind="Internal").ap()
        results = nc.dram_tensor("results", (TOPK * T, D), F32, kind="Internal").ap()

        x_all = sb("x_all", [P, NT, D])
        consts = sb("consts", [P, NCONST])
        wts = sb("wts", [P, NW])
        brow = sb("brow", [P, NR])
        w1 = sb("w1", [P, NE, DF])
        w2 = sb("w2", [P, NE, FC, D])
        rows = sb("rows", [P, NT, TOPK], U32)
        top_all = sb("top_all", [P, NT, TOPK])
        tri16 = sb("tri16", [P, P], BF16)
        one16 = sb("one16", [P, P], BF16)
        ident16 = sb("ident16", [P, P], BF16)
        powers = sb("powers", [P, 2, QT])
        biasqk = sb("biasqk", [P, 2, S])

        st1 = sb("st1", [P, QT, 6])
        mv1 = sb("mv1", [P, QT, 2])
        ve1 = sb("ve1", [P, QT])
        rstd1 = sb("rstd1", [P, QT])
        xn = sb("xn", [P, QT, D])
        xnT = sb("xnT", [P, S])
        ct = sb("ct", [P, S])
        turn1 = sb("turn1", [P, 2 * S])
        turn2 = sb("turn2", [P, 2 * S])
        qk = sb("qk", [P, 2 * S])
        rest = sb("rest", [P, 2 * S])
        qkp = sb("qkp", [P, 2, NP, S], BF16)
        vst = sb("vst", [P, QT, D])
        vm = [sb(f"vm{i}", [P, QT, NQ, NG * 2 * QW]) for i in range(2)]
        mx = [sb(f"mx{i}", [P, QT, NG]) for i in range(2)]
        mrest = sb("mrest", [P, QT, NG])
        mxp = [sb(f"mxp{i}", [P, QT, NP, NG], BF16) for i in range(2)]
        mrow = [sb(f"mrow{i}", [NP * NG, S], BF16) for i in range(2)]
        pr = [sb(f"pr{i}", [P, NG, QT, S]) for i in range(2)]
        sums = sb("sums", [P, S])
        outT = sb("outT", [P, S])
        spread = w2[:, :, :, :].rearrange("p e c d -> p (e c d)")[:, 0:2 * H * S].bitcast(BF16).rearrange(
            "p (i z h s) -> p i z h s", i=2, z=2, h=H)
        qrows = [spread[:, i, 0, :, :] for i in range(2)]
        krows = [spread[:, i, 1, :, :] for i in range(2)]

        st2 = sb("st2", [P, QT, 6])
        mv2 = sb("mv2", [P, QT, 2])
        ve2 = sb("ve2", [P, QT])
        rstd2 = sb("rstd2", [P, QT])
        pay = sb("pay", [P, QT, TOPK, ROWW])
        xn2T = sb("xn2T", [P, S])
        sc = sb("sc", [P, QT, NE])
        top8 = sb("top8", [P, QT, 8])
        arg8 = sb("arg8", [P, QT, 8], U32)
        argf = sb("argf", [P, QT, TOPK])
        oh = sb("oh", [P, QT * TOPK, NE])
        chosen = sb("chosen", [P, QT, NE], BF16)
        rk = [sb(f"rk{i}", [P, QT + 1, NE]) for i in range(2)]
        ohrk = sb("ohrk", [P, QT * TOPK, NE])
        posf = sb("posf", [P, QT * TOPK])
        pos = sb("pos", [P, QT * TOPK], U32)

        count = sb("count", [P, 3, NE])
        counti = sb("counti", [P, NE], I32)
        past = sb("past", [P, 2, NE])
        place_ = sb("place_", [P, 4])
        table = sb("table", [1, 2, P], I32)
        ends = sb("ends", [1, NE], I32)
        padt = sb("padt", [P, ROWW])
        gates = sb("gates", [P, NT, TOPK])
        gtmp = sb("gtmp", [P, 2, NT])
        tin = [sb(f"tin{i}", [P, ROWW]) for i in range(UNROLL)]
        ridx = [sb(f"ridx{i}", [P, 1], U32) for i in range(UNROLL)]
        tT = [sb(f"tT{i}", [P, P]) for i in range(2)]
        w1s = [sb(f"w1s{i}", [P, DF]) for i in range(2)]
        hT = [pr[i][:, :, 0, 0:P] for i in range(2)]
        yo = [sb(f"yo{i}", [P, D]) for i in range(UNROLL)]

        s1 = [ps(f"s1_{i}", [P, QT, S]) for i in range(2)]
        s2 = [ps(f"s2_{i}", [P, QT, S]) for i in range(2)]
        pv = [ps(f"pv{i}", [P, 2, S]) for i in range(2)]
        pa = ps("pa", [P, 512])
        pb = ps("pb", [P, 512])

        tps = [pa, pb]
        hps = s2
        yps = s1

        def own_columns(i, first):
            v = vm[i][:, :, :, :]
            return bass.AP(tensor=v.tensor, offset=v.offset + first,
                           ap=[v.ap[0], [NG * 2 * QW, QT * NQ], [2 * QW + HD, NG], [1, HD]])

        ident = consts[:, C_ID:C_ID + P]
        mturn = pa[0:NP * NG, 0:S]
        SPREAD = 16 * (NP + 1)

        ld_x0, ld_c, ld_w, ld_x, ld_r, ld_w1, ld_w2 = (sem(n) for n in (
            "ld_x0", "ld_c", "ld_w", "ld_x", "ld_r", "ld_w1", "ld_w2"))
        set_v, set_p, bias_st = sem("set_v"), sem("set_p"), sem("bias_st")
        s1_full, max_done, split_st, split_done = sem("s1_full"), sem("max_done"), sem("split_st"), sem("split_done")
        mt_full, mt_done = sem("mt_full"), sem("mt_done")
        sums_done, inv_st = sem("sums_done"), sem("inv_st")
        max_in = [sem(f"max_in{j}") for j in range(NQ)]
        part1_done, rest_done, part2_done, part3_done = sem("part1_done"), sem("rest_done"), sem("part2_done"), sem("part3_done")
        stored_parts, spread_in, neg_st = sem("stored_parts"), sem("spread_in"), sem("neg_st")
        s2_full, exp_done, pv_full, norm_st = sem("s2_full"), sem("exp_done"), sem("pv_full"), sem("norm_st")
        ln1_st, rstd1_st, xn_done, xb_done = sem("ln1_st"), sem("rstd1_st"), sem("xn_done"), sem("xb_done")
        xT_full, xT_done, ct_full, ct_done = sem("xT_full"), sem("xT_done"), sem("ct_full"), sem("ct_done")
        r1_full, r1_done, r2_full, r2_done = sem("r1_full"), sem("r1_done"), sem("r2_full"), sem("r2_done")
        turn_st, qk_full, qk_done = sem("turn_st"), sem("qk_full"), sem("qk_done")
        v_full, vst_done, v_done = sem("v_full"), sem("vst_done"), sem("v_done")
        wo_full, x2_done, ln2_st, rstd2_st, xn2_done = sem("wo_full"), sem("x2_done"), sem("ln2_st"), sem("rstd2_st"), sem("xn2_done")
        x2T_full, x2T_done, gate_full, sc_done = sem("x2T_full"), sem("x2T_done"), sem("gate_full"), sem("sc_done")
        top_st, chosen_done, rank_full, rank_done = sem("top_st"), sem("chosen_done"), sem("rank_full"), sem("rank_done")
        pos_st, idx_done, sent = sem("pos_st"), sem("idx_done"), sem("sent")
        plan_st, table_full, table_done, pads_out = sem("plan_st"), sem("table_full"), sem("table_done"), sem("pads_out")
        gate_st, gexp_done = sem("gate_st"), sem("gexp_done")
        tile_in = [sem(f"tile_in{i}") for i in range(UNROLL)]
        tile_out = [sem(f"tile_out{i}") for i in range(UNROLL)]
        tT_full, tT_done, ridx_done, w1_done = sem("tT_full"), sem("tT_done"), sem("ridx_done"), sem("w1_done")
        h_full, gelu_done, y_full, y_done = sem("h_full"), sem("gelu_done"), sem("y_full"), sem("y_done")
        back = [sem(f"back{i}") for i in range(NT // CHUNK)]
        weighed, summed, final, stored = sem("weighed"), sem("summed"), sem("final"), sem("stored")

        def wait(eng, s, value):
            if isinstance(value, int) and value <= 0:
                return
            eng.wait_ge(s, value)

        def known_count(eng, value):
            return value if isinstance(value, int) else eng.compute_val(value)

        def wait_apart(eng, s, value):
            if isinstance(value, int):
                wait(eng, s, value)
                return
            value = known_count(eng, value)
            eng.wait_ge(ld_c, 16)
            eng.wait_ge(s, value)

        def pipeline(eng, step):
            step(0, 0)
            step(1, 1)
            with eng.Fori(0, (NB - 4) // 2) as i:
                for odd in range(2):
                    step(i * 2 + (2 + odd), odd)
            for b in range(NB - 2, NB + 2):
                step(b, b % 2)

        def tile_pipeline(eng, step):
            turns = TILES // UNROLL
            for k in range(UNROLL):
                step(0, k)
            with eng.Fori(1, turns - 1) as turn:
                for k in range(UNROLL):
                    step(turn, k)
            for k in range(UNROLL + 1):
                step(turns - 1 + k // UNROLL, k % UNROLL)

        def chunk(c):
            return w1[:, 2 * c:2 * c + 2, :].rearrange("p a f -> p (a f)").rearrange("p (t k d) -> p t k d", t=CHUNK, k=TOPK)

        class Tile:
            def __init__(self, turn, k, ahead):
                self.turn, self.slot = turn + (k + ahead) // UNROLL, (k + ahead) % UNROLL
                self.n = self.turn * UNROLL + self.slot
                self.pair = self.slot % 2
                self.real = not isinstance(self.n, int) or 0 <= self.n < TILES

        def expert_of(eng, tile):
            return eng.value_load(table[0:1, 0, bass.ds(tile.n, 1)], min_val=0, max_val=NE - 1)

        class Held:
            def __init__(self, b):
                known = isinstance(b, int)
                self.attend, self.lead, self.project = (not known or b + i < NB for i in range(3))
                self.route, self.send = (not known or 0 <= b - i < NB for i in (1, 2))

        def leading(b, s, q):
            return (b, s, q + 2) if q < 2 else (b + 1, 1 - s, q - 2)

        def turning(b, s, q):
            return (b, s, q + 1) if q < NQ - 1 else (b + 1, 1 - s, 0)

        block = ctx.enter_context(nc.Block())

        @block.sync
        def _(sp):
            xv = x_in.rearrange("p (t d) -> p t d", t=NT)
            sp.dma_start(x_all[:, 0:2 * QT, :], xv[:, 0:2 * QT, :]).then_inc(ld_x0, 16)
            sp.dma_start(consts[:, :], c_in).then_inc(ld_c, 16)
            sp.dma_start(wts[:, :], w_in).then_inc(ld_w, 16)
            sp.dma_start(brow[:, :], r_in.partition_broadcast(P)).then_inc(ld_r, 16)
            sp.dma_start(x_all[:, 2 * QT:NT, :], xv[:, 2 * QT:NT, :]).then_inc(ld_x, 16)
            sp.dma_start(rows[:, :, :], rows_in.rearrange("p (t k) -> p t k", t=NT)).then_inc(ld_x, 16)
            w1v = w1_in.rearrange("p (e f) -> p e f", e=NE)
            w2v = w2_in.rearrange("p (e c d) -> p e c d", e=NE, c=FC)

            def spread_rows(m, s):
                done, read, scored = (known_count(sp, n) for n in ((m + 1), m * SPREAD, (m - 1) * H))
                stores = known_count(sp, (m + 1) * 16)
                wait(sp, part3_done, done)
                wait(sp, spread_in, read)
                sp.dma_start(parts_out.rearrange("z i (p s) -> p (z i) s", s=S),
                             qkp[:, :, :, :].rearrange("p z i s -> p (z i) s")).then_inc(stored_parts, 16)
                wait(sp, stored_parts, stores)
                wait(sp, s2_full, scored)
                q, k = parts_out[0], parts_out[1]
                w = NP * HD
                for i in range(NP):
                    sp.dma_start(qrows[s][w * i:w * (i + 1), :, :],
                                 q[i][None, :].broadcast_to([NP, D * S])).then_inc(spread_in, 16)
                sp.dma_start(krows[s][0:KR, :, :],
                             k.rearrange("i f -> (i f)")[None, :].broadcast_to([NP, NP * D * S])).then_inc(spread_in, 16)

            def add_maxima(m, s, j):
                wait(sp, mt_done, m * NQ + (j + 1))
                sp.dma_start(qrows[s][KR:KR + NP, NG * j:NG * j + NG, :], mrow[j % 2][:, :]).then_inc(max_in[j], 16)

            def step(b, s):
                held = Held(b)
                for q in range(NQ):
                    if held.lead if q == NQ - 1 else held.attend:
                        add_maxima(*turning(b, s, q))
                if not isinstance(b, int):
                    e = (b - 2) * (NE // (NB - 4))
                    sp.dma_start(w1[:, bass.ds(e, NE // (NB - 4)), :], w1v[:, bass.ds(e, NE // (NB - 4)), :]).then_inc(ld_w1, 16)
                if held.project:
                    spread_rows(b + 2, s)

            sp.wait_ge(neg_st, 1)
            spread_rows(0, 0)
            spread_rows(1, 1)
            add_maxima(0, 0, 0)
            free = 2 * H * S // DF
            sp.dma_start(w2[:, free:NE, :, :], w2v[:, free:NE, :, :]).then_inc(ld_w2, 16)
            pipeline(sp, step)
            sp.wait_ge(s2_full, NB * H)
            for e in range(0, free, 4):
                sp.dma_start(w2[:, e:e + 4, :, :], w2v[:, e:e + 4, :, :]).then_inc(ld_w2, 16)
            sp.wait_ge(plan_st, PADT)
            sp.dma_start(dispatched[NE * REG:NE * REG + P, :], padt[:, :]).then_inc(pads_out, 16)
            sp.wait_ge(table_done, 2)
            with sp.Fori(0, NE) as e:
                end = sp.value_load(ends[0:1, bass.ds(e, 1)], min_val=0, max_val=NE * REG - P)
                sp.dma_start(dispatched[bass.ds(end, P), :], padt[:, :]).then_inc(pads_out, 16)
            sp.wait_ge(pads_out, 16 * (NE + 1))
            sp.wait_ge(sent, QT * TOPK * 16 * NB)

            def step(turn, k):
                t = Tile(turn, k, 0)
                if not t.real:
                    return
                first = sp.value_load(table[0:1, 1, bass.ds(t.n, 1)], min_val=0, max_val=NE * REG)
                wait(sp, tT_full, t.n - (UNROLL - 1))
                wait(sp, ridx_done, t.n - (UNROLL - 1))
                sp.dma_start(tin[t.slot][:, :], dispatched[bass.ds(first, P), :]).then_inc(tile_in[t.slot], 16)

            tile_pipeline(sp, step)
            for u in range(UNROLL):
                sp.wait_ge(tile_out[u], 16 * (TILES // UNROLL))
            sp.wait_ge(w1_done, TILES)
            rv = results.rearrange("(t p k) d -> p t (k d)", p=P, k=TOPK)
            for c in range(NT // CHUNK):
                sp.dma_start(chunk(c).rearrange("p t k d -> p t (k d)"), rv[:, c * CHUNK:(c + 1) * CHUNK, :]).then_inc(back[c], 16)
            ov = out.rearrange("p (t d) -> p t d", t=NT)
            for c in range(NT // CHUNK):
                sp.wait_ge(final, c + 1)
                sp.dma_start(ov[:, c * CHUNK:(c + 1) * CHUNK, :], x_all[:, c * CHUNK:(c + 1) * CHUNK, :]).then_inc(stored, 16)
            sp.wait_ge(stored, 16 * (NT // CHUNK))

        @block.tensor
        def _(pe):
            def pass1(m, s, h):
                if h == 0:
                    wait(pe, spread_in, (m + 1) * SPREAD)
                wait(pe, max_done, m * H + (h - 1))
                for t in range(QT):
                    mm = nc.tensor.matmul(s1[h % 2][:, t, :], qrows[s][0:KR, h, t * P:(t + 1) * P],
                                          krows[s][0:KR, h, :], start=True, stop=True)
                mm.then_inc(s1_full, 1)

            def turn_max(m, s, j):
                wait(pe, split_done, m * NQ + (j + 1))
                wait(pe, mt_done, m * NQ + j)
                for t in range(QT):
                    mm = nc.tensor.matmul(mturn[:, t * P:(t + 1) * P], mxp[j % 2][:, t, :, :].rearrange("p i g -> p (i g)"),
                                          ident16[:, :], start=True, stop=True)
                mm.then_inc(mt_full, 1)

            def pass2(b, s, h):
                if h % NG == 0:
                    wait(pe, max_in[h // NG], (b + 1) * 16)
                wait(pe, exp_done, b * H + (h - 1))
                for t in range(QT):
                    mm = nc.tensor.matmul(s2[h % 2][:, t, :], krows[s][0:KR + NP, h, t * P:(t + 1) * P],
                                          qrows[s][0:KR + NP, h, :], start=True, stop=True)
                mm.then_inc(s2_full, 1)

            def weigh(b, s, h):
                j, g = divmod(h, NG)
                if h == 0:
                    wait(pe, v_done, b + 1)
                    wait(pe, norm_st, b - 1)
                wait(pe, exp_done, b * H + (h + 1))
                r = slice(2 * QW * (j % 2), 2 * QW * (j % 2 + 1))
                for t in range(QT):
                    mm = nc.tensor.matmul(pv[s][r, j // 2, :], vm[s][:, t, j, 2 * QW * g:2 * QW * (g + 1)], pr[j % 2][:, g, t, :],
                                          start=(g == 0 and t == 0), stop=(g == NG - 1 and t == QT - 1), skip_group_check=True)
                mm.then_inc(pv_full, 1)

            def x_turned(b):
                wait(pe, xn_done, b + 1)
                wait(pe, vst_done, b)
                for t in range(QT):
                    mm = nc.tensor.transpose(pb[:, t * P:(t + 1) * P], xn[:, t, :], ident)
                mm.then_inc(xT_full, 1)

            def compress(b):
                wait(pe, xT_done, b + 1)
                nc.tensor.matmul(pb[:, 0:S], wts[:, W_D:W_D + P], xnT[:, :], start=True, stop=True).then_inc(ct_full, 1)

            def rotary(b, turned, full):
                if turned:
                    wait(pe, r1_done, b + 1)
                else:
                    wait(pe, ct_done, b + 1)
                wq = W_U + (1 + turned) * P
                wk = W_KR + turned * P
                nc.tensor.matmul(pb[:, 0:S], wts[:, wq:wq + P], ct[:, :], start=True, stop=True)
                nc.tensor.matmul(pb[:, S:2 * S], wts[:, wk:wk + P], xnT[:, :], start=True, stop=True).then_inc(full, 1)

            def plain(b):
                wait(pe, r2_done, b + 1)
                nc.tensor.matmul(pb[:, 0:S], wts[:, W_U:W_U + P], ct[:, :], start=True, stop=True)
                nc.tensor.matmul(pb[:, S:2 * S], wts[:, W_U + 3 * P:W_U + 4 * P], ct[:, :], start=True, stop=True).then_inc(qk_full, 1)

            def values(b):
                wait(pe, qk_done, b + 1)
                for t in range(QT):
                    mm = nc.tensor.matmul(pb[:, t * P:(t + 1) * P], ct[:, t * P:(t + 1) * P],
                                          wts[:, W_U + 4 * P:W_U + 5 * P], start=True, stop=True)
                mm.then_inc(v_full, 1)

            def project_out(b):
                wait(pe, norm_st, b + 1)
                for t in range(QT):
                    mm = nc.tensor.matmul(pa[:, t * P:(t + 1) * P], outT[:, t * P:(t + 1) * P],
                                          wts[:, W_O:W_O + P], start=True, stop=True)
                mm.then_inc(wo_full, 1)

            def x2_turned(b, s):
                wait(pe, xn2_done, b + 1)
                for t in range(QT):
                    mm = nc.tensor.transpose(pa[:, t * P:(t + 1) * P], pay[:, t, 0, 0:D], ident)
                mm.then_inc(x2T_full, 1)

            def gate(b):
                wait(pe, x2T_done, b + 1)
                for t in range(QT):
                    mm = nc.tensor.matmul(pa[:, t * NE:(t + 1) * NE], xn2T[:, t * P:(t + 1) * P],
                                          wts[:, W_G:W_G + NE], start=True, stop=True)
                mm.then_inc(gate_full, 1)

            def rank(b):
                wait(pe, chosen_done, b + 1)
                w = QT * NE
                nc.tensor.matmul(pa[:, 0:w], tri16[:, :], chosen[:, :, :].rearrange("p t e -> p (t e)"),
                                 start=True, stop=False, skip_group_check=True)
                nc.tensor.matmul(pa[:, NE:w], one16[:, :], chosen[:, 0, :], start=False, stop=False, skip_group_check=True)
                nc.tensor.matmul(pa[:, w:w + NE], one16[:, :], chosen[:, 0, :], start=False, stop=False, skip_group_check=True)
                nc.tensor.matmul(pa[:, w:w + NE], one16[:, :], chosen[:, 1, :], start=False, stop=True,
                                 skip_group_check=True).then_inc(rank_full, 1)

            def step(b, s):
                held = Held(b)
                for h in range(H):
                    q, g = divmod(h, NG)
                    if held.attend:
                        pass2(b, s, h)
                    if held.attend if q < 2 else held.lead:
                        m, ms, j = leading(b, s, q)
                        pass1(m, ms, NG * j + g)
                    if q == 0 and held.route:
                        weigh(b - 1, 1 - s, H - NG + g)
                    elif q > 0 and held.attend:
                        weigh(b, s, h - NG)
                    turns = held.lead if q == NQ - 1 else held.attend
                    if g == 1 and turns:
                        if q == 0:
                            wait(pe, sc_done, b - 1)
                        elif q == 1:
                            wait(pe, rank_done, b)
                        elif q == 2:
                            wait(pe, x2_done, b)
                        else:
                            wait(pe, x2T_done, b)
                        turn_max(*turning(b, s, q))
                    if held.project:
                        if (q, g) == (0, 1):
                            x_turned(b + 2)
                        elif (q, g) == (0, 3):
                            compress(b + 2)
                        elif (q, g) == (1, 1):
                            rotary(b + 2, 0, r1_full)
                        elif (q, g) == (1, 3):
                            rotary(b + 2, 1, r2_full)
                        elif (q, g) == (2, 1):
                            plain(b + 2)
                        elif (q, g) == (2, 3):
                            values(b + 2)
                    if held.send and (q, g) == (0, 3):
                        if held.attend:
                            wait(pe, mt_done, b * NQ + 2)
                        rank(b - 2)
                    if held.route:
                        if (q, g) == (1, 3):
                            if held.attend:
                                wait(pe, mt_done, b * NQ + 3)
                            else:
                                wait(pe, rank_done, b)
                            project_out(b - 1)
                        elif (q, g) == (3, 0):
                            if held.attend:
                                wait(pe, mt_done, b * NQ + 4)
                            x2_turned(b - 1, 1 - s)
                        elif (q, g) == (3, 3):
                            if held.lead:
                                wait(pe, mt_done, b * NQ + 5)
                            gate(b - 1)

            pe.wait_ge(ld_c, 16)
            pe.wait_ge(ld_w, 16)
            pe.wait_ge(set_v, 8)
            for m in range(2):
                x_turned(m)
                compress(m)
                rotary(m, 0, r1_full)
                rotary(m, 1, r2_full)
                plain(m)
                values(m)
            for h in range(NG):
                pass1(0, 0, h)
            turn_max(0, 0, 0)
            for h in range(NG, 2 * NG):
                pass1(0, 0, h)
            pipeline(pe, step)

            pe.wait_ge(plan_st, PLAN)
            pe.wait_ge(rank_done, NB + 1)
            for i in range(2):
                mm = nc.tensor.transpose(pa[0:1, i * P:(i + 1) * P], place_[:, i:i + 1], ident)
            mm.then_inc(table_full, 1)
            pe.wait_ge(table_done, 1)
            pe.wait_ge(ld_w2, 80)

            def turn_tile(t):
                wait(pe, tile_in[t.slot], (t.turn + 1) * 16)
                wait(pe, tT_done, t.n - 1)
                nc.tensor.transpose(tps[t.pair][:, 0:P], tin[t.slot][:, 0:D], ident).then_inc(tT_full, 1)

            def hidden(t):
                wait(pe, tT_done, t.n + 1)
                wait(pe, w1_done, t.n + 1)
                wait(pe, gelu_done, t.n - 1)
                for c in range(FC):
                    mm = nc.tensor.matmul(hps[t.pair][:, :, :].rearrange("p a s -> p (a s)")[:, c * P:(c + 1) * P],
                                          w1s[t.pair][:, c * P:(c + 1) * P], tT[t.pair][:, :], start=True, stop=True)
                mm.then_inc(h_full, 1)

            def result(t, e):
                wait(pe, gelu_done, t.n + 1)
                wait(pe, y_done, t.n - 1)
                for c in range(FC):
                    mm = nc.tensor.matmul(yps[t.pair][:, 0, 0:D], hT[t.pair][:, c, :],
                                          w2[:, bass.ds(e, 1), c, :].rearrange("p o d -> p (o d)"), start=(c == 0), stop=(c == FC - 1))
                mm.then_inc(y_full, 1)

            def tile_step(turn, k):
                after, now, before = Tile(turn, k, 1), Tile(turn, k, 0), Tile(turn, k, -1)
                if before.real:
                    e = expert_of(pe, before)
                if after.real:
                    turn_tile(after)
                if now.real:
                    hidden(now)
                if before.real:
                    result(before, e)

            turn_tile(Tile(0, 0, 0))
            tile_pipeline(pe, tile_step)

        @block.scalar
        def _(act):
            def exponents(b, h):
                if h % NG == 0:
                    wait(act, pv_full, b * H + (h - NG))
                wait(act, s2_full, b * H + (h + 1))
                nc.scalar.activation(pr[h // NG % 2][:, h % NG, :, :], s2[h % 2][:, :, :], ACT.Exp,
                                     scale=SCALE).then_inc(exp_done, 1)

            def take_maxima(m, s, j):
                wait(act, mt_full, m * NQ + (j + 1))
                if j < 2:
                    wait(act, max_in[j + 2], m * 16)
                else:
                    wait(act, max_in[j - 2], (m + 1) * 16)
                nc.scalar.copy(mrow[j % 2][:, :], mturn).then_inc(mt_done, 1)

            def first_part(b):
                wait(act, qk_done, b + 1)
                wait(act, stored_parts, b * 16)
                nc.scalar.copy(qkp[:, :, 0, :], qk[:, :].rearrange("p (z s) -> p z s", z=2)).then_inc(part1_done, 1)

            def second_part(b):
                wait(act, rest_done, b + 1)
                nc.scalar.copy(qkp[:, :, 1, :], rest[:, :].rearrange("p (z s) -> p z s", z=2)).then_inc(part2_done, 1)

            def take_xT(b):
                wait(act, xT_full, b + 1)
                nc.scalar.copy(xnT[:, :], pb[:, 0:S]).then_inc(xT_done, 1)

            def take_ct(b):
                wait(act, ct_full, b + 1)
                nc.scalar.activation(ct[:, :], pb[:, 0:S], ACT.Identity, bias=wts[:, W_B:W_B + 1]).then_inc(ct_done, 1)

            def take_sums(b, s):
                wait(act, pv_full, (b + 1) * H)
                wait(act, norm_st, b)
                for j in range(NQ):
                    r = QW * (2 * (j % 2) + 1)
                    last = nc.scalar.copy(sums[QW * j:QW * (j + 1), :], pv[s][r:r + QW, j // 2, :])
                last.then_inc(sums_done, 1)

            def take_x2T(b):
                wait(act, x2T_full, b + 1)
                nc.scalar.copy(xn2T[:, :], pa[:, 0:S]).then_inc(x2T_done, 1)

            def step(b, s):
                held = Held(b)
                for h in range(H):
                    q, g = divmod(h, NG)
                    if held.project and (q, g) == (1, 0):
                        take_ct(b + 2)
                    if held.attend:
                        exponents(b, h)
                    if g == 1 and (held.lead if q == NQ - 1 else held.attend):
                        take_maxima(*turning(b, s, q))
                    if held.project:
                        if (q, g) == (0, 1):
                            wait(act, vst_done, b + 2)
                            take_xT(b + 2)
                        elif (q, g) == (2, 2):
                            first_part(b + 2)
                        elif (q, g) == (3, 0):
                            second_part(b + 2)
                    if held.route:
                        if (q, g) == (1, 0):
                            take_sums(b - 1, 1 - s)
                        elif (q, g) == (3, 0):
                            take_x2T(b - 1)

            act.wait_ge(ld_w, 16)
            for m in range(2):
                wait(act, vst_done, m)
                take_xT(m)
                take_ct(m)
                first_part(m)
                second_part(m)
            take_maxima(0, 0, 0)
            pipeline(act, step)

            act.wait_ge(gate_st, 1)
            nc.scalar.activation(gtmp[:, 1, :], gtmp[:, 0, :], ACT.Exp).then_inc(gexp_done, 1)
            act.wait_ge(table_done, 1)

            def tile_step(turn, k):
                t = Tile(turn, k, 0)
                if not t.real:
                    return
                e = expert_of(act, t)
                wait(act, h_full, t.n + 1)
                wait(act, y_full, t.n - 1)
                for c in range(FC):
                    last = nc.scalar.activation(hT[t.pair][:, c, :], hps[t.pair][:, :, :].rearrange("p a s -> p (a s)")[:, c * P:(c + 1) * P],
                                                ACT.Gelu, bias=wts[:, bass.ds(e * FC + (W_B1 + c), 1)])
                last.then_inc(gelu_done, 1)

            tile_pipeline(act, tile_step)

        @block.vector
        def _(dve):
            def maximum(m, s, j, g):
                h = NG * j + g
                wait(dve, s1_full, m * H + (h + 1))
                nc.vector.tensor_reduce(mx[j % 2][:, :, g], s1[h % 2][:, :, :], AX.X, ALU.max).then_inc(max_done, 1)

            def split_maxima(m, s, j):
                n = m * NQ + j
                x, xp = mx[j % 2][:, :, :], mxp[j % 2]
                wait(dve, max_done, m * H + NG * (j + 1))
                wait(dve, mt_full, n - 1)
                nc.vector.tensor_copy(xp[:, :, 0, :], x).then_inc(split_st, 1)
                wait(dve, split_st, n * 3 + 1)
                nc.vector.tensor_tensor(xp[:, :, 1, :], x, xp[:, :, 0, :], ALU.subtract).then_inc(split_st, 1)
                nc.vector.tensor_tensor(mrest[:, :, :], x, xp[:, :, 0, :], ALU.subtract).then_inc(split_st, 1)
                wait(dve, split_st, n * 3 + 3)
                nc.vector.tensor_tensor(xp[:, :, 2, :], mrest[:, :, :], xp[:, :, 1, :], ALU.subtract).then_inc(split_done, 1)

            def stats(b, st, mv, done):
                for t in range(QT):
                    nc.vector.bn_stats(st[:, t, :], x_all[:, bass.ds(b * QT + t, 1), :].rearrange("p o d -> p (o d)")).then_inc(done, 1)
                wait_apart(dve, done, b * 2 * QT + QT)
                for t in range(QT):
                    nc.vector.bn_aggr(mv[:, t, :], st[:, t, :]).then_inc(done, 1)

            def normalise_x(b):
                wait(dve, rstd1_st, (b + 1) * 2)
                wait(dve, xT_full, b)
                for t in range(QT):
                    last = nc.vector.tensor_scalar(xn[:, t, :], x_all[:, bass.ds(b * QT + t, 1), :].rearrange("p o d -> p (o d)"),
                                                   mv1[:, t, 0:1], rstd1[:, t:t + 1], ALU.subtract, ALU.mult)
                last.then_inc(xn_done, 1)

            def take_rotary(b, full, turn, col, done, free):
                wait(dve, full, b + 1)
                wait(dve, turn_st, b * 2)
                if free:
                    wait(dve, qk_done, b)
                nc.vector.tensor_tensor(turn[:, :], pb[:, :], consts[:, col:col + 2 * S], ALU.mult).then_inc(done, 1)

            def take_qk(b):
                wait(dve, qk_full, b + 1)
                wait(dve, turn_st, (b + 1) * 2)
                wait(dve, rest_done, b)
                nc.vector.tensor_tensor(qk[:, :], pb[:, :], turn1[:, :], ALU.add).then_inc(qk_done, 1)

            def take_values(b):
                wait(dve, v_full, b + 1)
                wait(dve, v_done, b)
                nc.vector.tensor_tensor(vst[:, :, :], pb[:, 0:S].rearrange("p (t d) -> p t d", t=QT),
                                        brow[:, None, R_V:R_V + P].broadcast_to([P, QT, D]), ALU.add).then_inc(vst_done, 1)

            def normalise_out(b, s):
                wait(dve, sums_done, b + 1)
                nc.vector.reciprocal(sums[:, :], sums[:, :]).then_inc(inv_st, 1)
                wait(dve, inv_st, b + 1)
                wait(dve, wo_full, b)
                for j in range(NQ):
                    o, r = slice(QW * j, QW * (j + 1)), 2 * QW * (j % 2)
                    last = nc.vector.tensor_tensor(outT[o, :], pv[s][r:r + QW, j // 2, :], sums[o, :], ALU.mult)
                last.then_inc(norm_st, 1)

            def take_out(b):
                wait(dve, wo_full, b + 1)
                wait(dve, xb_done, b + 1)
                xs = x_all[:, bass.ds(b * QT, QT), :]
                nc.vector.tensor_tensor(xs, pa[:, 0:S].rearrange("p (t d) -> p t d", t=QT), xs, ALU.add).then_inc(x2_done, 1)
                wait_apart(dve, x2_done, b + 1)
                stats(b, st2, mv2, ln2_st)

            def normalise_rows(b):
                wait(dve, rstd2_st, (b + 1) * 2)
                wait(dve, sent, b * (QT * TOPK * 16))
                for t in range(QT):
                    src = x_all[:, bass.ds(b * QT + t, 1), :].broadcast_to([P, TOPK, D])
                    last = nc.vector.tensor_scalar(pay[:, t, :, 0:D], src, mv2[:, t, 0:1], rstd2[:, t:t + 1],
                                                   ALU.subtract, ALU.mult)
                last.then_inc(xn2_done, 1)

            TOP = 8

            def choose(b):
                wait(dve, gate_full, b + 1)
                nc.vector.tensor_tensor(sc[:, :, :], pa[:, 0:QT * NE].rearrange("p (t e) -> p t e", t=QT),
                                        brow[:, None, R_G:R_G + NE].broadcast_to([P, QT, NE]), ALU.add).then_inc(sc_done, 1)
                wait_apart(dve, sc_done, b + 1)
                for t in range(QT):
                    nc.vector.max(top8[:, t, :], sc[:, t, :]).then_inc(top_st, 1)
                wait_apart(dve, top_st, b * TOP + 2)
                for t in range(QT):
                    nc.vector.max_index(arg8[:, t, :], top8[:, t, :], sc[:, t, :]).then_inc(top_st, 1)
                nc.vector.tensor_copy(top_all[:, bass.ds(b * QT, QT), :], top8[:, :, 0:TOPK]).then_inc(top_st, 1)
                wait(dve, top_st, b * TOP + 5)
                nc.vector.tensor_copy(argf[:, :, :], arg8[:, :, 0:TOPK]).then_inc(top_st, 1)
                wait(dve, top_st, b * TOP + 6)
                nc.vector.tensor_tensor(oh[:, :, :], argf[:, :, :].rearrange("p t k -> p (t k)")[:, :, None].broadcast_to([P, QT * TOPK, NE]),
                                        consts[:, None, C_EXP:C_EXP + NE].broadcast_to([P, QT * TOPK, NE]), ALU.is_equal).then_inc(top_st, 1)
                wait(dve, top_st, b * TOP + 7)
                wait(dve, rank_full, b)
                ov = oh[:, :, :].rearrange("p (t k) e -> p t k e", k=TOPK)
                nc.vector.tensor_tensor(chosen[:, :, :], ov[:, :, 0, :], ov[:, :, 1, :], ALU.add).then_inc(chosen_done, 1)
                nc.vector.engine_nop().then_inc(top_st, 1)

            POS = 3

            def place(b, s):
                wait(dve, rank_full, b + 1)
                wait(dve, rank_done, b + 1)
                nc.vector.tensor_tensor(rk[s][:, :, :], pa[:, 0:(QT + 1) * NE].rearrange("p (t e) -> p t e", e=NE),
                                        rk[1 - s][:, QT:QT + 1, :].broadcast_to([P, QT + 1, NE]), ALU.add).then_inc(rank_done, 1)
                wait(dve, rank_done, b + 2)
                nc.vector.tensor_tensor(ohrk[:, :, :].rearrange("p (t k) e -> p t k e", k=TOPK),
                                        oh[:, :, :].rearrange("p (t k) e -> p t k e", k=TOPK),
                                        rk[s][:, 0:QT, None, :].broadcast_to([P, QT, TOPK, NE]), ALU.mult).then_inc(pos_st, 1)
                wait(dve, pos_st, b * POS + 1)
                nc.vector.tensor_reduce(posf[:, :], ohrk[:, :, :], AX.X, ALU.add).then_inc(pos_st, 1)
                wait(dve, pos_st, b * POS + 2)
                nc.vector.tensor_copy(pos[:, :], posf[:, :]).then_inc(pos_st, 1)

            def step(b, s):
                held = Held(b)
                if held.project:
                    stats(b + 2, st1, mv1, ln1_st)
                for h in range(H):
                    q, g = divmod(h, NG)
                    lead = held.attend if q < 2 else held.lead
                    if held.route and (q, g) == (3, 0):
                        normalise_rows(b - 1)
                    if held.project and (q, g) == (2, 3):
                        take_qk(b + 2)
                    if lead:
                        maximum(*leading(b, s, q), g)
                        if g == NG - 1:
                            split_maxima(*leading(b, s, q))
                    if held.project:
                        if (q, g) == (0, 0):
                            normalise_x(b + 2)
                        elif (q, g) == (1, 1):
                            take_rotary(b + 2, r1_full, turn1, C_COS, r1_done, True)
                        elif (q, g) == (1, 3):
                            take_rotary(b + 2, r2_full, turn2, C_SIN, r2_done, False)
                        elif (q, g) == (3, 0):
                            take_values(b + 2)
                    if held.send and (q, g) == (0, 3):
                        place(b - 2, s)
                    if held.route:
                        if (q, g) == (1, 0):
                            normalise_out(b - 1, 1 - s)
                        elif (q, g) == (2, 0):
                            take_out(b - 1)
                        elif (q, g) == (3, 3):
                            choose(b - 1)

            for i in range(2):
                nc.vector.memset(vm[i][:, :, :, :], 0.0).then_inc(set_v, 1)
            dve.wait_ge(set_v, 2)
            for i in range(2):
                nc.vector.memset(own_columns(i, QW), 1.0).then_inc(set_v, 1)
            dve.wait_ge(ld_x0, 16)
            stats(0, st1, mv1, ln1_st)
            dve.wait_ge(ld_c, 16)
            nc.vector.tensor_copy(tri16[:, :], consts[:, C_TRI:C_TRI + P]).then_inc(set_v, 1)
            nc.vector.tensor_copy(one16[:, :], consts[:, C_ONE:C_ONE + P]).then_inc(set_v, 1)
            nc.vector.tensor_copy(ident16[:, :], ident).then_inc(set_v, 1)
            nc.vector.tensor_copy(rk[1][:, QT, :], consts[:, C_BASE:C_BASE + NE]).then_inc(rank_done, 1)
            nc.vector.memset(pay[:, :, :, D:ROWW], 0.0).then_inc(set_v, 1)
            normalise_x(0)
            dve.wait_ge(ld_w, 16)
            for i in range(2):
                c = W_B + 1 + 3 * i
                nc.vector.tensor_scalar(biasqk[:, i, :], consts[:, C_COS:C_COS + S], wts[:, c + 1:c + 2], wts[:, c:c + 1],
                                        ALU.mult, ALU.add).then_inc(bias_st, 1)
            dve.wait_ge(bias_st, 2)
            for i in range(2):
                c = W_B + 1 + 3 * i
                nc.vector.scalar_tensor_tensor(biasqk[:, i, :], consts[:, C_SIN:C_SIN + S], wts[:, c + 2:c + 3],
                                               biasqk[:, i, :], ALU.mult, ALU.add).then_inc(bias_st, 1)
            stats(1, st1, mv1, ln1_st)
            dve.wait_ge(ld_r, 16)
            for m in range(2):
                take_rotary(m, r1_full, turn1, C_COS, r1_done, True)
                if m == 0:
                    normalise_x(1)
                take_rotary(m, r2_full, turn2, C_SIN, r2_done, False)
                take_qk(m)
                take_values(m)
            for j in range(2):
                for g in range(NG):
                    maximum(0, 0, j, g)
                split_maxima(0, 0, j)
            dve.wait_ge(ld_x, 32)
            pipeline(dve, step)

            links = [0]

            def link(ins):
                links[0] += 1
                ins.then_inc(plan_st, 1)
                dve.wait_ge(plan_st, links[0])

            link(nc.vector.memset(padt[:, :], 0.0))
            link(nc.vector.tensor_copy(padt[:, D:D + 1].bitcast(U32), consts[:, C_PAD:C_PAD + 1]))
            assert links[0] == PADT
            after = rk[(NB - 1) % 2][:, QT, :]
            dve.wait_ge(rank_done, NB + 1)
            link(nc.vector.tensor_tensor(count[:, 0, :], after, consts[:, C_BASE:C_BASE + NE], ALU.subtract))
            link(nc.vector.tensor_scalar(counti[:, :], count[:, 0, :], float(P - 1), None, ALU.add))
            link(nc.vector.tensor_scalar(counti[:, :], counti[:, :], 7, None, ALU.arith_shift_right))
            link(nc.vector.tensor_copy(count[:, 1, :], counti[:, :]))
            link(nc.vector.tensor_tensor_scan(count[:, 2, :], consts[:, C_ONE:C_ONE + NE], count[:, 1, :], 0.0, ALU.mult, ALU.add))
            part = consts[:, C_PART:C_PART + 1]
            link(nc.vector.tensor_scalar(past[:, 0, :], count[:, 2, :], part, None, ALU.is_le))
            link(nc.vector.tensor_tensor(past[:, 1, :], past[:, 0, :], count[:, 1, :], ALU.mult))
            link(nc.vector.tensor_reduce(place_[:, 2:4], past[:, :, :], AX.X, ALU.add))
            link(nc.vector.tensor_scalar(place_[:, 0:1], place_[:, 2:3], float(NE - 1), None, ALU.min))
            link(nc.vector.tensor_tensor(place_[:, 3:4], part, place_[:, 3:4], ALU.subtract))
            link(nc.vector.tensor_scalar(place_[:, 2:3], place_[:, 2:3], float(REG), None, ALU.mult))
            link(nc.vector.scalar_tensor_tensor(place_[:, 1:2], place_[:, 3:4], float(P), place_[:, 2:3], ALU.mult, ALU.add))
            link(nc.vector.tensor_scalar(place_[:, 1:2], place_[:, 1:2], float(NE * REG), None, ALU.min))
            assert links[0] == PLAN
            dve.wait_ge(table_full, 1)
            nc.vector.tensor_copy(table[:, :, :].rearrange("p a s -> p (a s)"), pa[0:1, 0:2 * P]).then_inc(table_done, 1)
            nc.vector.tensor_copy(ends[:, :], after[0:1, :]).then_inc(table_done, 1)
            nc.vector.tensor_tensor(gtmp[:, 0, :], top_all[:, :, 1], top_all[:, :, 0], ALU.subtract).then_inc(gate_st, 1)
            dve.wait_ge(table_done, 2)

            def take_tile(t):
                wait(dve, tT_full, t.n + 1)
                wait(dve, h_full, t.n - 1)
                nc.vector.tensor_copy(tT[t.pair][:, :], tps[t.pair][:, 0:P]).then_inc(tT_done, 1)
                wait(dve, tile_out[t.slot], t.turn * 16)
                nc.vector.tensor_copy(ridx[t.slot][:, :], tin[t.slot][:, D:D + 1].bitcast(U32)).then_inc(ridx_done, 1)

            def take_weights(t, e):
                wait(dve, h_full, t.n - 1)
                nc.vector.tensor_copy(w1s[t.pair][:, :], w1[:, bass.ds(e, 1), :].rearrange("p o f -> p (o f)")).then_inc(w1_done, 1)

            def take_result(t, e):
                wait(dve, y_full, t.n + 1)
                wait(dve, tile_out[t.slot], t.turn * 16)
                nc.vector.tensor_tensor(yo[t.slot][:, :], yps[t.pair][:, 0, 0:D], brow[:, bass.ds(e * D + R_B2, D)], ALU.add).then_inc(y_done, 1)

            def tile_step(turn, k):
                after, before = Tile(turn, k, 1), Tile(turn, k, -1)
                if after.real:
                    ea = expert_of(dve, after)
                if before.real:
                    eb = expert_of(dve, before)
                if after.real:
                    take_tile(after)
                    take_weights(after, ea)
                if before.real:
                    take_result(before, eb)

            dve.wait_ge(ld_w1, 16 * (NB - 4))
            t0 = Tile(0, 0, 0)
            take_weights(t0, expert_of(dve, t0))
            take_tile(t0)
            tile_pipeline(dve, tile_step)

            dve.wait_ge(gexp_done, 1)
            nc.vector.tensor_scalar(gtmp[:, 0, :], gtmp[:, 1, :], 1.0, None, ALU.add).then_inc(gate_st, 1)
            dve.wait_ge(gate_st, 2)
            nc.vector.reciprocal(gates[:, :, 0], gtmp[:, 0, :]).then_inc(gate_st, 1)
            dve.wait_ge(gate_st, 3)
            nc.vector.tensor_tensor(gates[:, :, 1], gtmp[:, 1, :], gates[:, :, 0], ALU.mult).then_inc(gate_st, 1)
            dve.wait_ge(gate_st, 4)
            for c in range(NT // CHUNK):
                dve.wait_ge(back[c], 16)
                y = chunk(c).rearrange("p t k d -> p (t k) d")
                g = gates[:, c * CHUNK:(c + 1) * CHUNK, :].rearrange("p t k -> p (t k)")[:, :, None]
                nc.vector.tensor_tensor(y, y, g.broadcast_to([P, CHUNK * TOPK, D]), ALU.mult).then_inc(weighed, 1)
                dve.wait_ge(weighed, c + 1)
                nc.vector.tensor_tensor(chunk(c)[:, :, 0, :], chunk(c)[:, :, 0, :], chunk(c)[:, :, 1, :], ALU.add).then_inc(summed, 1)

        @block.gpsimd
        def _(pool):
            def deviation(b, mv, ve, rstd, stat, done):
                wait(pool, stat, (b + 1) * 2 * QT)
                nc.gpsimd.tensor_tensor(ve[:, :], mv[:, :, 1], powers[:, 1, :], ALU.add).then_inc(done, 1)
                wait(pool, done, b * 2 + 1)
                nc.gpsimd.tensor_tensor(rstd[:, :], ve[:, :], powers[:, 0, :], ALU.pow).then_inc(done, 1)

            def add_out_bias(b):
                wait(pool, xn_done, b + 1)
                xs = x_all[:, bass.ds(b * QT, QT), :]
                nc.gpsimd.tensor_tensor(xs, xs, brow[:, None, R_O:R_O + D].broadcast_to([P, QT, D]), ALU.add).then_inc(xb_done, 1)

            def sum_turns(b):
                wait(pool, r1_done, b + 1)
                wait(pool, r2_done, b + 1)
                nc.gpsimd.tensor_tensor(turn1[:, :], turn1[:, :], turn2[:, :], ALU.add).then_inc(turn_st, 1)
                wait(pool, turn_st, b * 2 + 1)
                nc.gpsimd.tensor_tensor(turn1[:, :], turn1[:, :], biasqk[:, :, :].rearrange("p i s -> p (i s)"),
                                        ALU.add).then_inc(turn_st, 1)

            def leave(b):
                wait(pool, part1_done, b + 1)
                wait(pool, part3_done, b)
                nc.gpsimd.tensor_tensor(rest[:, :].rearrange("p (z s) -> p z s", z=2), qk[:, :].rearrange("p (z s) -> p z s", z=2),
                                        qkp[:, :, 0, :], ALU.subtract).then_inc(rest_done, 1)

            def third_part(b):
                wait(pool, part2_done, b + 1)
                nc.gpsimd.tensor_tensor(qkp[:, :, 2, :], rest[:, :].rearrange("p (z s) -> p z s", z=2),
                                        qkp[:, :, 1, :], ALU.subtract).then_inc(part3_done, 1)

            def give_values(b, s):
                wait(pool, vst_done, b + 1)
                wait_apart(pool, pv_full, (b - 1) * H)
                nc.gpsimd.tensor_copy(own_columns(s, 0),
                                      vst[:, :, :].rearrange("p t (j g d) -> p (t j) g d", j=NQ, g=NG)).then_inc(v_done, 1)

            def send(b, s):
                wait(pool, xn2_done, b + 1)
                nc.gpsimd.tensor_copy(pay[:, :, :, D].bitcast(U32),
                                      rows[:, bass.ds(b * QT, QT), :]).then_inc(idx_done, 1)
                wait(pool, idx_done, b + 1)
                wait_apart(pool, pos_st, (b + 1) * 3)
                for t in range(QT):
                    for k in range(TOPK):
                        n = t * TOPK + k
                        nc.gpsimd.indirect_dma_start(
                            dispatched, bass.IndirectOffsetOnAxis(ap=pos[:, n:n + 1], axis=0),
                            pay[:, t, k, :], None).then_inc(sent, 16)

            def step(b, s):
                held = Held(b)
                if held.project:
                    deviation(b + 2, mv1, ve1, rstd1, ln1_st, rstd1_st)
                if held.send:
                    send(b - 2, s)
                if held.lead:
                    give_values(b + 1, 1 - s)
                if held.project:
                    add_out_bias(b + 2)
                    sum_turns(b + 2)
                if held.route:
                    deviation(b - 1, mv2, ve2, rstd2, ln2_st, rstd2_st)
                if held.project:
                    leave(b + 2)
                    third_part(b + 2)

            nc.gpsimd.memset(powers[:, 0, :], -0.5).then_inc(set_p, 1)
            nc.gpsimd.memset(powers[:, 1, :], EPS).then_inc(set_p, 1)
            pool.wait_ge(set_p, 2)
            pool.wait_ge(set_v, 8)
            deviation(0, mv1, ve1, rstd1, ln1_st, rstd1_st)
            deviation(1, mv1, ve1, rstd1, ln1_st, rstd1_st)
            pool.wait_ge(rstd1_st, 4)
            nc.gpsimd.memset(spread[64:96, :, 1, :, :].rearrange("p i h s -> p i (h s)"), -1.0).then_inc(neg_st, 1)
            pool.wait_ge(neg_st, 1)
            pool.wait_ge(ld_r, 16)
            pool.wait_ge(bias_st, 4)
            for m in range(2):
                add_out_bias(m)
                sum_turns(m)
                leave(m)
                third_part(m)
                if m == 0:
                    give_values(0, 0)
            pool.wait_ge(ld_x, 32)
            pipeline(pool, step)

            def tile_step(turn, k):
                t = Tile(turn, k, -1)
                if not t.real:
                    return
                wait_apart(pool, y_done, t.n + 1)
                nc.gpsimd.indirect_dma_start(results, bass.IndirectOffsetOnAxis(ap=ridx[t.slot][:, 0:1], axis=0),
                                             yo[t.slot][:, :], None, bounds_check=TOPK * T - 1,
                                             oob_is_err=False).then_inc(tile_out[t.slot], 16)

            tile_pipeline(pool, tile_step)
            for c in range(NT // CHUNK):
                pool.wait_ge(summed, c + 1)
                xs = x_all[:, c * CHUNK:(c + 1) * CHUNK, :]
                nc.gpsimd.tensor_tensor(xs, xs, chunk(c)[:, :, 0, :], ALU.add).then_inc(final, 1)


def kernel(**inputs):
    import concourse.bacc as bacc
    from concourse.bass_utils import run_bass_kernel_spmd

    a = {k.split("_", 1)[1]: np.ascontiguousarray(v) for k, v in inputs.items()}
    x = a["attn_x"].reshape(NT, P, D).transpose(1, 0, 2).reshape(P, NT * D)

    def turned(w):
        return w.reshape(*w.shape[:-1], D // 2, 2)[..., ::-1].reshape(w.shape)

    def col(v):
        return v.reshape(-1, 1)

    def heads(w):
        return w[..., by_dimension()]

    upper = np.concatenate([heads(a["attn_Wu_q_w"]), heads(a["attn_Wq_r_w"]), heads(turned(a["attn_Wq_r_w"]))], 1)
    lower = np.concatenate([heads(a["attn_Wu_k_w"]), a["attn_Wu_v_w"]], 1)
    b1 = a["ffn_b1"].reshape(NE, FC, P).transpose(2, 0, 1).reshape(P, NE * FC)
    weights = np.concatenate([
        a["attn_Wd_q_w"], a["attn_Wd_kv_w"], np.pad(upper, ((0, DQ), (0, 0))), np.pad(lower, ((DQ, 0), (0, 0))),
        heads(a["attn_Wk_r_w"]), heads(turned(a["attn_Wk_r_w"])), a["attn_Wo_w"], a["ffn_gate_w"], b1,
        col(np.concatenate([a["attn_Wd_q_b"], a["attn_Wd_kv_b"]])),
        col(heads(a["attn_Wu_q_b"])), col(heads(a["attn_Wq_r_b"])), col(heads(turned(a["attn_Wq_r_b"]))),
        col(heads(a["attn_Wu_k_b"])), col(heads(a["attn_Wk_r_b"])), col(heads(turned(a["attn_Wk_r_b"])))], 1)
    bias_rows = np.concatenate([a["attn_Wu_v_b"], a["attn_Wo_b"], a["ffn_gate_b"], a["ffn_b2"].reshape(-1)])
    w1 = a["ffn_w1"].transpose(1, 0, 2).reshape(P, NE * DF)
    w2 = a["ffn_w2"].reshape(NE, FC, P, D).transpose(2, 0, 1, 3).reshape(P, NE * FC * D)
    arrays = {"x": x, "weights": weights, "bias_rows": bias_rows, "w1": w1, "w2": w2,
              "constants": shape_constants(), "rows": result_rows()}
    arrays = {k: np.ascontiguousarray(v) for k, v in arrays.items()}

    nc = bacc.Bacc("TRN2", target_bir_lowering=False, num_devices=1)
    aps = [nc.dram_tensor("in_" + k, v.shape, mybir.dt.from_np(v.dtype), kind="ExternalInput").ap() for k, v in arrays.items()]
    out = nc.dram_tensor("out", (P, NT * D), F32, kind="ExternalOutput").ap()
    build(nc, *aps, out)
    r = run_bass_kernel_spmd(nc, [{"in_" + k: v for k, v in arrays.items()}], core_ids=[0])
    got = r.results[0]["out"]
    return got.reshape(P, NT, D).transpose(1, 0, 2).reshape(NB, S, D)
```

```python
from contextlib import ExitStack

import numpy as np
import concourse.bass as bass
from concourse import mybir

F32 = mybir.dt.float32
BF16 = mybir.dt.bfloat16
U32 = mybir.dt.uint32
I32 = mybir.dt.int32
ALU = mybir.AluOpType
ACT = mybir.ActivationFunctionType
AX = mybir.AxisListType

P = 128
NB, S, D = 16, 256, 128
H, HD = 16, 8
DQ = 64
NE, DF, TOPK = 24, 512, 2
FC = DF // P
QT = S // P
T = NB * S
NT = T // P
NG = 4
NQ = H // NG
NP = 3
QW = NG * HD
KR = NP * NP * HD
SCALE = float(H + 2 * DQ) ** -0.5
EPS = 1e-5
REG = T + P
ROWW = D + 4
TILES = (TOPK * T + NE * (P - 1)) // P
UNROLL, SLOTS = 8, 8
TILES = -(-TILES // UNROLL) * UNROLL
CHUNK = 4
PADT, PLAN = 2, 15

C_ID, C_TRI, C_ONE = 0, P, 2 * P
C_COS = 3 * P
C_SIN = C_COS + 2 * S
C_EXP = C_SIN + 2 * S
C_BASE = C_EXP + NE
C_PART = C_BASE + NE
C_PAD = C_PART + 1
NCONST = C_PAD + 1

W_D = 0
W_U = W_D + P
W_KR = W_U + 5 * P
W_O = W_KR + 2 * P
W_G = W_O + P
W_B1 = W_G + NE
W_B = W_B1 + NE * FC
NW = W_B + 7
R_V, R_O, R_G = 0, P, 2 * P
NR = R_G + NE


def by_dimension():
    return np.arange(D).reshape(H, HD).T.reshape(-1)


def by_half():
    return np.arange(D).reshape(H // 8, NG, 2, HD).transpose(0, 2, 1, 3).reshape(-1)


def shape_constants():
    c = np.zeros((P, NCONST), np.float32)
    p = np.arange(P)
    c[:, C_ID:C_ID + P] = np.eye(P)
    c[:, C_TRI:C_TRI + P] = p[:, None] < p[None, :]
    c[:, C_ONE:C_ONE + P] = 1.0
    ids = np.arange(D // 2, dtype=np.float32)
    theta = (np.float32(10000.0) ** (np.float32(-2.0) * ids) / np.float32(D // 2)).astype(np.float32)
    angle = (np.arange(S, dtype=np.float32)[:, None] * theta[None, :]).astype(np.float32)
    cos = np.repeat(np.cos(angle).astype(np.float32).T, 2, axis=0)
    sin = np.repeat(np.sin(angle).astype(np.float32).T, 2, axis=0)
    sin[0::2] *= -1.0
    cos, sin = cos[by_dimension()], sin[by_dimension()]
    for i in range(2):
        c[:, C_COS + i * S:C_COS + (i + 1) * S] = cos
        c[:, C_SIN + i * S:C_SIN + (i + 1) * S] = sin
    c[:, C_EXP:C_EXP + NE] = np.arange(NE)
    c[:, C_BASE:C_BASE + NE] = np.arange(NE) * REG
    c[:, C_PART] = p
    c[:, C_PAD] = TOPK * T
    return c


def result_rows():
    p, t, k = np.ogrid[0:P, 0:NT, 0:TOPK]
    return (TOPK * (P * t + p) + k).astype(np.uint32).reshape(P, NT * TOPK)


def build(nc, x_in, w_in, r_in, b2_in, w1_in, w2_in, c_in, rows_in, out):
    with ExitStack() as ctx:
        def sb(name, shape, dt=F32):
            return ctx.enter_context(nc.sbuf_tensor(name, shape, dt))

        def ps(name, shape):
            return ctx.enter_context(nc.psum_tensor(name, shape, F32))

        def sem(name):
            return ctx.enter_context(nc.semaphore(name))

        dispatched = nc.dram_tensor("dispatched", ((NE + 1) * REG, ROWW), F32, kind="Internal").ap()
        parts_out = nc.dram_tensor("parts_out", (2, NP, D * S), BF16, kind="Internal").ap()
        results = nc.dram_tensor("results", (TOPK * T, D), F32, kind="Internal").ap()

        x_all = sb("x_all", [P, NT, D])
        consts = sb("consts", [P, NCONST])
        wts = sb("wts", [P, NW])
        brow = sb("brow", [P, NR])
        w1 = sb("w1", [P, NE, DF + D])
        w2 = sb("w2", [P, NE, FC, D])
        rows = sb("rows", [P, NT, TOPK], U32)
        top_all = sb("top_all", [P, NT, TOPK])
        tri16 = sb("tri16", [P, P], BF16)
        one16 = sb("one16", [P, P], BF16)
        ident16 = sb("ident16", [P, P], BF16)
        powers = sb("powers", [P, 2, NT])
        biasqk = sb("biasqk", [P, 2, S])

        st1 = sb("st1", [P, NT, 6])
        mv1 = sb("mv1", [P, NT, 2])
        ve1 = sb("ve1", [P, NT])
        rstd1 = sb("rstd1", [P, NT])
        xn = sb("xn", [P, QT, D])
        xnT = sb("xnT", [P, S])
        ct = sb("ct", [P, S])
        turn1 = sb("turn1", [P, 2 * S])
        turn2 = sb("turn2", [P, 2 * S])
        qk = sb("qk", [P, 2 * S])
        rest = sb("rest", [P, 2 * S])
        weighed_sb = rest[:, :].rearrange("p (r s) -> p r s", r=2)
        qkp = sb("qkp", [P, 2, NP, S], BF16)
        vst = sb("vst", [P, QT, D])
        vm = [sb(f"vm{i}", [P, QT, NQ, NG * 2 * QW]) for i in range(2)]
        mx = [sb(f"mx{i}", [P, QT, NG]) for i in range(2)]
        mrest = sb("mrest", [P, QT, NG])
        mxp = [sb(f"mxp{i}", [P, QT, NP, NG], BF16) for i in range(2)]
        mrow = [sb(f"mrow{i}", [NP * NG, S], BF16) for i in range(2)]
        pr = [sb(f"pr{i}", [P, NG, QT, S]) for i in range(2)]
        sums = sb("sums", [P, S])
        outT = sb("outT", [P, S])
        spread = w2[:, :, :, :].rearrange("p e c d -> p (e c d)")[:, 0:2 * H * S].bitcast(BF16).rearrange(
            "p (i z h s) -> p i z h s", i=2, z=2, h=H)
        qrows = [spread[:, i, 0, :, :] for i in range(2)]
        krows = [spread[:, i, 1, :, :] for i in range(2)]

        st2 = sb("st2", [P, QT, 6])
        mv2 = sb("mv2", [P, QT, 2])
        ve2 = sb("ve2", [P, QT])
        rstd2 = sb("rstd2", [P, QT])
        pay = sb("pay", [P, QT, TOPK, ROWW])
        xn2T = sb("xn2T", [P, S])
        sc = sb("sc", [P, QT, NE])
        top8 = sb("top8", [P, QT, 8])
        arg8 = sb("arg8", [P, QT, 8], U32)
        argf = sb("argf", [P, QT, TOPK])
        oh = sb("oh", [P, QT * TOPK, NE])
        chosen = sb("chosen", [P, QT, NE], BF16)
        rk = [sb(f"rk{i}", [P, QT + 1, NE]) for i in range(2)]
        ohrk = sb("ohrk", [P, QT * TOPK, NE])
        posf = sb("posf", [P, QT * TOPK])
        pos = sb("pos", [P, QT * TOPK], U32)

        count = sb("count", [P, 3, NE])
        counti = sb("counti", [P, NE], I32)
        past = sb("past", [P, 2, NE])
        place_ = sb("place_", [P, 4])
        table = sb("table", [1, 2, P], I32)
        ends = sb("ends", [1, NE], I32)
        padt = sb("padt", [P, ROWW])
        gates = sb("gates", [P, NT, TOPK])
        gtmp = sb("gtmp", [P, 2, NT])
        tin = [sb(f"tin{i}", [P, ROWW]) for i in range(SLOTS)]
        ridx = [sb(f"ridx{i}", [P, 1], U32) for i in range(SLOTS)]
        tT = [turn1[:, 0:P], turn2[:, 0:P]]
        w1s = [vm[i // 2][:, :, :, :].rearrange("p t j f -> p (t j f)")[:, i % 2 * (DF + D):(i % 2 + 1) * (DF + D)]
               for i in range(4)]
        hT = [pr[i][:, :, 0, 0:P] for i in range(2)]
        yo = [sb(f"yo{i}", [P, D]) for i in range(SLOTS)]

        s1 = [ps(f"s1_{i}", [P, QT, S]) for i in range(2)]
        s2 = [ps(f"s2_{i}", [P, QT, S]) for i in range(2)]
        pv = ps("pv", [P, 2, S])
        pa = ps("pa", [P, 512])
        pm = ps("pm", [P, 512])
        pb = ps("pb", [P, 512])

        tps = [pa, pb]
        hps = s2
        yps = s1

        def own_columns(i, first):
            v = vm[i][:, :, :, :]
            return bass.AP(tensor=v.tensor, offset=v.offset + first,
                           ap=[v.ap[0], [NG * 2 * QW, QT * NQ], [2 * QW + HD, NG], [1, HD]])

        ident = consts[:, C_ID:C_ID + P]
        mturn = pm[0:NP * NG, 0:S]
        IN_USE = 2 * H * S // DF
        SPREAD = 16 * (NP + 1)

        ld_x0, ld_id, ld_c, ld_w, ld_x, ld_r, ld_w1, ld_b2, ld_w2 = (sem(n) for n in (
            "ld_x0", "ld_id", "ld_c", "ld_w", "ld_x", "ld_r", "ld_w1", "ld_b2", "ld_w2"))
        set_v, set_p, bias_st = sem("set_v"), sem("set_p"), sem("bias_st")
        s1_full, max_done, split_st, split_done = sem("s1_full"), sem("max_done"), sem("split_st"), sem("split_done")
        mt_full, mt_done = sem("mt_full"), sem("mt_done")
        sums_done, nums_done, inv_st, pv_done = sem("sums_done"), sem("nums_done"), sem("inv_st"), sem("pv_done")
        max_in = [sem(f"max_in{j}") for j in range(NQ)]
        part1_done, rest_done, part2_done, part3_done = sem("part1_done"), sem("rest_done"), sem("part2_done"), sem("part3_done")
        stored_parts, spread_in, neg_st = sem("stored_parts"), sem("spread_in"), sem("neg_st")
        s2_full, exp_done, pv_full, norm_st = sem("s2_full"), sem("exp_done"), sem("pv_full"), sem("norm_st")
        ln1_st, rstd1_st, xn_done, xb_done = sem("ln1_st"), sem("rstd1_st"), sem("xn_done"), sem("xb_done")
        xT_full, xT_done, ct_full, ct_done = sem("xT_full"), sem("xT_done"), sem("ct_full"), sem("ct_done")
        r1_full, r1_done, r2_full, r2_done = sem("r1_full"), sem("r1_done"), sem("r2_full"), sem("r2_done")
        turn_st, qk_full, qk_done = sem("turn_st"), sem("qk_full"), sem("qk_done")
        v_full, vst_done, v_done = sem("v_full"), sem("vst_done"), sem("v_done")
        wo_full, x2_done, ln2_st, rstd2_st, xn2_done = sem("wo_full"), sem("x2_done"), sem("ln2_st"), sem("rstd2_st"), sem("xn2_done")
        x2T_full, x2T_done, gate_full, sc_done = sem("x2T_full"), sem("x2T_done"), sem("gate_full"), sem("sc_done")
        top_st, chosen_done, rank_full, rank_done = sem("top_st"), sem("chosen_done"), sem("rank_full"), sem("rank_done")
        pos_st, idx_done, sent = sem("pos_st"), sem("idx_done"), sem("sent")
        plan_st, table_full, table_done, pads_out, ends_done = sem("plan_st"), sem("table_full"), sem("table_done"), sem("pads_out"), sem("ends_done")
        gate_st, gexp_done = sem("gate_st"), sem("gexp_done")
        tile_in = [sem(f"tile_in{i}") for i in range(SLOTS)]
        tile_out = [sem(f"tile_out{i}") for i in range(SLOTS)]
        tT_full, tT_done, ridx_done, w1_done = sem("tT_full"), sem("tT_done"), sem("ridx_done"), sem("w1_done")
        h_full, gelu_done, y_full, y_done = sem("h_full"), sem("gelu_done"), sem("y_full"), sem("y_done")
        back = [sem(f"back{i}") for i in range(NT // CHUNK)]
        weighed, summed, stored = sem("weighed"), sem("summed"), sem("stored")
        final = [sem(f"final{i}") for i in range(2)]

        def wait(eng, s, value):
            if isinstance(value, int) and value <= 0:
                return
            eng.wait_ge(s, value)

        def known_count(eng, value):
            return value if isinstance(value, int) else eng.compute_val(value)

        def wait_apart(eng, s, value):
            if isinstance(value, int):
                wait(eng, s, value)
                return
            value = known_count(eng, value)
            eng.wait_ge(ld_c, 16)
            eng.wait_ge(s, value)

        def pipeline(eng, step):
            step(0, 0)
            step(1, 1)
            with eng.Fori(0, (NB - 6) // 2) as i:
                for odd in range(2):
                    step(i * 2 + (2 + odd), odd)
            for b in range(NB - 4, NB + 2):
                step(b, b % 2)

        def tile_pipeline(eng, step):
            turns = TILES // UNROLL
            for k in range(UNROLL):
                step(0, k)
            with eng.Fori(1, turns - 1) as turn:
                for k in range(UNROLL):
                    step(turn, k)
            for k in range(UNROLL + 1):
                step(turns - 1 + k // UNROLL, k % UNROLL)

        def chunk(c):
            n = CHUNK * TOPK * D
            return w1[:, :, :].rearrange("p e f -> p (e f)")[:, c * n:(c + 1) * n].rearrange("p (t k d) -> p t k d", t=CHUNK, k=TOPK)

        class Tile:
            def __init__(self, turn, k, ahead):
                self.n = turn * UNROLL + (k + ahead)
                self.round, self.slot = turn * (UNROLL // SLOTS) + (k + ahead) // SLOTS, (k + ahead) % SLOTS
                self.pair = self.slot % 2
                self.real = not isinstance(self.n, int) or 0 <= self.n < TILES

        def expert_of(eng, tile):
            return eng.value_load(table[0:1, 0, bass.ds(tile.n, 1)], min_val=0, max_val=NE - 1)

        class Held:
            def __init__(self, b):
                known = isinstance(b, int)
                self.attend, self.lead, self.project, self.normalise = (not known or b + i < NB for i in range(4))
                self.route, self.send = (not known or 0 <= b - i < NB for i in (1, 2))

        def leading(b, s, q):
            return (b, s, q + 2) if q < 2 else (b + 1, 1 - s, q - 2)

        def turning(b, s, q):
            return (b, s, q + 1) if q < NQ - 1 else (b + 1, 1 - s, 0)

        SP_PADS = 16

        def pad(eng, first, last):
            eng.wait_ge(ends_done, 1)
            with eng.Fori(0, (last - first) // 4) as i:
                for k in range(4):
                    end = eng.value_load(ends[0:1, bass.ds(i * 4 + (first + k), 1)], min_val=0, max_val=NE * REG - (P + S))
                    eng.dma_start(dispatched[bass.ds(end, P + S), :].rearrange("(k p) w -> p k w", p=P),
                                  padt[:, None, :].broadcast_to([P, 1 + QT, ROWW])).then_inc(pads_out, 16)

        block = ctx.enter_context(nc.Block())

        @block.sync
        def _(sp):
            xv = x_in.rearrange("p (t d) -> p t d", t=NT)
            sp.dma_start(x_all[:, 0:2 * QT, :], xv[:, 0:2 * QT, :]).then_inc(ld_x0, 16)
            sp.dma_start(consts[:, 0:C_COS], c_in[:, 0:C_COS]).then_inc(ld_id, 16)
            sp.dma_start(wts[:, 0:W_O], w_in[:, 0:W_O]).then_inc(ld_w, 16)
            sp.dma_start(wts[:, W_O:NW], w_in[:, W_O:NW]).then_inc(ld_w, 16)
            sp.dma_start(consts[:, C_COS:NCONST], c_in[:, C_COS:NCONST]).then_inc(ld_c, 16)
            sp.dma_start(brow[:, :], r_in.partition_broadcast(P)).then_inc(ld_r, 16)
            sp.dma_start(x_all[:, 2 * QT:NT, :], xv[:, 2 * QT:NT, :]).then_inc(ld_x, 16)
            sp.dma_start(rows[:, :, :], rows_in.rearrange("p (t k) -> p t k", t=NT)).then_inc(ld_x, 16)
            w1v = w1_in.rearrange("p (e f) -> p e f", e=NE)
            w2v = w2_in.rearrange("p (e c d) -> p e c d", e=NE, c=FC)

            def spread_rows(m, s):
                done, read, scored = (known_count(sp, n) for n in ((m + 1), m * SPREAD, (m - 1) * H))
                stores = known_count(sp, (m + 1) * 16)
                wait(sp, part3_done, done)
                wait(sp, spread_in, read)
                sp.dma_start(parts_out.rearrange("z i (p s) -> p (z i) s", s=S),
                             qkp[:, :, :, :].rearrange("p z i s -> p (z i) s")).then_inc(stored_parts, 16)
                wait(sp, stored_parts, stores)
                wait(sp, s2_full, scored)
                q, k = parts_out[0], parts_out[1]
                w = NP * HD
                for i in range(NP):
                    sp.dma_start(qrows[s][w * i:w * (i + 1), :, :],
                                 q[i][None, :].broadcast_to([NP, D * S])).then_inc(spread_in, 16)
                sp.dma_start(krows[s][0:KR, :, :],
                             k.rearrange("i f -> (i f)")[None, :].broadcast_to([NP, NP * D * S])).then_inc(spread_in, 16)

            def step(b, s):
                held = Held(b)
                if held.project and not (isinstance(b, int) and b < 2):
                    e = (b - 2) * (NE // (NB - 4))
                    sp.dma_start(w1[:, bass.ds(e, NE // (NB - 4)), 0:DF], w1v[:, bass.ds(e, NE // (NB - 4)), :]).then_inc(ld_w1, 16)
                if held.project:
                    spread_rows(b + 2, s)
                if isinstance(b, int) and b < 2:
                    e = slice(b * NE // 2, (b + 1) * NE // 2)
                    sp.dma_start(w1[:, e, DF:DF + D], b2_in.partition_broadcast(P).rearrange("p (e d) -> p e d", e=NE)[:, e, :]
                                 ).then_inc(ld_b2, 16)
                if isinstance(b, int) and NB - 4 <= b < NB:
                    n = (NE - IN_USE) // 4
                    e = IN_USE + n * (b - (NB - 4))
                    sp.dma_start(w2[:, e:e + n, :, :], w2v[:, e:e + n, :, :]).then_inc(ld_w2, 16)

            sp.wait_ge(neg_st, 1)
            spread_rows(0, 0)
            spread_rows(1, 1)
            pipeline(sp, step)
            def second_weights(first, last):
                for e in range(first, last, 4):
                    sp.dma_start(w2[:, e:e + 4, :, :], w2v[:, e:e + 4, :, :]).then_inc(ld_w2, 16)

            sp.wait_ge(s2_full, NB * H)
            second_weights(0, IN_USE // 2)
            sp.wait_ge(plan_st, PADT)
            sp.dma_start(dispatched[NE * REG:NE * REG + P, :], padt[:, :]).then_inc(pads_out, 16)
            pad(sp, 0, SP_PADS)
            second_weights(IN_USE // 2, IN_USE)
            sp.wait_ge(table_done, 1)
            sp.wait_ge(sent, QT * TOPK * 16 * NB)

            def step(turn, k):
                t = Tile(turn, k, 0)
                if not t.real:
                    return
                first = sp.value_load(table[0:1, 1, bass.ds(t.n, 1)], min_val=0, max_val=NE * REG)
                wait(sp, tT_full, t.n - (SLOTS - 1))
                wait(sp, ridx_done, t.n - (SLOTS - 1))
                sp.dma_start(tin[t.slot][:, :], dispatched[bass.ds(first, P), :]).then_inc(tile_in[t.slot], 16)

            tile_pipeline(sp, step)
            for u in range(SLOTS):
                sp.wait_ge(tile_out[u], 16 * (TILES // SLOTS))
            sp.wait_ge(w1_done, TILES)
            rv = results.rearrange("(t p k) d -> p t (k d)", p=P, k=TOPK)
            for c in range(NT // CHUNK):
                sp.dma_start(chunk(c).rearrange("p t k d -> p t (k d)"), rv[:, c * CHUNK:(c + 1) * CHUNK, :]).then_inc(back[c], 16)
            ov = out.rearrange("p (t d) -> p t d", t=NT)
            for c in range(NT // CHUNK):
                sp.wait_ge(final[c % 2], c // 2 + 1)
                sp.dma_start(ov[:, c * CHUNK:(c + 1) * CHUNK, :], x_all[:, c * CHUNK:(c + 1) * CHUNK, :]).then_inc(stored, 16)
            sp.wait_ge(stored, 16 * (NT // CHUNK))

        @block.tensor
        def _(pe):
            def pass1(m, s, h):
                if h == 0:
                    wait(pe, spread_in, (m + 1) * SPREAD)
                wait(pe, max_done, m * H + (h - 1))
                for t in range(QT):
                    mm = nc.tensor.matmul(s1[h % 2][:, t, :], qrows[s][0:KR, h, t * P:(t + 1) * P],
                                          krows[s][0:KR, h, :], start=True, stop=True)
                mm.then_inc(s1_full, 1)

            def turn_max(m, s, j):
                wait(pe, split_done, m * NQ + (j + 1))
                wait(pe, mt_done, m * NQ + j)
                for t in range(QT):
                    mm = nc.tensor.matmul(mturn[:, t * P:(t + 1) * P], mxp[j % 2][:, t, :, :].rearrange("p i g -> p (i g)"),
                                          ident16[:, :], start=True, stop=True)
                mm.then_inc(mt_full, 1)

            def pass2(b, s, h):
                if h % NG == 0:
                    wait(pe, max_in[h // NG], (b + 1) * 16)
                wait(pe, exp_done, b * H + (h - 1))
                for t in range(QT):
                    mm = nc.tensor.matmul(s2[h % 2][:, t, :], krows[s][0:KR + NP, h, t * P:(t + 1) * P],
                                          qrows[s][0:KR + NP, h, :], start=True, stop=True)
                mm.then_inc(s2_full, 1)

            def weigh(b, s, h):
                r, i = divmod(h // 2, NG)
                if h == 0:
                    wait(pe, v_done, b + 1)
                    wait(pe, pv_done, b)
                wait(pe, exp_done, b * H + (h + 2))
                for t in range(QT):
                    for c in range(2):
                        mm = nc.tensor.matmul(pv[2 * QW * c:2 * QW * (c + 1), r, :],
                                              vm[s][:, t, 2 * r + c, 2 * QW * i:2 * QW * (i + 1)],
                                              pr[h // NG % 2][:, h % NG + c, t, :],
                                              start=(i == 0 and t == 0), stop=(i == NG - 1 and t == QT - 1), skip_group_check=True)
                mm.then_inc(pv_full, 2)

            def x_turned(b):
                wait(pe, xn_done, b + 1)
                wait(pe, vst_done, b)
                for t in range(QT):
                    mm = nc.tensor.transpose(pb[:, t * P:(t + 1) * P], xn[:, t, :], ident)
                mm.then_inc(xT_full, 1)

            def compress(b):
                wait(pe, xT_done, b + 1)
                nc.tensor.matmul(pb[:, 0:S], wts[:, W_D:W_D + P], xnT[:, :], start=True, stop=True).then_inc(ct_full, 1)

            def rotary(b, turned, full):
                if turned:
                    wait(pe, r1_done, b + 1)
                else:
                    wait(pe, ct_done, b + 1)
                wq = W_U + (1 + turned) * P
                wk = W_KR + turned * P
                nc.tensor.matmul(pb[:, 0:S], wts[:, wq:wq + P], ct[:, :], start=True, stop=True)
                nc.tensor.matmul(pb[:, S:2 * S], wts[:, wk:wk + P], xnT[:, :], start=True, stop=True).then_inc(full, 1)

            def plain(b):
                wait(pe, r2_done, b + 1)
                nc.tensor.matmul(pb[:, 0:S], wts[:, W_U:W_U + P], ct[:, :], start=True, stop=True)
                nc.tensor.matmul(pb[:, S:2 * S], wts[:, W_U + 3 * P:W_U + 4 * P], ct[:, :], start=True, stop=True).then_inc(qk_full, 1)

            def values(b):
                wait(pe, qk_done, b + 1)
                for t in range(QT):
                    mm = nc.tensor.matmul(pb[:, t * P:(t + 1) * P], ct[:, t * P:(t + 1) * P],
                                          wts[:, W_U + 4 * P:W_U + 5 * P], start=True, stop=True)
                mm.then_inc(v_full, 1)

            def project_out(b):
                wait(pe, norm_st, b + 1)
                wait(pe, rank_done, b + 1)
                for t in range(QT):
                    mm = nc.tensor.matmul(pa[:, t * P:(t + 1) * P], outT[:, t * P:(t + 1) * P],
                                          wts[:, W_O:W_O + P], start=True, stop=True)
                mm.then_inc(wo_full, 1)

            def x2_turned(b, s):
                wait(pe, xn2_done, b + 1)
                for t in range(QT):
                    mm = nc.tensor.transpose(pa[:, t * P:(t + 1) * P], pay[:, t, 0, 0:D], ident)
                mm.then_inc(x2T_full, 1)

            def gate(b):
                wait(pe, x2T_done, b + 1)
                for t in range(QT):
                    mm = nc.tensor.matmul(pa[:, t * NE:(t + 1) * NE], xn2T[:, t * P:(t + 1) * P],
                                          wts[:, W_G:W_G + NE], start=True, stop=True)
                mm.then_inc(gate_full, 1)

            def rank(b):
                wait(pe, chosen_done, b + 1)
                w = QT * NE
                nc.tensor.matmul(pa[:, 0:w], tri16[:, :], chosen[:, :, :].rearrange("p t e -> p (t e)"),
                                 start=True, stop=False, skip_group_check=True)
                nc.tensor.matmul(pa[:, NE:w], one16[:, :], chosen[:, 0, :], start=False, stop=False, skip_group_check=True)
                nc.tensor.matmul(pa[:, w:w + NE], one16[:, :], chosen[:, 0, :], start=False, stop=False, skip_group_check=True)
                nc.tensor.matmul(pa[:, w:w + NE], one16[:, :], chosen[:, 1, :], start=False, stop=True,
                                 skip_group_check=True).then_inc(rank_full, 1)

            def step(b, s):
                held = Held(b)
                for h in range(H):
                    q, g = divmod(h, NG)
                    if held.attend if q < 2 else held.lead:
                        m, ms, j = leading(b, s, q)
                        pass1(m, ms, NG * j + g)
                    if held.attend:
                        pass2(b, s, h)
                    if g == 1 and (held.lead if q == NQ - 1 else held.attend):
                        turn_max(*turning(b, s, q))
                    if g % 2 == 1:
                        if q == 0 and held.route:
                            weigh(b - 1, 1 - s, H - NG + g - 1)
                        elif q > 0 and held.attend:
                            weigh(b, s, h - NG - 1)
                    if held.project:
                        if (q, g) == (0, 0):
                            x_turned(b + 2)
                        elif (q, g) == (0, 2):
                            compress(b + 2)
                        elif (q, g) == (1, 1):
                            rotary(b + 2, 0, r1_full)
                        elif (q, g) == (2, 0):
                            rotary(b + 2, 1, r2_full)
                        elif (q, g) == (2, 3):
                            plain(b + 2)
                        elif (q, g) == (3, 1):
                            values(b + 2)
                    if held.send:
                        if (q, g) == (0, 1):
                            gate(b - 2)
                        elif (q, g) == (1, 0):
                            rank(b - 2)
                    if held.route:
                        if (q, g) == (2, 1):
                            project_out(b - 1)
                        elif (q, g) == (3, 3):
                            x2_turned(b - 1, 1 - s)

            pe.wait_ge(ld_id, 16)
            pe.wait_ge(ld_w, 32)
            pe.wait_ge(set_v, 8)
            for m in range(2):
                x_turned(m)
                compress(m)
                rotary(m, 0, r1_full)
                rotary(m, 1, r2_full)
                if m == 1:
                    for h in range(NG):
                        pass1(0, 0, h)
                plain(m)
                values(m)
            turn_max(0, 0, 0)
            for h in range(NG, 2 * NG):
                pass1(0, 0, h)
            pipeline(pe, step)

            pe.wait_ge(plan_st, PLAN)
            pe.wait_ge(rank_done, NB + 1)
            for i in range(2):
                mm = nc.tensor.transpose(pa[0:1, i * P:(i + 1) * P], place_[:, i:i + 1], ident)
            mm.then_inc(table_full, 1)
            pe.wait_ge(table_done, 1)
            pe.wait_ge(ld_w2, 16 * (4 + IN_USE // 4))

            def turn_tile(t):
                wait(pe, tile_in[t.slot], (t.round + 1) * 16)
                wait(pe, tT_done, t.n - 1)
                nc.tensor.transpose(tps[t.pair][:, 0:P], tin[t.slot][:, 0:D], ident).then_inc(tT_full, 1)

            def hidden(t):
                wait(pe, tT_done, t.n + 1)
                wait(pe, w1_done, t.n + 1)
                wait(pe, gelu_done, t.n - 1)
                for c in range(FC):
                    mm = nc.tensor.matmul(hps[t.pair][:, :, :].rearrange("p a s -> p (a s)")[:, c * P:(c + 1) * P],
                                          w1s[t.slot % 4][:, c * P:(c + 1) * P], tT[t.pair], start=True, stop=True)
                mm.then_inc(h_full, 1)

            def result(t, e):
                wait(pe, gelu_done, t.n + 1)
                wait(pe, y_done, t.n - 1)
                for c in range(FC):
                    mm = nc.tensor.matmul(yps[t.pair][:, 0, 0:D], hT[t.pair][:, c, :],
                                          w2[:, bass.ds(e, 1), c, :].rearrange("p o d -> p (o d)"), start=(c == 0), stop=(c == FC - 1))
                mm.then_inc(y_full, 1)

            def tile_step(turn, k):
                after, now, before = Tile(turn, k, 1), Tile(turn, k, 0), Tile(turn, k, -1)
                if before.real:
                    e = expert_of(pe, before)
                if after.real:
                    turn_tile(after)
                if now.real:
                    hidden(now)
                if before.real:
                    result(before, e)

            turn_tile(Tile(0, 0, 0))
            tile_pipeline(pe, tile_step)

        @block.scalar
        def _(act):
            def exponents(b, h):
                if h % NG == 0:
                    wait(act, pv_full, b * H + (h - NG))
                wait(act, s2_full, b * H + (h + 1))
                nc.scalar.activation(pr[h // NG % 2][:, h % NG, :, :], s2[h % 2][:, :, :], ACT.Exp,
                                     scale=SCALE).then_inc(exp_done, 1)

            def take_maxima(m, s, j):
                wait(act, mt_full, m * NQ + (j + 1))
                if j < 2:
                    wait(act, max_in[j + 2], m * 16)
                else:
                    wait(act, max_in[j - 2], (m + 1) * 16)
                nc.scalar.copy(mrow[j % 2][:, :], mturn).then_inc(mt_done, 1)
                wait(act, mt_done, m * NQ + (j + 1))
                act.dma_start(qrows[s][KR:KR + NP, NG * j:NG * j + NG, :], mrow[j % 2][:, :]).then_inc(max_in[j], 16)

            def first_part(b):
                wait(act, qk_done, b + 1)
                wait(act, stored_parts, b * 16)
                nc.scalar.copy(qkp[:, :, 0, :], qk[:, :].rearrange("p (z s) -> p z s", z=2)).then_inc(part1_done, 1)

            def second_part(b):
                wait(act, rest_done, b + 1)
                nc.scalar.copy(qkp[:, :, 1, :], rest[:, :].rearrange("p (z s) -> p z s", z=2)).then_inc(part2_done, 1)

            def take_xT(b):
                wait(act, xT_full, b + 1)
                nc.scalar.copy(xnT[:, :], pb[:, 0:S]).then_inc(xT_done, 1)

            def take_ct(b):
                wait(act, ct_full, b + 1)
                nc.scalar.activation(ct[:, :], pb[:, 0:S], ACT.Identity, bias=wts[:, W_B:W_B + 1]).then_inc(ct_done, 1)

            def spread_sums(b):
                wait(act, pv_done, b + 1)
                wait(act, norm_st, b)
                for j in range(NQ):
                    r = QW * (2 * (j % 2) + 1)
                    last = nc.scalar.copy(sums[QW * j:QW * (j + 1), :], weighed_sb[r:r + QW, j // 2, :])
                last.then_inc(sums_done, 1)

            def spread_weighted(b):
                wait(act, wo_full, b)
                for j in range(NQ):
                    r = 2 * QW * (j % 2)
                    last = nc.scalar.copy(outT[QW * j:QW * (j + 1), :], weighed_sb[r:r + QW, j // 2, :])
                last.then_inc(nums_done, 1)

            def take_x2T(b):
                wait(act, x2T_full, b + 1)
                nc.scalar.copy(xn2T[:, :], pa[:, 0:S]).then_inc(x2T_done, 1)

            def step(b, s):
                held = Held(b)
                for h in range(H):
                    q, g = divmod(h, NG)
                    if held.attend:
                        exponents(b, h)
                    if g == 1 and (held.lead if q == NQ - 1 else held.attend):
                        take_maxima(*turning(b, s, q))
                    if held.send and (q, g) == (0, 0):
                        take_x2T(b - 2)
                    if held.project:
                        if (q, g) == (0, 0):
                            wait(act, vst_done, b + 2)
                            take_xT(b + 2)
                        elif (q, g) == (0, 3):
                            take_ct(b + 2)
                        elif (q, g) == (3, 2):
                            first_part(b + 2)
                        elif (q, g) == (3, 3):
                            second_part(b + 2)
                    if held.route:
                        if (q, g) == (1, 1):
                            spread_sums(b - 1)
                        elif (q, g) == (1, 2):
                            spread_weighted(b - 1)

            act.wait_ge(ld_w, 32)
            for m in range(2):
                wait(act, vst_done, m)
                take_xT(m)
                take_ct(m)
                first_part(m)
                second_part(m)
            take_maxima(0, 0, 0)
            pipeline(act, step)

            act.wait_ge(plan_st, PADT)
            pad(act, SP_PADS, NE)
            act.wait_ge(gate_st, 1)
            nc.scalar.activation(gtmp[:, 1, :], gtmp[:, 0, :], ACT.Exp).then_inc(gexp_done, 1)
            act.wait_ge(table_done, 1)

            def tile_step(turn, k):
                t = Tile(turn, k, 0)
                if not t.real:
                    return
                e = expert_of(act, t)
                wait(act, h_full, t.n + 1)
                wait(act, y_full, t.n - 1)
                for c in range(FC):
                    last = nc.scalar.activation(hT[t.pair][:, c, :], hps[t.pair][:, :, :].rearrange("p a s -> p (a s)")[:, c * P:(c + 1) * P],
                                                ACT.Gelu, bias=wts[:, bass.ds(e * FC + (W_B1 + c), 1)])
                last.then_inc(gelu_done, 1)

            tile_pipeline(act, tile_step)

            act.wait_ge(gate_st, 4)
            for c in range(NT // CHUNK):
                act.wait_ge(back[c], 16)
                for i in range(CHUNK):
                    t = c * CHUNK + i
                    y = chunk(c)[:, i, 1, :]
                    last = nc.scalar.activation(y, y, ACT.Copy, scale=gates[:, t, 1:2])
                last.then_inc(weighed, 1)

        @block.vector
        def _(dve):
            def maximum(m, s, j, g):
                h = NG * j + g
                wait(dve, s1_full, m * H + (h + 1))
                nc.vector.tensor_reduce(mx[j % 2][:, :, g], s1[h % 2][:, :, :], AX.X, ALU.max).then_inc(max_done, 1)

            def split_maxima(m, s, j):
                n = m * NQ + j
                x, xp = mx[j % 2][:, :, :], mxp[j % 2]
                wait(dve, max_done, m * H + NG * (j + 1))
                wait(dve, mt_full, n - 1)
                nc.vector.tensor_copy(xp[:, :, 0, :], x).then_inc(split_st, 1)
                wait(dve, split_st, n * 3 + 1)
                nc.vector.tensor_tensor(xp[:, :, 1, :], x, xp[:, :, 0, :], ALU.subtract).then_inc(split_st, 1)
                nc.vector.tensor_tensor(mrest[:, :, :], x, xp[:, :, 0, :], ALU.subtract).then_inc(split_st, 1)
                wait(dve, split_st, n * 3 + 3)
                nc.vector.tensor_tensor(xp[:, :, 2, :], mrest[:, :, :], xp[:, :, 1, :], ALU.subtract).then_inc(split_done, 1)

            def stats(b, st, mv, done):
                for t in range(QT):
                    nc.vector.bn_stats(st[:, t, :], x_all[:, bass.ds(b * QT + t, 1), :].rearrange("p o d -> p (o d)")).then_inc(done, 1)
                wait_apart(dve, done, b * 2 * QT + QT)
                for t in range(QT):
                    nc.vector.bn_aggr(mv[:, t, :], st[:, t, :]).then_inc(done, 1)

            def stats_x(first, last, before):
                for t in range(first, last):
                    nc.vector.bn_stats(st1[:, t, :], x_all[:, t, :]).then_inc(ln1_st, 1)
                dve.wait_ge(ln1_st, before + last - first)
                for t in range(first, last):
                    nc.vector.bn_aggr(mv1[:, t, :], st1[:, t, :]).then_inc(ln1_st, 1)

            def normalise_x(b):
                dve.wait_ge(rstd1_st, 2 if isinstance(b, int) and b < 2 else 4)
                wait(dve, xT_full, b)
                for t in range(QT):
                    last = nc.vector.tensor_scalar(xn[:, t, :], x_all[:, bass.ds(b * QT + t, 1), :].rearrange("p o d -> p (o d)"),
                                                   mv1[:, bass.ds(b * QT + t, 1), 0:1].rearrange("p o d -> p (o d)"),
                                                   rstd1[:, bass.ds(b * QT + t, 1)], ALU.subtract, ALU.mult)
                last.then_inc(xn_done, 1)

            def take_rotary(b, full, turn, col, done, free):
                wait(dve, full, b + 1)
                wait(dve, turn_st, b * 2)
                if free:
                    wait(dve, qk_done, b)
                nc.vector.tensor_tensor(turn[:, :], pb[:, :], consts[:, col:col + 2 * S], ALU.mult).then_inc(done, 1)

            def take_qk(b):
                wait(dve, qk_full, b + 1)
                wait(dve, turn_st, (b + 1) * 2)
                wait(dve, rest_done, b)
                nc.vector.tensor_tensor(qk[:, :], pb[:, :], turn1[:, :], ALU.add).then_inc(qk_done, 1)

            def take_values(b):
                wait(dve, v_full, b + 1)
                wait(dve, v_done, b)
                nc.vector.tensor_tensor(vst[:, :, :], pb[:, 0:S].rearrange("p (t d) -> p t d", t=QT),
                                        brow[:, None, R_V:R_V + P].broadcast_to([P, QT, D]), ALU.add).then_inc(vst_done, 1)

            def take_weighted(b):
                wait(dve, pv_full, (b + 1) * H)
                wait(dve, part3_done, min(b + 3, NB) if isinstance(b, int) else b + 3)
                nc.vector.tensor_copy(weighed_sb, pv[:, :, :]).then_inc(pv_done, 1)

            def invert_sums(b, t):
                if t == 0:
                    wait(dve, sums_done, b + 1)
                half = sums[:, t * P:(t + 1) * P]
                nc.vector.reciprocal(half, half).then_inc(inv_st, 1)

            def normalise_out(b):
                wait(dve, nums_done, b + 1)
                wait(dve, inv_st, (b + 1) * QT)
                nc.vector.tensor_tensor(outT[:, :], outT[:, :], sums[:, :], ALU.mult).then_inc(norm_st, 1)

            def take_out(b):
                wait(dve, wo_full, b + 1)
                wait(dve, xb_done, b + 1)
                xs = x_all[:, bass.ds(b * QT, QT), :]
                nc.vector.tensor_tensor(xs, pa[:, 0:S].rearrange("p (t d) -> p t d", t=QT), xs, ALU.add).then_inc(x2_done, 1)
                wait_apart(dve, x2_done, b + 1)
                stats(b, st2, mv2, ln2_st)

            def normalise_rows(b):
                wait(dve, rstd2_st, (b + 1) * 2)
                wait(dve, sent, b * (QT * TOPK * 16))
                for t in range(QT):
                    src = x_all[:, bass.ds(b * QT + t, 1), :].broadcast_to([P, TOPK, D])
                    last = nc.vector.tensor_scalar(pay[:, t, :, 0:D], src, mv2[:, t, 0:1], rstd2[:, t:t + 1],
                                                   ALU.subtract, ALU.mult)
                last.then_inc(xn2_done, 1)

            TOP = 8

            def choose(b):
                wait(dve, gate_full, b + 1)
                nc.vector.tensor_tensor(sc[:, :, :], pa[:, 0:QT * NE].rearrange("p (t e) -> p t e", t=QT),
                                        brow[:, None, R_G:R_G + NE].broadcast_to([P, QT, NE]), ALU.add).then_inc(sc_done, 1)
                wait_apart(dve, sc_done, b + 1)
                for t in range(QT):
                    nc.vector.max(top8[:, t, :], sc[:, t, :]).then_inc(top_st, 1)
                wait_apart(dve, top_st, b * TOP + 2)
                for t in range(QT):
                    nc.vector.max_index(arg8[:, t, :], top8[:, t, :], sc[:, t, :]).then_inc(top_st, 1)

            def mark(b):
                nc.vector.tensor_copy(top_all[:, bass.ds(b * QT, QT), :], top8[:, :, 0:TOPK]).then_inc(top_st, 1)
                wait(dve, top_st, b * TOP + 5)
                nc.vector.tensor_copy(argf[:, :, :], arg8[:, :, 0:TOPK]).then_inc(top_st, 1)
                wait(dve, top_st, b * TOP + 6)
                nc.vector.tensor_tensor(oh[:, :, :], argf[:, :, :].rearrange("p t k -> p (t k)")[:, :, None].broadcast_to([P, QT * TOPK, NE]),
                                        consts[:, None, C_EXP:C_EXP + NE].broadcast_to([P, QT * TOPK, NE]), ALU.is_equal).then_inc(top_st, 1)
                wait(dve, top_st, b * TOP + 7)
                wait(dve, rank_full, b)
                ov = oh[:, :, :].rearrange("p (t k) e -> p t k e", k=TOPK)
                nc.vector.tensor_tensor(chosen[:, :, :], ov[:, :, 0, :], ov[:, :, 1, :], ALU.add).then_inc(chosen_done, 1)
                nc.vector.engine_nop().then_inc(top_st, 1)

            POS = 3

            def place(b, s):
                wait(dve, rank_full, b + 1)
                wait(dve, rank_done, b + 1)
                nc.vector.tensor_tensor(rk[s][:, :, :], pa[:, 0:(QT + 1) * NE].rearrange("p (t e) -> p t e", e=NE),
                                        rk[1 - s][:, QT:QT + 1, :].broadcast_to([P, QT + 1, NE]), ALU.add).then_inc(rank_done, 1)
                wait(dve, rank_done, b + 2)
                nc.vector.tensor_tensor(ohrk[:, :, :].rearrange("p (t k) e -> p t k e", k=TOPK),
                                        oh[:, :, :].rearrange("p (t k) e -> p t k e", k=TOPK),
                                        rk[s][:, 0:QT, None, :].broadcast_to([P, QT, TOPK, NE]), ALU.mult).then_inc(pos_st, 1)
                wait(dve, pos_st, b * POS + 1)
                nc.vector.tensor_reduce(posf[:, :], ohrk[:, :, :], AX.X, ALU.add).then_inc(pos_st, 1)
                wait(dve, pos_st, b * POS + 2)
                nc.vector.tensor_copy(pos[:, :], posf[:, :]).then_inc(pos_st, 1)

            def step(b, s):
                held = Held(b)
                for h in range(H):
                    q, g = divmod(h, NG)
                    if held.project and (q, g) == (3, 0):
                        take_qk(b + 2)
                    if held.attend if q < 2 else held.lead:
                        maximum(*leading(b, s, q), g)
                        if g == NG - 1:
                            split_maxima(*leading(b, s, q))
                            if held.route and q == 0:
                                take_weighted(b - 1)
                    elif held.route and (q, g) == (0, 3):
                        take_weighted(b - 1)
                    if held.send:
                        if (q, g) == (0, 1):
                            choose(b - 2)
                        elif (q, g) == (0, 2):
                            mark(b - 2)
                        elif (q, g) == (1, 1):
                            place(b - 2, s)
                            if isinstance(b, int) and b == NB:
                                dve.wait_ge(rank_done, NB)
                                nc.vector.tensor_copy(ends[:, :], rk[s][0:1, QT, :]).then_inc(ends_done, 1)
                    if held.project:
                        if (q, g) == (1, 2):
                            take_rotary(b + 2, r1_full, turn1, C_COS, r1_done, True)
                        elif (q, g) == (2, 1):
                            take_rotary(b + 2, r2_full, turn2, C_SIN, r2_done, False)
                        elif (q, g) == (3, 2):
                            take_values(b + 2)
                    if held.route:
                        if (q, g) in ((1, 2), (1, 3)):
                            invert_sums(b - 1, g - 2)
                        elif (q, g) == (2, 0):
                            normalise_out(b - 1)
                        elif (q, g) == (2, 2):
                            take_out(b - 1)
                        elif (q, g) == (3, 1):
                            normalise_rows(b - 1)
                    if held.normalise and (q, g) == (3, 2):
                        normalise_x(b + 3)

            links = [0]

            def link(ins):
                links[0] += 1
                ins.then_inc(plan_st, 1)
                dve.wait_ge(plan_st, links[0])

            for i in range(2):
                nc.vector.memset(vm[i][:, :, :, :], 0.0).then_inc(set_v, 1)
            dve.wait_ge(set_v, 2)
            for i in range(2):
                nc.vector.memset(own_columns(i, QW), 1.0).then_inc(set_v, 1)
            dve.wait_ge(ld_x0, 16)
            early = 2 * QT
            stats_x(0, early, 0)
            dve.wait_ge(ld_c, 16)
            nc.vector.tensor_copy(tri16[:, :], consts[:, C_TRI:C_TRI + P]).then_inc(set_v, 1)
            nc.vector.tensor_copy(one16[:, :], consts[:, C_ONE:C_ONE + P]).then_inc(set_v, 1)
            nc.vector.tensor_copy(ident16[:, :], ident).then_inc(set_v, 1)
            nc.vector.tensor_copy(rk[1][:, QT, :], consts[:, C_BASE:C_BASE + NE]).then_inc(rank_done, 1)
            nc.vector.memset(pay[:, :, :, D:ROWW], 0.0).then_inc(set_v, 1)
            normalise_x(0)
            dve.wait_ge(ld_w, 32)
            for i in range(2):
                c = W_B + 1 + 3 * i
                nc.vector.tensor_scalar(biasqk[:, i, :], consts[:, C_COS:C_COS + S], wts[:, c + 1:c + 2], wts[:, c:c + 1],
                                        ALU.mult, ALU.add).then_inc(bias_st, 1)
            dve.wait_ge(bias_st, 2)
            for i in range(2):
                c = W_B + 1 + 3 * i
                nc.vector.scalar_tensor_tensor(biasqk[:, i, :], consts[:, C_SIN:C_SIN + S], wts[:, c + 2:c + 3],
                                               biasqk[:, i, :], ALU.mult, ALU.add).then_inc(bias_st, 1)
            take_rotary(0, r1_full, turn1, C_COS, r1_done, True)
            normalise_x(1)
            take_rotary(0, r2_full, turn2, C_SIN, r2_done, False)
            dve.wait_ge(ld_x, 32)
            half = (early + NT) // 2
            stats_x(early, half, 2 * early)
            take_qk(0)
            dve.wait_ge(ld_r, 16)
            take_values(0)
            stats_x(half, NT, 2 * half)
            take_rotary(1, r1_full, turn1, C_COS, r1_done, True)
            take_rotary(1, r2_full, turn2, C_SIN, r2_done, False)
            for g in range(NG):
                maximum(0, 0, 0, g)
            split_maxima(0, 0, 0)
            take_qk(1)
            take_values(1)
            for g in range(NG):
                maximum(0, 0, 1, g)
            split_maxima(0, 0, 1)
            normalise_x(2)
            link(nc.vector.memset(padt[:, :], 0.0))
            link(nc.vector.tensor_copy(padt[:, D:D + 1].bitcast(U32), consts[:, C_PAD:C_PAD + 1]))
            assert links[0] == PADT
            pipeline(dve, step)

            after = rk[(NB - 1) % 2][:, QT, :]
            dve.wait_ge(rank_done, NB + 1)
            link(nc.vector.tensor_tensor(count[:, 0, :], after, consts[:, C_BASE:C_BASE + NE], ALU.subtract))
            link(nc.vector.tensor_scalar(counti[:, :], count[:, 0, :], float(P - 1), None, ALU.add))
            link(nc.vector.tensor_scalar(counti[:, :], counti[:, :], 7, None, ALU.arith_shift_right))
            link(nc.vector.tensor_copy(count[:, 1, :], counti[:, :]))
            link(nc.vector.tensor_tensor_scan(count[:, 2, :], consts[:, C_ONE:C_ONE + NE], count[:, 1, :], 0.0, ALU.mult, ALU.add))
            part = consts[:, C_PART:C_PART + 1]
            link(nc.vector.tensor_scalar(past[:, 0, :], count[:, 2, :], part, None, ALU.is_le))
            link(nc.vector.tensor_tensor(past[:, 1, :], past[:, 0, :], count[:, 1, :], ALU.mult))
            link(nc.vector.tensor_reduce(place_[:, 2:4], past[:, :, :], AX.X, ALU.add))
            link(nc.vector.tensor_scalar(place_[:, 0:1], place_[:, 2:3], float(NE - 1), None, ALU.min))
            link(nc.vector.tensor_tensor(place_[:, 3:4], part, place_[:, 3:4], ALU.subtract))
            link(nc.vector.tensor_scalar(place_[:, 2:3], place_[:, 2:3], float(REG), None, ALU.mult))
            link(nc.vector.scalar_tensor_tensor(place_[:, 1:2], place_[:, 3:4], float(P), place_[:, 2:3], ALU.mult, ALU.add))
            link(nc.vector.tensor_scalar(place_[:, 1:2], place_[:, 1:2], float(NE * REG), None, ALU.min))
            assert links[0] == PLAN
            dve.wait_ge(table_full, 1)
            nc.vector.tensor_copy(table[:, :, :].rearrange("p a s -> p (a s)"), pa[0:1, 0:2 * P]).then_inc(table_done, 1)
            nc.vector.tensor_tensor(gtmp[:, 0, :], top_all[:, :, 1], top_all[:, :, 0], ALU.subtract).then_inc(gate_st, 1)
            dve.wait_ge(table_done, 1)

            def take_tile(t):
                wait(dve, tT_full, t.n + 1)
                wait(dve, h_full, t.n - 1)
                nc.vector.tensor_copy(tT[t.pair], tps[t.pair][:, 0:P]).then_inc(tT_done, 1)
                wait(dve, tile_out[t.slot], t.round * 16)
                nc.vector.tensor_copy(ridx[t.slot][:, :], tin[t.slot][:, D:D + 1].bitcast(U32)).then_inc(ridx_done, 1)

            def take_weights(t, e):
                wait(dve, y_done, t.n - 3)
                nc.vector.tensor_copy(w1s[t.slot % 4], w1[:, bass.ds(e, 1), :].rearrange("p o f -> p (o f)")).then_inc(w1_done, 1)

            def take_result(t):
                wait(dve, y_full, t.n + 1)
                wait(dve, tile_out[t.slot], t.round * 16)
                nc.vector.tensor_tensor(yo[t.slot][:, :], yps[t.pair][:, 0, 0:D], w1s[t.slot % 4][:, DF:DF + D], ALU.add).then_inc(y_done, 1)

            def tile_step(turn, k):
                after, before = Tile(turn, k, 1), Tile(turn, k, -1)
                if after.real:
                    take_tile(after)
                    take_weights(after, expert_of(dve, after))
                if before.real:
                    take_result(before)

            dve.wait_ge(ld_b2, 32)
            dve.wait_ge(ld_w1, 16 * (NB - 4))
            t0 = Tile(0, 0, 0)
            take_weights(t0, expert_of(dve, t0))
            take_tile(t0)
            tile_pipeline(dve, tile_step)

            dve.wait_ge(gexp_done, 1)
            nc.vector.tensor_scalar(gtmp[:, 0, :], gtmp[:, 1, :], 1.0, None, ALU.add).then_inc(gate_st, 1)
            dve.wait_ge(gate_st, 2)
            nc.vector.reciprocal(gates[:, :, 0], gtmp[:, 0, :]).then_inc(gate_st, 1)
            dve.wait_ge(gate_st, 3)
            nc.vector.tensor_tensor(gates[:, :, 1], gtmp[:, 1, :], gates[:, :, 0], ALU.mult).then_inc(gate_st, 1)
            dve.wait_ge(gate_st, 4)
            for c in range(NT // CHUNK):
                dve.wait_ge(back[c], 16)
                dve.wait_ge(weighed, c + 1)
                y = chunk(c)
                for i in range(CHUNK):
                    t = c * CHUNK + i
                    last = nc.vector.scalar_tensor_tensor(y[:, i, 0, :], y[:, i, 0, :], gates[:, t, 0:1], y[:, i, 1, :],
                                                          ALU.mult, ALU.add)
                last.then_inc(summed, 1)
                if c % 2 == 0:
                    dve.wait_ge(summed, c + 1)
                    xs = x_all[:, c * CHUNK:(c + 1) * CHUNK, :]
                    nc.vector.tensor_tensor(xs, xs, y[:, :, 0, :], ALU.add).then_inc(final[0], 1)

        @block.gpsimd
        def _(pool):
            def deviation(mv, ve, rstd, done, before):
                n = ve.shape[1]
                nc.gpsimd.tensor_tensor(ve, mv, powers[:, 1, 0:n], ALU.add).then_inc(done, 1)
                wait(pool, done, before + 1)
                nc.gpsimd.tensor_tensor(rstd, ve, powers[:, 0, 0:n], ALU.pow).then_inc(done, 1)

            def deviation_rows(b):
                wait(pool, ln2_st, (b + 1) * 2 * QT)
                deviation(mv2[:, :, 1], ve2[:, :], rstd2[:, :], rstd2_st, b * 2)

            def deviation_x(first, last, before):
                pool.wait_ge(ln1_st, 2 * last)
                deviation(mv1[:, first:last, 1], ve1[:, first:last], rstd1[:, first:last], rstd1_st, before)

            def add_out_bias(b):
                wait(pool, xn_done, b + 1)
                xs = x_all[:, bass.ds(b * QT, QT), :]
                nc.gpsimd.tensor_tensor(xs, xs, brow[:, None, R_O:R_O + D].broadcast_to([P, QT, D]), ALU.add).then_inc(xb_done, 1)

            def sum_turns(b):
                wait(pool, r1_done, b + 1)
                nc.gpsimd.tensor_tensor(turn1[:, :], turn1[:, :], biasqk[:, :, :].rearrange("p i s -> p (i s)"),
                                        ALU.add).then_inc(turn_st, 1)
                wait(pool, r2_done, b + 1)
                wait(pool, turn_st, b * 2 + 1)
                nc.gpsimd.tensor_tensor(turn1[:, :], turn1[:, :], turn2[:, :], ALU.add).then_inc(turn_st, 1)

            def leave(b):
                wait(pool, part1_done, b + 1)
                wait(pool, part3_done, b)
                nc.gpsimd.tensor_tensor(rest[:, :].rearrange("p (z s) -> p z s", z=2), qk[:, :].rearrange("p (z s) -> p z s", z=2),
                                        qkp[:, :, 0, :], ALU.subtract).then_inc(rest_done, 1)

            def third_part(b):
                wait(pool, part2_done, b + 1)
                nc.gpsimd.tensor_tensor(qkp[:, :, 2, :], rest[:, :].rearrange("p (z s) -> p z s", z=2),
                                        qkp[:, :, 1, :], ALU.subtract).then_inc(part3_done, 1)

            def give_values(b, s):
                wait(pool, vst_done, b + 1)
                wait_apart(pool, pv_full, (b - 1) * H)
                nc.gpsimd.tensor_copy(own_columns(s, 0),
                                      vst[:, :, :].rearrange("p t (j g d) -> p (t j) g d", j=NQ, g=NG)).then_inc(v_done, 1)

            def send(b, s):
                wait(pool, xn2_done, b + 1)
                nc.gpsimd.tensor_copy(pay[:, :, :, D].bitcast(U32),
                                      rows[:, bass.ds(b * QT, QT), :]).then_inc(idx_done, 1)
                wait(pool, idx_done, b + 1)
                if isinstance(b, int) and b == NB - 1:
                    pool.wait_ge(pads_out, 16 * (NE + 1))
                wait_apart(pool, pos_st, (b + 1) * 3)
                for t in range(QT):
                    for k in range(TOPK):
                        n = t * TOPK + k
                        nc.gpsimd.indirect_dma_start(
                            dispatched, bass.IndirectOffsetOnAxis(ap=pos[:, n:n + 1], axis=0),
                            pay[:, t, k, :], None).then_inc(sent, 16)

            def step(b, s):
                held = Held(b)
                if held.send:
                    send(b - 2, s)
                if held.lead:
                    give_values(b + 1, 1 - s)
                if held.project:
                    add_out_bias(b + 2)
                    sum_turns(b + 2)
                if held.route:
                    deviation_rows(b - 1)
                if held.project:
                    leave(b + 2)
                    third_part(b + 2)

            nc.gpsimd.memset(powers[:, 0, :], -0.5).then_inc(set_p, 1)
            nc.gpsimd.memset(powers[:, 1, :], EPS).then_inc(set_p, 1)
            pool.wait_ge(set_p, 2)
            pool.wait_ge(set_v, 8)
            deviation_x(0, 2 * QT, 0)
            pool.wait_ge(rstd1_st, 2)
            nc.gpsimd.memset(spread[64:96, :, 1, :, :].rearrange("p i h s -> p i (h s)"), -1.0).then_inc(neg_st, 1)
            pool.wait_ge(neg_st, 1)
            pool.wait_ge(ld_r, 16)
            pool.wait_ge(bias_st, 4)
            for m in range(2):
                add_out_bias(m)
                sum_turns(m)
                leave(m)
                third_part(m)
                if m == 0:
                    give_values(0, 0)
                    deviation_x(2 * QT, NT, 2)
            pool.wait_ge(ld_x, 32)
            pipeline(pool, step)

            def tile_step(turn, k):
                t = Tile(turn, k, -1)
                if not t.real:
                    return
                wait_apart(pool, y_done, t.n + 1)
                nc.gpsimd.indirect_dma_start(results, bass.IndirectOffsetOnAxis(ap=ridx[t.slot][:, 0:1], axis=0),
                                             yo[t.slot][:, :], None, bounds_check=TOPK * T - 1,
                                             oob_is_err=False).then_inc(tile_out[t.slot], 16)

            tile_pipeline(pool, tile_step)
            for c in range(1, NT // CHUNK, 2):
                pool.wait_ge(summed, c + 1)
                xs = x_all[:, c * CHUNK:(c + 1) * CHUNK, :]
                nc.gpsimd.tensor_tensor(xs, xs, chunk(c)[:, :, 0, :], ALU.add).then_inc(final[1], 1)


def kernel(**inputs):
    import concourse.bacc as bacc
    from concourse.bass_utils import run_bass_kernel_spmd

    a = {k.split("_", 1)[1]: np.ascontiguousarray(v) for k, v in inputs.items()}
    x = a["attn_x"].reshape(NT, P, D).transpose(1, 0, 2).reshape(P, NT * D)

    def turned(w):
        return w.reshape(*w.shape[:-1], D // 2, 2)[..., ::-1].reshape(w.shape)

    def col(v):
        return v.reshape(-1, 1)

    def heads(w):
        return w[..., by_dimension()]

    upper = np.concatenate([heads(a["attn_Wu_q_w"]), heads(a["attn_Wq_r_w"]), heads(turned(a["attn_Wq_r_w"]))], 1)
    lower = np.concatenate([heads(a["attn_Wu_k_w"]), a["attn_Wu_v_w"][:, by_half()]], 1)
    b1 = a["ffn_b1"].reshape(NE, FC, P).transpose(2, 0, 1).reshape(P, NE * FC)
    weights = np.concatenate([
        a["attn_Wd_q_w"], a["attn_Wd_kv_w"], np.pad(upper, ((0, DQ), (0, 0))), np.pad(lower, ((DQ, 0), (0, 0))),
        heads(a["attn_Wk_r_w"]), heads(turned(a["attn_Wk_r_w"])), a["attn_Wo_w"][by_half()], a["ffn_gate_w"], b1,
        col(np.concatenate([a["attn_Wd_q_b"], a["attn_Wd_kv_b"]])),
        col(heads(a["attn_Wu_q_b"])), col(heads(a["attn_Wq_r_b"])), col(heads(turned(a["attn_Wq_r_b"]))),
        col(heads(a["attn_Wu_k_b"])), col(heads(a["attn_Wk_r_b"])), col(heads(turned(a["attn_Wk_r_b"])))], 1)
    bias_rows = np.concatenate([a["attn_Wu_v_b"][by_half()], a["attn_Wo_b"], a["ffn_gate_b"]])
    w1 = a["ffn_w1"].transpose(1, 0, 2).reshape(P, NE * DF)
    w2 = a["ffn_w2"].reshape(NE, FC, P, D).transpose(2, 0, 1, 3).reshape(P, NE * FC * D)
    arrays = {"x": x, "weights": weights, "bias_rows": bias_rows, "second_bias": a["ffn_b2"].reshape(-1), "w1": w1, "w2": w2,
              "constants": shape_constants(), "rows": result_rows()}
    arrays = {k: np.ascontiguousarray(v) for k, v in arrays.items()}

    nc = bacc.Bacc("TRN2", target_bir_lowering=False, num_devices=1)
    aps = [nc.dram_tensor("in_" + k, v.shape, mybir.dt.from_np(v.dtype), kind="ExternalInput").ap() for k, v in arrays.items()]
    out = nc.dram_tensor("out", (P, NT * D), F32, kind="ExternalOutput").ap()
    build(nc, *aps, out)
    r = run_bass_kernel_spmd(nc, [{"in_" + k: v for k, v in arrays.items()}], core_ids=[0])
    got = r.results[0]["out"]
    return got.reshape(P, NT, D).transpose(1, 0, 2).reshape(NB, S, D)
```

```python
from contextlib import ExitStack

import numpy as np
import concourse.bass as bass
from concourse import mybir

F32 = mybir.dt.float32
BF16 = mybir.dt.bfloat16
U32 = mybir.dt.uint32
I32 = mybir.dt.int32
ALU = mybir.AluOpType
ACT = mybir.ActivationFunctionType
AX = mybir.AxisListType

P = 128
NB, S, D = 16, 256, 128
H, HD = 16, 8
DQ = 64
NE, DF, TOPK = 24, 512, 2
FC = DF // P
QT = S // P
T = NB * S
NT = T // P
NG = 4
NQ = H // NG
NP = 3
QW = NG * HD
KR = NP * NP * HD
SCALE = float(H + 2 * DQ) ** -0.5
EPS = 1e-5
REG = T + P
ROWW = D + 4
TILES = (TOPK * T + NE * (P - 1)) // P
UNROLL, SLOTS = 8, 8
TILES = -(-TILES // UNROLL) * UNROLL
CHUNK = 4
PADR = 1 + QT
PLAN = 13

C_ID, C_TRI, C_ONE = 0, P, 2 * P
C_COS = 3 * P
C_SIN = C_COS + 2 * S
C_EXP = C_SIN + 2 * S
C_BASE = C_EXP + NE
C_PART = C_BASE + NE
C_PAD = C_PART + 1
NCONST = C_PAD + 1

W_D = 0
W_U = W_D + P
W_KR = W_U + 5 * P
W_O = W_KR + 2 * P
W_G = W_O + P
W_B1 = W_G + NE
W_B = W_B1 + NE * FC
NW = W_B + 7
R_V, R_O, R_G = 0, P, 2 * P
NR = R_G + NE


def by_dimension():
    return np.arange(D).reshape(H, HD).T.reshape(-1)


def by_half():
    return np.arange(D).reshape(H // 8, NG, 2, HD).transpose(0, 2, 1, 3).reshape(-1)


def shape_constants():
    c = np.zeros((P, NCONST), np.float32)
    p = np.arange(P)
    c[:, C_ID:C_ID + P] = np.eye(P)
    c[:, C_TRI:C_TRI + P] = p[:, None] < p[None, :]
    c[:, C_ONE:C_ONE + P] = 1.0
    ids = np.arange(D // 2, dtype=np.float32)
    theta = (np.float32(10000.0) ** (np.float32(-2.0) * ids) / np.float32(D // 2)).astype(np.float32)
    angle = (np.arange(S, dtype=np.float32)[:, None] * theta[None, :]).astype(np.float32)
    cos = np.repeat(np.cos(angle).astype(np.float32).T, 2, axis=0)
    sin = np.repeat(np.sin(angle).astype(np.float32).T, 2, axis=0)
    sin[0::2] *= -1.0
    cos, sin = cos[by_dimension()], sin[by_dimension()]
    for i in range(2):
        c[:, C_COS + i * S:C_COS + (i + 1) * S] = cos
        c[:, C_SIN + i * S:C_SIN + (i + 1) * S] = sin
    c[:, C_EXP:C_EXP + NE] = np.arange(NE)
    c[:, C_BASE:C_BASE + NE] = np.arange(NE) * REG
    c[:, C_PART] = p
    c[:, C_PAD] = TOPK * T
    return c


def result_rows():
    p, t, k = np.ogrid[0:P, 0:NT, 0:TOPK]
    return (TOPK * (P * t + p) + k).astype(np.uint32).reshape(P, NT * TOPK)


def build(nc, x_in, w_in, r_in, b2_in, w1_in, w2_in, c_in, rows_in, out):
    with ExitStack() as ctx:
        def sb(name, shape, dt=F32):
            return ctx.enter_context(nc.sbuf_tensor(name, shape, dt))

        def ps(name, shape):
            return ctx.enter_context(nc.psum_tensor(name, shape, F32))

        def sem(name):
            return ctx.enter_context(nc.semaphore(name))

        dispatched = nc.dram_tensor("dispatched", ((NE + 1) * REG, ROWW), F32, kind="Internal").ap()
        parts_out = nc.dram_tensor("parts_out", (2, NP, D * S), BF16, kind="Internal").ap()
        results = nc.dram_tensor("results", (TOPK * T, D), F32, kind="Internal").ap()

        x_all = sb("x_all", [P, NT, D])
        consts = sb("consts", [P, NCONST])
        wts = sb("wts", [P, NW])
        brow = sb("brow", [P, NR])
        w1 = sb("w1", [P, NE, DF + D])
        w2 = sb("w2", [P, NE, FC, D])
        rows = sb("rows", [P, NT, TOPK], U32)
        top_all = sb("top_all", [P, NT, TOPK])
        tri16 = sb("tri16", [P, P], BF16)
        one16 = sb("one16", [P, P], BF16)
        ident16 = sb("ident16", [P, P], BF16)
        powers = sb("powers", [P, 2, NT])
        biasqk = sb("biasqk", [P, 2, S])

        st1 = sb("st1", [P, NT, 6])
        mv1 = sb("mv1", [P, NT, 2])
        ve1 = sb("ve1", [P, NT])
        rstd1 = sb("rstd1", [P, NT])
        xn = sb("xn", [P, QT, D])
        xnT = sb("xnT", [P, S])
        ct = sb("ct", [P, S])
        turn1 = sb("turn1", [P, 2 * S])
        turn2 = sb("turn2", [P, 2 * S])
        qk = sb("qk", [P, 2 * S])
        rest = sb("rest", [P, 2 * S])
        weighed_sb = rest[:, :].rearrange("p (r s) -> p r s", r=2)
        qkp = sb("qkp", [P, 2, NP, S], BF16)
        vst = sb("vst", [P, QT, D])
        vm = [sb(f"vm{i}", [P, QT, NQ, NG * 2 * QW]) for i in range(2)]
        mx = [sb(f"mx{i}", [P, QT, NG]) for i in range(2)]
        mrest = sb("mrest", [P, QT, NG])
        mxp = [sb(f"mxp{i}", [P, QT, NP, NG], BF16) for i in range(2)]
        mrow = [sb(f"mrow{i}", [NP * NG, S], BF16) for i in range(2)]
        pr = [sb(f"pr{i}", [P, NG, QT, S]) for i in range(2)]
        sums = sb("sums", [P, S])
        outT = sb("outT", [P, S])
        spread = w2[:, :, :, :].rearrange("p e c d -> p (e c d)")[:, 0:2 * H * S].bitcast(BF16).rearrange(
            "p (i z h s) -> p i z h s", i=2, z=2, h=H)
        qrows = [spread[:, i, 0, :, :] for i in range(2)]
        krows = [spread[:, i, 1, :, :] for i in range(2)]

        st2 = sb("st2", [P, QT, 6])
        mv2 = sb("mv2", [P, QT, 2])
        ve2 = sb("ve2", [P, QT])
        rstd2 = sb("rstd2", [P, QT])
        pay = sb("pay", [P, QT, TOPK, ROWW])
        xn2T = sb("xn2T", [P, S])
        sc = sb("sc", [P, QT, NE])
        top8 = sb("top8", [P, QT, 8])
        arg8 = sb("arg8", [P, QT, 8], U32)
        argf = sb("argf", [P, QT, TOPK])
        oh = sb("oh", [P, QT * TOPK, NE])
        chosen = sb("chosen", [P, QT, NE], BF16)
        rk = [sb(f"rk{i}", [P, QT + 1, NE]) for i in range(2)]
        ohrk = sb("ohrk", [P, QT * TOPK, NE])
        posf = sb("posf", [P, QT * TOPK])
        pos = sb("pos", [P, QT * TOPK], U32)

        count = sb("count", [P, 3, NE])
        counti = sb("counti", [P, NE], I32)
        past = sb("past", [P, 2, NE])
        spot = sb("spot", [P, 4])
        table = sb("table", [1, 2, P], I32)
        ends = sb("ends", [1, NE], I32)
        padt = qkp[:, :, :, :].rearrange("p z i s -> p (z i s)")[:, 0:2 * PADR * ROWW].bitcast(F32).rearrange(
            "p (k w) -> p k w", k=PADR)
        warm = sb("warm", [P, 1])
        gates = sb("gates", [P, NT, TOPK])
        gtmp = sb("gtmp", [P, 2, NT])
        tin = [sb(f"tin{i}", [P, ROWW]) for i in range(SLOTS)]
        ridx = [sb(f"ridx{i}", [P, 1], U32) for i in range(SLOTS)]
        tT = [turn1[:, 0:P], turn2[:, 0:P]]
        w1s = [vm[i // 2][:, :, :, :].rearrange("p t j f -> p (t j f)")[:, i % 2 * (DF + D):(i % 2 + 1) * (DF + D)]
               for i in range(4)]
        hT = [pr[i][:, :, 0, 0:P] for i in range(2)]
        yo = [sb(f"yo{i}", [P, D]) for i in range(SLOTS)]

        s1 = [ps(f"s1_{i}", [P, QT, S]) for i in range(2)]
        s2 = [ps(f"s2_{i}", [P, QT, S]) for i in range(2)]
        pv = ps("pv", [P, 2, S])
        pa = ps("pa", [P, 512])
        pm = ps("pm", [P, 512])
        pb = ps("pb", [P, 512])

        tps = [pa, pb]
        hps = s2
        yps = s1

        lead_banks = [pa, *(bank[:, :, :].rearrange("p t s -> p (t s)") for bank in s2)]

        def own_columns(i, first):
            v = vm[i][:, :, :, :]
            return bass.AP(tensor=v.tensor, offset=v.offset + first,
                           ap=[v.ap[0], [NG * 2 * QW, QT * NQ], [2 * QW + HD, NG], [1, HD]])

        ident = consts[:, C_ID:C_ID + P]
        mturn = pm[0:NP * NG, 0:S]
        IN_USE = 2 * H * S // DF
        SPREAD = 16 * (NP + 1)

        ld_x0, ld_id, ld_c, ld_w, ld_x, ld_r, ld_w1, ld_b2, ld_w2 = (sem(n) for n in (
            "ld_x0", "ld_id", "ld_c", "ld_w", "ld_x", "ld_r", "ld_w1", "ld_b2", "ld_w2"))
        set_v, set_p, bias_st = sem("set_v"), sem("set_p"), sem("bias_st")
        id_done = sem("id_done")
        pad_st = sem("pad_st")
        s1_full, max_done, split_st, split_done = sem("s1_full"), sem("max_done"), sem("split_st"), sem("split_done")
        mt_full, mt_done = sem("mt_full"), sem("mt_done")
        sums_done, nums_done, inv_st, pv_done = sem("sums_done"), sem("nums_done"), sem("inv_st"), sem("pv_done")
        max_in = [sem(f"max_in{j}") for j in range(NQ)]
        part1_done, rest_done = sem("part1_done"), sem("rest_done")
        part2_done, part3_done = sem("part2_done"), sem("part3_done")
        stored_parts, spread_in, neg_st = sem("stored_parts"), sem("spread_in"), sem("neg_st")
        s2_full, exp_done, pv_full, norm_st = sem("s2_full"), sem("exp_done"), sem("pv_full"), sem("norm_st")
        ln1_st, rstd1_st, xn_done, xb_done = sem("ln1_st"), sem("rstd1_st"), sem("xn_done"), sem("xb_done")
        xT_full, xT_done, ct_full, ct_done = sem("xT_full"), sem("xT_done"), sem("ct_full"), sem("ct_done")
        r1_full, r1_done, r2_full, r2_done = sem("r1_full"), sem("r1_done"), sem("r2_full"), sem("r2_done")
        turn_st, qk_full, qk_done = sem("turn_st"), sem("qk_full"), sem("qk_done")
        v_full, vst_done, v_done = sem("v_full"), sem("vst_done"), sem("v_done")
        wo_full, x2_done, xn2_done = sem("wo_full"), sem("x2_done"), sem("xn2_done")
        ln2_st, rstd2_st = sem("ln2_st"), sem("rstd2_st")
        centred, twin_done, xc_done = sem("centred"), sem("twin_done"), sem("xc_done")
        x2T_full, x2T_done, gate_full, sc_done = sem("x2T_full"), sem("x2T_done"), sem("gate_full"), sem("sc_done")
        top_st, chosen_done, rank_full, rank_done = sem("top_st"), sem("chosen_done"), sem("rank_full"), sem("rank_done")
        pos_st, idx_done, sent = sem("pos_st"), sem("idx_done"), sem("sent")
        plan_st, table_full, table_done = sem("plan_st"), sem("table_full"), sem("table_done")
        pads_out, ends_done = sem("pads_out"), sem("ends_done")
        gate_st, gexp_done = sem("gate_st"), sem("gexp_done")
        tile_in = [sem(f"tile_in{i}") for i in range(SLOTS)]
        tile_out = [sem(f"tile_out{i}") for i in range(SLOTS)]
        tT_full, tT_done, ridx_done, w1_done = sem("tT_full"), sem("tT_done"), sem("ridx_done"), sem("w1_done")
        h_full, gelu_done, y_full, y_done = sem("h_full"), sem("gelu_done"), sem("y_full"), sem("y_done")
        back = [sem(f"back{i}") for i in range(NT // CHUNK)]
        weighed, summed, stored = sem("weighed"), sem("summed"), sem("stored")
        final = [sem(f"final{i}") for i in range(2)]

        def wait(eng, s, value):
            if isinstance(value, int) and value <= 0:
                return
            eng.wait_ge(s, value)

        def known_count(eng, value):
            return value if isinstance(value, int) else eng.compute_val(value)

        def wait_apart(eng, s, value):
            if isinstance(value, int):
                wait(eng, s, value)
                return
            value = known_count(eng, value)
            eng.wait_ge(ld_c, 16)
            eng.wait_ge(s, value)

        def pipeline(eng, step):
            step(0, 0)
            step(1, 1)
            with eng.Fori(0, (NB - 6) // 2) as i:
                for odd in range(2):
                    step(i * 2 + (2 + odd), odd)
            for b in range(NB - 4, NB + 2):
                step(b, b % 2)

        def tile_pipeline(eng, step):
            turns = TILES // UNROLL
            for k in range(UNROLL):
                step(0, k)
            with eng.Fori(1, turns - 1) as turn:
                for k in range(UNROLL):
                    step(turn, k)
            for k in range(UNROLL + 1):
                step(turns - 1 + k // UNROLL, k % UNROLL)

        def chunk(c):
            n = CHUNK * TOPK * D
            return w1[:, :, :].rearrange("p e f -> p (e f)")[:, c * n:(c + 1) * n].rearrange("p (t k d) -> p t k d", t=CHUNK, k=TOPK)

        class Tile:
            def __init__(self, turn, k, ahead):
                self.n = turn * UNROLL + (k + ahead)
                self.round, self.slot = turn * (UNROLL // SLOTS) + (k + ahead) // SLOTS, (k + ahead) % SLOTS
                self.pair = self.slot % 2
                self.real = not isinstance(self.n, int) or 0 <= self.n < TILES

        def expert_of(eng, tile):
            return eng.value_load(table[0:1, 0, bass.ds(tile.n, 1)], min_val=0, max_val=NE - 1)

        class Held:
            def __init__(self, b):
                known = isinstance(b, int)
                self.attend, self.lead, self.project, self.normalise = (not known or b + i < NB for i in range(4))
                self.route, self.send = (not known or 0 <= b - i < NB for i in (1, 2))

        def leading(b, s, q):
            return (b, s, q + 2) if q < 2 else (b + 1, 1 - s, q - 2)

        def turning(b, s, q):
            return (b, s, q + 1) if q < NQ - 1 else (b + 1, 1 - s, 0)

        SP_PADS = NE // 2

        def pad(eng, first, last):
            eng.wait_ge(ends_done, 1)
            with eng.Fori(0, (last - first) // 4) as i:
                for k in range(4):
                    end = eng.value_load(ends[0:1, bass.ds(i * 4 + (first + k), 1)], min_val=0, max_val=NE * REG - PADR * P)
                    eng.dma_start(dispatched[bass.ds(end, PADR * P), :].rearrange("(p k) w -> p k w", p=P),
                                  padt).then_inc(pads_out, 16)

        block = ctx.enter_context(nc.Block())

        @block.sync
        def _(sp):
            xv = x_in.rearrange("p (t d) -> p t d", t=NT)
            sp.dma_start(x_all[:, 0:2 * QT, :], xv[:, 0:2 * QT, :]).then_inc(ld_x0, 16)
            sp.dma_start(consts[:, 0:C_COS], c_in[:, 0:C_COS]).then_inc(ld_id, 16)
            sp.dma_start(wts[:, 0:W_O], w_in[:, 0:W_O]).then_inc(ld_w, 16)
            sp.dma_start(wts[:, W_O:NW], w_in[:, W_O:NW]).then_inc(ld_w, 16)
            sp.dma_start(consts[:, C_COS:NCONST], c_in[:, C_COS:NCONST]).then_inc(ld_c, 16)
            sp.dma_start(brow[:, :], r_in.partition_broadcast(P)).then_inc(ld_r, 16)
            sp.dma_start(x_all[:, 2 * QT:NT, :], xv[:, 2 * QT:NT, :]).then_inc(ld_x, 16)
            sp.dma_start(rows[:, :, :], rows_in.rearrange("p (t k) -> p t k", t=NT)).then_inc(ld_x, 16)
            w1v = w1_in.rearrange("p (e f) -> p e f", e=NE)
            w2v = w2_in.rearrange("p (e c d) -> p e c d", e=NE, c=FC)

            def store_parts(m):
                done, read = known_count(sp, m + 1), known_count(sp, m * SPREAD)
                wait(sp, part3_done, done)
                wait(sp, spread_in, read)
                sp.dma_start(parts_out.rearrange("z i (p s) -> p (z i) s", s=S),
                             qkp[:, :, :, :].rearrange("p z i s -> p (z i) s")).then_inc(stored_parts, 16)

            def spread_rows(m, s):
                stores, scored = known_count(sp, (m + 1) * 16), known_count(sp, (m - 1) * H)
                wait(sp, stored_parts, stores)
                wait(sp, s2_full, scored)
                q, k = parts_out[0], parts_out[1]
                w = NP * HD
                sp.dma_start(krows[s][0:KR, :, :],
                             k.rearrange("i f -> (i f)")[None, :].broadcast_to([NP, NP * D * S])).then_inc(spread_in, 16)
                for i in range(NP):
                    sp.dma_start(qrows[s][w * i:w * (i + 1), :, :],
                                 q[i][None, :].broadcast_to([NP, D * S])).then_inc(spread_in, 16)

            def add_maxima(m, s, j):
                turned = known_count(sp, m * NQ + (j + 1))
                wait(sp, mt_done, turned)
                sp.dma_start(qrows[s][KR:KR + NP, NG * j:NG * j + NG, :], mrow[j % 2][:, :]).then_inc(max_in[j], 16)

            def step(b, s):
                held = Held(b)
                for q in range(NQ):
                    if held.lead if q == NQ - 1 else held.attend:
                        add_maxima(*turning(b, s, q))
                    if q == 0 and held.lead and not (isinstance(b, int) and b == 0):
                        spread_rows(b + 1, 1 - s)
                    if q == 1 and held.project and not (isinstance(b, int) and b < 2):
                        e = (b - 2) * (NE // (NB - 4))
                        sp.dma_start(w1[:, bass.ds(e, NE // (NB - 4)), 0:DF], w1v[:, bass.ds(e, NE // (NB - 4)), :]).then_inc(ld_w1, 16)
                    if q == 1 and isinstance(b, int) and b < 2:
                        e = slice(b * NE // 2, (b + 1) * NE // 2)
                        sp.dma_start(w1[:, e, DF:DF + D], b2_in.partition_broadcast(P).rearrange("p (e d) -> p e d", e=NE)[:, e, :]
                                     ).then_inc(ld_b2, 16)
                    if q == 1 and isinstance(b, int) and NB - 4 <= b < NB:
                        n = (NE - IN_USE) // 4
                        e = IN_USE + n * (b - (NB - 4))
                        sp.dma_start(w2[:, e:e + n, :, :], w2v[:, e:e + n, :, :]).then_inc(ld_w2, 16)
                if held.project:
                    store_parts(b + 2)

            sp.wait_ge(neg_st, 2)
            store_parts(0)
            spread_rows(0, 0)
            store_parts(1)
            add_maxima(0, 0, 0)
            spread_rows(1, 1)
            pipeline(sp, step)

            def second_weights(first, last):
                for e in range(first, last, 4):
                    sp.dma_start(w2[:, e:e + 4, :, :], w2v[:, e:e + 4, :, :]).then_inc(ld_w2, 16)

            sp.wait_ge(s2_full, NB * H)
            second_weights(0, IN_USE // 2)
            pad(sp, 0, SP_PADS)
            sp.dma_start(dispatched[NE * REG:NE * REG + P, :], padt[:, 0, :]).then_inc(pads_out, 16)
            second_weights(IN_USE // 2, IN_USE)
            sp.wait_ge(table_done, 1)
            sp.wait_ge(sent, QT * TOPK * 16 * NB)

            def step(turn, k):
                t = Tile(turn, k, 0)
                if not t.real:
                    return
                first = sp.value_load(table[0:1, 1, bass.ds(t.n, 1)], min_val=0, max_val=NE * REG)
                wait(sp, ridx_done, t.n - (SLOTS - 1))
                sp.dma_start(tin[t.slot][:, :], dispatched[bass.ds(first, P), :]).then_inc(tile_in[t.slot], 16)

            tile_pipeline(sp, step)
            for u in range(SLOTS):
                sp.wait_ge(tile_out[u], 16 * (TILES // SLOTS))
            sp.wait_ge(w1_done, TILES)
            rv = results.rearrange("(t p k) d -> p t (k d)", p=P, k=TOPK)
            for c in range(NT // CHUNK):
                sp.dma_start(chunk(c).rearrange("p t k d -> p t (k d)"), rv[:, c * CHUNK:(c + 1) * CHUNK, :]).then_inc(back[c], 16)
            ov = out.rearrange("p (t d) -> p t d", t=NT)
            for c in range(NT // CHUNK):
                sp.wait_ge(final[c % 2], c // 2 + 1)
                sp.dma_start(ov[:, c * CHUNK:(c + 1) * CHUNK, :], x_all[:, c * CHUNK:(c + 1) * CHUNK, :]).then_inc(stored, 16)
            sp.wait_ge(stored, 16 * (NT // CHUNK))

        @block.tensor
        def _(pe):
            def pass1(m, s, h):
                if h == 0:
                    wait(pe, spread_in, (m + 1) * SPREAD)
                wait(pe, max_done, m * H + (h - 1))
                for t in range(QT):
                    mm = nc.tensor.matmul(s1[h % 2][:, t, :], qrows[s][0:KR, h, t * P:(t + 1) * P],
                                          krows[s][0:KR, h, :], start=True, stop=True)
                mm.then_inc(s1_full, 1)

            def turn_max(m, s, j):
                wait(pe, split_done, m * NQ + (j + 1))
                wait(pe, mt_done, m * NQ + j)
                for t in range(QT):
                    mm = nc.tensor.matmul(mturn[:, t * P:(t + 1) * P], mxp[j % 2][:, t, :, :].rearrange("p i g -> p (i g)"),
                                          ident16[:, :], start=True, stop=True)
                mm.then_inc(mt_full, 1)

            def pass2(b, s, h):
                if h % NG == 0:
                    wait(pe, max_in[h // NG], (b + 1) * 16)
                wait(pe, exp_done, b * H + (h - 1))
                for t in range(QT):
                    mm = nc.tensor.matmul(s2[h % 2][:, t, :], krows[s][0:KR + NP, h, t * P:(t + 1) * P],
                                          qrows[s][0:KR + NP, h, :], start=True, stop=True)
                mm.then_inc(s2_full, 1)

            def weigh(b, s, h):
                r, i = divmod(h // 2, NG)
                if h == 0:
                    wait(pe, v_done, b + 1)
                    wait(pe, pv_done, b)
                wait(pe, exp_done, b * H + (h + 2))
                for t in range(QT):
                    for c in range(2):
                        mm = nc.tensor.matmul(pv[2 * QW * c:2 * QW * (c + 1), r, :],
                                              vm[s][:, t, 2 * r + c, 2 * QW * i:2 * QW * (i + 1)],
                                              pr[h // NG % 2][:, h % NG + c, t, :],
                                              start=(i == 0 and t == 0), stop=(i == NG - 1 and t == QT - 1), skip_group_check=True)
                mm.then_inc(pv_full, 2)

            def x_turned(b):
                wait(pe, xn_done, b + 1)
                wait(pe, vst_done, b)
                for t in range(QT):
                    mm = nc.tensor.transpose(pb[:, t * P:(t + 1) * P], xn[:, t, :], ident)
                mm.then_inc(xT_full, 1)

            def compress(b):
                wait(pe, xT_done, b + 1)
                nc.tensor.matmul(pb[:, 0:S], wts[:, W_D:W_D + P], xnT[:, :], start=True, stop=True).then_inc(ct_full, 1)

            def rotary(b, turned, full, bank):
                wq = W_U + (1 + turned) * P
                wk = W_KR + turned * P
                nc.tensor.matmul(bank[:, 0:S], wts[:, wq:wq + P], ct[:, :], start=True, stop=True)
                nc.tensor.matmul(bank[:, S:2 * S], wts[:, wk:wk + P], xnT[:, :], start=True, stop=True).then_inc(full, 1)

            def plain(b, bank):
                nc.tensor.matmul(bank[:, 0:S], wts[:, W_U:W_U + P], ct[:, :], start=True, stop=True)
                nc.tensor.matmul(bank[:, S:2 * S], wts[:, W_U + 3 * P:W_U + 4 * P], ct[:, :], start=True, stop=True).then_inc(qk_full, 1)

            def values(b):
                for t in range(QT):
                    mm = nc.tensor.matmul(pb[:, t * P:(t + 1) * P], ct[:, t * P:(t + 1) * P],
                                          wts[:, W_U + 4 * P:W_U + 5 * P], start=True, stop=True)
                mm.then_inc(v_full, 1)

            def project_out(b):
                wait(pe, norm_st, b + 1)
                wait(pe, rank_done, b + 1)
                for t in range(QT):
                    mm = nc.tensor.matmul(pa[:, t * P:(t + 1) * P], outT[:, t * P:(t + 1) * P],
                                          wts[:, W_O:W_O + P], start=True, stop=True)
                mm.then_inc(wo_full, 1)

            def x2_turned(b, s):
                wait(pe, xn2_done, b + 1)
                for t in range(QT):
                    mm = nc.tensor.transpose(pa[:, t * P:(t + 1) * P], pay[:, t, 0, 0:D], ident)
                mm.then_inc(x2T_full, 1)

            def gate(b):
                wait(pe, x2T_done, b + 1)
                for t in range(QT):
                    mm = nc.tensor.matmul(pa[:, t * NE:(t + 1) * NE], xn2T[:, t * P:(t + 1) * P],
                                          wts[:, W_G:W_G + NE], start=True, stop=True)
                mm.then_inc(gate_full, 1)

            def rank(b):
                wait(pe, chosen_done, b + 1)
                w = QT * NE
                nc.tensor.matmul(pa[:, 0:w], tri16[:, :], chosen[:, :, :].rearrange("p t e -> p (t e)"),
                                 start=True, stop=False, skip_group_check=True)
                nc.tensor.matmul(pa[:, NE:w], one16[:, :], chosen[:, 0, :], start=False, stop=False, skip_group_check=True)
                nc.tensor.matmul(pa[:, w:w + NE], one16[:, :], chosen[:, 0, :], start=False, stop=False, skip_group_check=True)
                nc.tensor.matmul(pa[:, w:w + NE], one16[:, :], chosen[:, 1, :], start=False, stop=True,
                                 skip_group_check=True).then_inc(rank_full, 1)

            def step(b, s):
                held = Held(b)
                for h in range(H):
                    q, g = divmod(h, NG)
                    if held.attend if q < 2 else held.lead:
                        m, ms, j = leading(b, s, q)
                        pass1(m, ms, NG * j + g)
                    if held.attend:
                        pass2(b, s, h)
                    if g == 1 and (held.lead if q == NQ - 1 else held.attend):
                        turn_max(*turning(b, s, q))
                    if held.send and (q, g) == (1, 1):
                        rank(b - 2)
                    if held.project and (q, g) == (0, 1):
                        x_turned(b + 2)
                    if g % 2 == 1:
                        if q == 0 and held.route:
                            weigh(b - 1, 1 - s, H - NG + g - 1)
                        elif q > 0 and held.attend:
                            weigh(b, s, h - NG - 1)
                    if held.project:
                        if (q, g) == (0, 2):
                            compress(b + 2)
                        elif (q, g) == (1, 1):
                            wait(pe, ct_done, b + 3)
                            rotary(b + 2, 0, r1_full, pb)
                        elif (q, g) == (2, 0):
                            wait(pe, r1_done, b + 3)
                            rotary(b + 2, 1, r2_full, pb)
                        elif (q, g) == (2, 3):
                            wait(pe, r2_done, b + 3)
                            plain(b + 2, pb)
                        elif (q, g) == (3, 1):
                            wait(pe, qk_done, b + 3)
                            values(b + 2)
                    if held.send:
                        if (q, g) == (0, 0):
                            gate(b - 2)
                    if held.route:
                        if (q, g) == (2, 2):
                            project_out(b - 1)
                        elif (q, g) == (3, 3):
                            x2_turned(b - 1, 1 - s)

            pe.wait_ge(ld_id, 16)
            pe.wait_ge(ld_w, 32)
            for m in range(2):
                x_turned(m)
                compress(m)
                pe.wait_ge(ct_done, m + 1)
                wait(pe, r1_done, m)
                rotary(m, 0, r1_full, lead_banks[0])
                wait(pe, r2_done, m)
                rotary(m, 1, r2_full, lead_banks[1])
                wait(pe, qk_done, m)
                plain(m, lead_banks[2])
                values(m)
            pe.wait_ge(set_v, 7)
            pe.wait_ge(id_done, 1)
            for h in range(NG):
                pass1(0, 0, h)
            turn_max(0, 0, 0)
            for h in range(NG, 2 * NG):
                pass1(0, 0, h)
            pe.wait_ge(qk_done, 2)
            pipeline(pe, step)

            pe.wait_ge(plan_st, PLAN)
            pe.wait_ge(rank_done, NB + 1)
            for i in range(2):
                mm = nc.tensor.transpose(pa[0:1, i * P:(i + 1) * P], spot[:, i:i + 1], ident)
            mm.then_inc(table_full, 1)
            pe.wait_ge(table_done, 1)
            pe.wait_ge(ld_w2, 16 * (4 + IN_USE // 4))

            def turn_tile(t):
                wait(pe, tile_in[t.slot], (t.round + 1) * 16)
                nc.tensor.transpose(tps[t.pair][:, 0:P], tin[t.slot][:, 0:D], ident).then_inc(tT_full, 1)

            def hidden(t):
                wait(pe, tT_done, t.n + 1)
                for c in range(FC):
                    mm = nc.tensor.matmul(hps[t.pair][:, :, :].rearrange("p a s -> p (a s)")[:, c * P:(c + 1) * P],
                                          w1s[t.slot % 4][:, c * P:(c + 1) * P], tT[t.pair], start=True, stop=True)
                mm.then_inc(h_full, 1)

            def result(t, e):
                wait(pe, gelu_done, t.n + 1)
                wait(pe, y_done, t.n - 1)
                for c in range(FC):
                    mm = nc.tensor.matmul(yps[t.pair][:, 0, 0:D], hT[t.pair][:, c, :],
                                          w2[:, bass.ds(e, 1), c, :].rearrange("p o d -> p (o d)"), start=(c == 0), stop=(c == FC - 1))
                mm.then_inc(y_full, 1)

            def tile_step(turn, k):
                after, now, before = Tile(turn, k, 1), Tile(turn, k, 0), Tile(turn, k, -1)
                if before.real:
                    e = expert_of(pe, before)
                if after.real:
                    turn_tile(after)
                if now.real:
                    hidden(now)
                if before.real:
                    result(before, e)

            turn_tile(Tile(0, 0, 0))
            tile_pipeline(pe, tile_step)

        @block.scalar
        def _(act):
            def exponents(b, h):
                if h % NG == 0:
                    wait(act, pv_full, b * H + (h - NG))
                wait(act, s2_full, b * H + (h + 1))
                nc.scalar.activation(pr[h // NG % 2][:, h % NG, :, :], s2[h % 2][:, :, :], ACT.Exp,
                                     scale=SCALE).then_inc(exp_done, 1)

            def take_maxima(m, j):
                wait(act, mt_full, m * NQ + (j + 1))
                if j < 2:
                    wait(act, max_in[j + 2], m * 16)
                else:
                    wait(act, max_in[j - 2], (m + 1) * 16)
                nc.scalar.copy(mrow[j % 2][:, :], mturn).then_inc(mt_done, 1)

            def first_part(b):
                wait(act, qk_done, b + 1)
                wait(act, stored_parts, b * 16)
                nc.scalar.copy(qkp[:, :, 0, :], qk[:, :].rearrange("p (z s) -> p z s", z=2)).then_inc(part1_done, 1)

            def second_part(b):
                wait(act, rest_done, b + 1)
                nc.scalar.copy(qkp[:, :, 1, :], rest[:, :].rearrange("p (z s) -> p z s", z=2)).then_inc(part2_done, 1)

            def take_xT(b):
                wait(act, xT_full, b + 1)
                nc.scalar.copy(xnT[:, :], pb[:, 0:S]).then_inc(xT_done, 1)

            def take_ct(b):
                wait(act, ct_full, b + 1)
                nc.scalar.activation(ct[:, :], pb[:, 0:S], ACT.Identity, bias=wts[:, W_B:W_B + 1]).then_inc(ct_done, 1)

            def take_weighted(b):
                wait(act, pv_full, (b + 1) * H)
                wait(act, part3_done, min(b + 3, NB) if isinstance(b, int) else b + 3)
                nc.scalar.copy(weighed_sb, pv[:, :, :]).then_inc(pv_done, 1)

            def spread_sums(b):
                wait(act, pv_done, b + 1)
                wait(act, norm_st, b)
                for j in range(NQ):
                    r = QW * (2 * (j % 2) + 1)
                    last = nc.scalar.copy(sums[QW * j:QW * (j + 1), :], weighed_sb[r:r + QW, j // 2, :])
                last.then_inc(sums_done, 1)

            def spread_weighted(b):
                wait(act, wo_full, b)
                for j in range(NQ):
                    r = 2 * QW * (j % 2)
                    last = nc.scalar.copy(outT[QW * j:QW * (j + 1), :], weighed_sb[r:r + QW, j // 2, :])
                last.then_inc(nums_done, 1)

            def take_x2T(b):
                wait(act, x2T_full, b + 1)
                nc.scalar.copy(xn2T[:, :], pa[:, 0:S]).then_inc(x2T_done, 1)

            def step(b, s):
                held = Held(b)
                for h in range(H):
                    q, g = divmod(h, NG)
                    if g == 1 and (held.lead if q == NQ - 1 else held.attend):
                        m, _, j = turning(b, s, q)
                        take_maxima(m, j)
                    if held.attend:
                        exponents(b, h)
                    if held.route and (q, g) == (3, 3) and not (isinstance(b, int) and b == NB):
                        take_x2T(b - 1)
                    if held.project:
                        if (q, g) == (0, 1):
                            wait(act, vst_done, b + 2)
                            take_xT(b + 2)
                        elif (q, g) == (0, 3):
                            take_ct(b + 2)
                        elif (q, g) == (3, 1):
                            first_part(b + 2)
                        elif (q, g) == (3, 2):
                            second_part(b + 2)
                    if held.route:
                        if (q, g) == (0, 3):
                            take_weighted(b - 1)
                            spread_sums(b - 1)
                        elif (q, g) == (1, 2):
                            spread_weighted(b - 1)

            act.wait_ge(ld_id, 16)
            nc.scalar.copy(ident16[:, :], ident).then_inc(id_done, 1)
            act.wait_ge(ld_w, 32)
            for m in range(2):
                wait(act, vst_done, m)
                take_xT(m)
                take_ct(m)
                first_part(m)
                second_part(m)
            take_maxima(0, 0)
            pipeline(act, step)

            pad(act, SP_PADS, NE)
            act.wait_ge(gate_st, 1)
            nc.scalar.activation(gtmp[:, 1, :], gtmp[:, 0, :], ACT.Exp).then_inc(gexp_done, 1)
            act.wait_ge(gexp_done, 1)
            nc.scalar.activation(warm[:, :], gtmp[:, 1, 0:1], ACT.Gelu)
            act.wait_ge(table_done, 1)

            def tile_step(turn, k):
                t = Tile(turn, k, 0)
                if not t.real:
                    return
                e = expert_of(act, t)
                wait(act, h_full, t.n + 1)
                for c in range(FC):
                    last = nc.scalar.activation(hT[t.pair][:, c, :], hps[t.pair][:, :, :].rearrange("p a s -> p (a s)")[:, c * P:(c + 1) * P],
                                                ACT.Gelu, bias=wts[:, bass.ds(e * FC + (W_B1 + c), 1)])
                last.then_inc(gelu_done, 1)

            tile_pipeline(act, tile_step)

            act.wait_ge(gate_st, 4)
            for c in range(NT // CHUNK):
                act.wait_ge(back[c], 16)
                for i in range(CHUNK):
                    t = c * CHUNK + i
                    y = chunk(c)[:, i, 1, :]
                    last = nc.scalar.activation(y, y, ACT.Copy, scale=gates[:, t, 1:2])
                last.then_inc(weighed, 1)

        @block.vector
        def _(dve):
            def maximum(m, s, j, g):
                h = NG * j + g
                wait(dve, s1_full, m * H + (h + 1))
                nc.vector.tensor_reduce(mx[j % 2][:, :, g], s1[h % 2][:, :, :], AX.X, ALU.max).then_inc(max_done, 1)

            def split_first(m, j):
                n = m * NQ + j
                wait(dve, max_done, m * H + NG * (j + 1))
                wait(dve, mt_full, n - 1)
                nc.vector.tensor_copy(mxp[j % 2][:, :, 0, :], mx[j % 2][:, :, :]).then_inc(split_st, 1)

            def split_second(m, j):
                x, xp = mx[j % 2][:, :, :], mxp[j % 2]
                wait(dve, split_st, (m * NQ + j) * 3 + 1)
                nc.vector.tensor_tensor(xp[:, :, 1, :], x, xp[:, :, 0, :], ALU.subtract).then_inc(split_st, 1)
                nc.vector.tensor_tensor(mrest[:, :, :], x, xp[:, :, 0, :], ALU.subtract).then_inc(split_st, 1)

            def split_third(m, j):
                xp = mxp[j % 2]
                wait(dve, split_st, (m * NQ + j) * 3 + 3)
                nc.vector.tensor_tensor(xp[:, :, 2, :], mrest[:, :, :], xp[:, :, 1, :], ALU.subtract).then_inc(split_done, 1)

            def split_maxima(m, j):
                split_first(m, j)
                split_second(m, j)
                split_third(m, j)

            def stats_x(first, last):
                for t in range(first, last):
                    nc.vector.bn_stats(st1[:, t, :], x_all[:, t, :]).then_inc(ln1_st, 1)
                dve.wait_ge(ln1_st, first + last)
                for t in range(first, last):
                    nc.vector.bn_aggr(mv1[:, t, :], st1[:, t, :]).then_inc(ln1_st, 1)

            def normalise_x(b):
                dve.wait_ge(rstd1_st, 2 if b < 2 else 4)
                wait(dve, xT_full, b)
                for t in range(QT):
                    last = nc.vector.tensor_scalar(xn[:, t, :], x_all[:, bass.ds(b * QT + t, 1), :].rearrange("p o d -> p (o d)"),
                                                   mv1[:, bass.ds(b * QT + t, 1), 0:1].rearrange("p o d -> p (o d)"),
                                                   rstd1[:, bass.ds(b * QT + t, 1)], ALU.subtract, ALU.mult)
                last.then_inc(xn_done, 1)

            def take_rotary(b, full, turn, col, done, free, bank):
                wait(dve, full, b + 1)
                wait(dve, turn_st, b * 2)
                if free:
                    wait(dve, qk_done, b)
                nc.vector.tensor_tensor(turn[:, :], bank[:, :], consts[:, col:col + 2 * S], ALU.mult).then_inc(done, 1)

            def take_qk(b, bank):
                wait(dve, qk_full, b + 1)
                wait(dve, turn_st, (b + 1) * 2)
                wait(dve, rest_done, b)
                nc.vector.tensor_tensor(qk[:, :], bank[:, :], turn1[:, :], ALU.add).then_inc(qk_done, 1)

            def leave(b):
                wait(dve, part1_done, b + 1)
                wait(dve, part3_done, b)
                nc.vector.tensor_tensor(rest[:, :].rearrange("p (z s) -> p z s", z=2), qk[:, :].rearrange("p (z s) -> p z s", z=2),
                                        qkp[:, :, 0, :], ALU.subtract).then_inc(rest_done, 1)

            def take_values(b):
                wait(dve, v_full, b + 1)
                wait(dve, v_done, b)
                nc.vector.tensor_tensor(vst[:, :, :], pb[:, 0:S].rearrange("p (t d) -> p t d", t=QT),
                                        brow[:, None, R_V:R_V + P].broadcast_to([P, QT, D]), ALU.add).then_inc(vst_done, 1)

            INV = 4

            def invert_sums(b, t):
                if t == 0:
                    wait(dve, sums_done, b + 1)
                some = sums[:, t * S // INV:(t + 1) * S // INV]
                nc.vector.reciprocal(some, some).then_inc(inv_st, 1)

            def normalise_out(b):
                wait(dve, nums_done, b + 1)
                wait(dve, inv_st, (b + 1) * INV)
                nc.vector.tensor_tensor(outT[:, :], outT[:, :], sums[:, :], ALU.mult).then_inc(norm_st, 1)

            def take_out(b):
                wait(dve, wo_full, b + 1)
                wait(dve, xb_done, b + 1)
                xs = x_all[:, bass.ds(b * QT, QT), :]
                nc.vector.tensor_tensor(xs, pa[:, 0:S].rearrange("p (t d) -> p t d", t=QT), xs, ALU.add).then_inc(x2_done, 1)

            def row_stats(b):
                wait_apart(dve, x2_done, b + 1)
                for t in range(QT):
                    nc.vector.bn_stats(st2[:, t, :], x_all[:, bass.ds(b * QT + t, 1), :].rearrange("p o d -> p (o d)")).then_inc(ln2_st, 1)

            def row_means(b):
                wait_apart(dve, ln2_st, b * 2 * QT + QT)
                for t in range(QT):
                    nc.vector.bn_aggr(mv2[:, t, :], st2[:, t, :]).then_inc(ln2_st, 1)

            TOP = 7

            def gate_scores(b):
                wait(dve, gate_full, b + 1)
                nc.vector.tensor_tensor(sc[:, :, :], pa[:, 0:QT * NE].rearrange("p (t e) -> p t e", t=QT),
                                        brow[:, None, R_G:R_G + NE].broadcast_to([P, QT, NE]), ALU.add).then_inc(sc_done, 1)

            def best_scores(b):
                wait_apart(dve, sc_done, b + 1)
                for t in range(QT):
                    nc.vector.max(top8[:, t, :], sc[:, t, :]).then_inc(top_st, 1)

            def best_experts(b):
                wait_apart(dve, top_st, b * TOP + 2)
                for t in range(QT):
                    nc.vector.max_index(arg8[:, t, :], top8[:, t, :], sc[:, t, :]).then_inc(top_st, 1)
                nc.vector.tensor_copy(top_all[:, bass.ds(b * QT, QT), :], top8[:, :, 0:TOPK]).then_inc(top_st, 1)

            def expert_numbers(b):
                wait(dve, top_st, b * TOP + 5)
                nc.vector.tensor_copy(argf[:, :, :], arg8[:, :, 0:TOPK]).then_inc(top_st, 1)

            def mark(b):
                wait(dve, top_st, b * TOP + 6)
                nc.vector.tensor_tensor(oh[:, :, :], argf[:, :, :].rearrange("p t k -> p (t k)")[:, :, None].broadcast_to([P, QT * TOPK, NE]),
                                        consts[:, None, C_EXP:C_EXP + NE].broadcast_to([P, QT * TOPK, NE]), ALU.is_equal).then_inc(top_st, 1)

            def mark_tokens(b):
                wait(dve, top_st, (b + 1) * TOP)
                wait(dve, rank_full, b)
                ov = oh[:, :, :].rearrange("p (t k) e -> p t k e", k=TOPK)
                nc.vector.tensor_tensor(chosen[:, :, :], ov[:, :, 0, :], ov[:, :, 1, :], ALU.add).then_inc(chosen_done, 1)

            POS = 3

            def next_rows(b, s):
                wait(dve, rank_full, b + 1)
                wait(dve, rank_done, b + 1)
                nc.vector.tensor_tensor(rk[s][:, :, :], pa[:, 0:(QT + 1) * NE].rearrange("p (t e) -> p t e", e=NE),
                                        rk[1 - s][:, QT:QT + 1, :].broadcast_to([P, QT + 1, NE]), ALU.add).then_inc(rank_done, 1)

            def choose_rows(b, s):
                wait(dve, rank_done, b + 2)
                nc.vector.tensor_tensor(ohrk[:, :, :].rearrange("p (t k) e -> p t k e", k=TOPK),
                                        oh[:, :, :].rearrange("p (t k) e -> p t k e", k=TOPK),
                                        rk[s][:, 0:QT, None, :].broadcast_to([P, QT, TOPK, NE]), ALU.mult).then_inc(pos_st, 1)

            def sum_rows(b):
                wait(dve, pos_st, b * POS + 1)
                nc.vector.tensor_reduce(posf[:, :], ohrk[:, :, :], AX.X, ALU.add).then_inc(pos_st, 1)

            def place(b):
                wait(dve, pos_st, b * POS + 2)
                nc.vector.tensor_copy(pos[:, :], posf[:, :]).then_inc(pos_st, 1)

            def make_padding():
                dve.wait_ge(stored_parts, NB * 16)
                nc.vector.memset(padt, 0.0).then_inc(pad_st, 1)
                dve.wait_ge(pad_st, 1)
                nc.vector.tensor_copy(padt[:, :, D].bitcast(U32),
                                      consts[:, C_PAD:C_PAD + 1].broadcast_to([P, PADR])).then_inc(pad_st, 1)

            def mark_ends(s):
                dve.wait_ge(pad_st, 2)
                dve.wait_ge(rank_done, NB)
                nc.vector.tensor_copy(ends[:, :], rk[s][0:1, QT, :]).then_inc(ends_done, 1)

            def step(b, s):
                held = Held(b)
                for h in range(H):
                    q, g = divmod(h, NG)
                    straight = isinstance(b, int) and b >= NB
                    if isinstance(b, int) and b == 0 and q < 2 and g == 0:
                        stats_x((10 + 3 * q) * QT, (13 + 3 * q) * QT)
                    if held.project and (q, g) == (3, 2):
                        leave(b + 2)
                    if (q, g) == (3, 0):
                        if held.project:
                            take_qk(b + 2, pb)
                        if held.route:
                            row_means(b - 1)
                    leads = held.attend if q < 2 else held.lead
                    m, ms, j = leading(b, s, q)
                    if leads:
                        maximum(m, ms, j, g)
                        if g == NG - 1:
                            split_first(m, j)
                    if held.send:
                        if (q, g) == (0, 0):
                            gate_scores(b - 2)
                        elif (q, g) == (0, 1):
                            best_scores(b - 2)
                        elif (q, g) == (0, 2):
                            best_experts(b - 2)
                        elif (q, g) == (0, 3):
                            expert_numbers(b - 2)
                        elif (q, g) == (1, 1):
                            next_rows(b - 2, s)
                            if straight:
                                if b == NB:
                                    mark_ends(s)
                                choose_rows(b - 2, s)
                                sum_rows(b - 2)
                                place(b - 2)
                        elif (q, g) == (1, 2) and not straight:
                            sum_rows(b - 2)
                    if held.project:
                        if (q, g) == (1, 2):
                            take_rotary(b + 2, r1_full, turn1, C_COS, r1_done, True, pb)
                        elif (q, g) == (2, 1):
                            take_rotary(b + 2, r2_full, turn2, C_SIN, r2_done, False, pb)
                        elif (q, g) == (3, 3):
                            take_values(b + 2)
                    if held.route:
                        if (q, g) == (1, 1):
                            invert_sums(b - 1, 0)
                            invert_sums(b - 1, 1)
                        elif (q, g) == (1, 3):
                            invert_sums(b - 1, 2)
                        elif (q, g) == (2, 0):
                            invert_sums(b - 1, 3)
                        elif (q, g) == (2, 3):
                            take_out(b - 1)
                    if leads and g == NG - 1:
                        split_second(m, j)
                    if held.send:
                        if (q, g) == (0, 3):
                            mark(b - 2)
                        elif (q, g) == (1, 1) and not straight:
                            choose_rows(b - 2, s)
                        elif (q, g) == (1, 2) and not straight:
                            place(b - 2)
                    if isinstance(b, int) and b == NB - 1 and (q, g) == (2, 0):
                        make_padding()
                    if leads and g == NG - 1:
                        split_third(m, j)
                    if held.send and (q, g) == (0, 3):
                        mark_tokens(b - 2)
                    if held.route:
                        if (q, g) == (2, 0):
                            normalise_out(b - 1)
                        elif (q, g) == (2, 3):
                            row_stats(b - 1)
                        elif (q, g) == (3, 3) and isinstance(b, int) and b == NB:
                            dve.wait_ge(x2T_full, NB)
                            nc.vector.tensor_copy(xn2T[:, :], pa[:, 0:S]).then_inc(x2T_done, 1)

            links = [0]

            def link(ins):
                links[0] += 1
                ins.then_inc(plan_st, 1)
                dve.wait_ge(plan_st, links[0])

            nc.vector.memset(vm[0][:, :, :, :], 0.0).then_inc(set_v, 1)
            nc.vector.memset(pay[:, :, :, D:ROWW], 0.0).then_inc(set_v, 1)
            dve.wait_ge(ld_x0, 16)
            stats_x(0, 2 * QT)
            dve.wait_ge(set_v, 1)
            nc.vector.memset(own_columns(0, QW), 1.0).then_inc(set_v, 1)
            normalise_x(0)
            nc.vector.memset(vm[1][:, :, :, :], 0.0).then_inc(set_v, 1)
            dve.wait_ge(ld_c, 16)
            nc.vector.tensor_copy(tri16[:, :], consts[:, C_TRI:C_TRI + P]).then_inc(set_v, 1)
            nc.vector.tensor_copy(one16[:, :], consts[:, C_ONE:C_ONE + P]).then_inc(set_v, 1)
            nc.vector.tensor_copy(rk[1][:, QT, :], consts[:, C_BASE:C_BASE + NE]).then_inc(rank_done, 1)
            dve.wait_ge(set_v, 4)
            nc.vector.memset(own_columns(1, QW), 1.0).then_inc(set_v, 1)
            dve.wait_ge(ld_w, 32)
            for i in range(2):
                c = W_B + 1 + 3 * i
                nc.vector.tensor_scalar(biasqk[:, i, :], consts[:, C_COS:C_COS + S], wts[:, c + 1:c + 2], wts[:, c:c + 1],
                                        ALU.mult, ALU.add).then_inc(bias_st, 1)
            dve.wait_ge(bias_st, 2)
            for i in range(2):
                c = W_B + 1 + 3 * i
                nc.vector.scalar_tensor_tensor(biasqk[:, i, :], consts[:, C_SIN:C_SIN + S], wts[:, c + 2:c + 3],
                                               biasqk[:, i, :], ALU.mult, ALU.add).then_inc(bias_st, 1)
            take_rotary(0, r1_full, turn1, C_COS, r1_done, True, lead_banks[0])
            normalise_x(1)
            take_rotary(0, r2_full, turn2, C_SIN, r2_done, False, lead_banks[1])
            dve.wait_ge(ld_x, 32)
            stats_x(2 * QT, 4 * QT)
            take_qk(0, lead_banks[2])
            dve.wait_ge(ld_r, 16)
            take_values(0)
            leave(0)
            stats_x(4 * QT, 10 * QT)
            take_rotary(1, r1_full, turn1, C_COS, r1_done, True, lead_banks[0])
            take_rotary(1, r2_full, turn2, C_SIN, r2_done, False, lead_banks[1])
            take_qk(1, lead_banks[2])
            take_values(1)
            leave(1)
            for g in range(NG):
                maximum(0, 0, 0, g)
            split_maxima(0, 0)
            normalise_x(2)
            for g in range(NG):
                maximum(0, 0, 1, g)
            split_maxima(0, 1)
            pipeline(dve, step)

            after = rk[(NB - 1) % 2][:, QT, :]
            dve.wait_ge(rank_done, NB + 1)
            link(nc.vector.tensor_tensor(count[:, 0, :], after, consts[:, C_BASE:C_BASE + NE], ALU.subtract))
            link(nc.vector.tensor_scalar(counti[:, :], count[:, 0, :], float(P - 1), None, ALU.add))
            link(nc.vector.tensor_scalar(counti[:, :], counti[:, :], 7, None, ALU.arith_shift_right))
            link(nc.vector.tensor_copy(count[:, 1, :], counti[:, :]))
            link(nc.vector.tensor_tensor_scan(count[:, 2, :], consts[:, C_ONE:C_ONE + NE], count[:, 1, :], 0.0, ALU.mult, ALU.add))
            part = consts[:, C_PART:C_PART + 1]
            link(nc.vector.tensor_scalar(past[:, 0, :], count[:, 2, :], part, None, ALU.is_le))
            link(nc.vector.tensor_tensor(past[:, 1, :], past[:, 0, :], count[:, 1, :], ALU.mult))
            link(nc.vector.tensor_reduce(spot[:, 2:4], past[:, :, :], AX.X, ALU.add))
            link(nc.vector.tensor_scalar(spot[:, 0:1], spot[:, 2:3], float(NE - 1), None, ALU.min))
            link(nc.vector.tensor_tensor(spot[:, 3:4], part, spot[:, 3:4], ALU.subtract))
            link(nc.vector.tensor_scalar(spot[:, 2:3], spot[:, 2:3], float(REG), None, ALU.mult))
            link(nc.vector.scalar_tensor_tensor(spot[:, 1:2], spot[:, 3:4], float(P), spot[:, 2:3], ALU.mult, ALU.add))
            link(nc.vector.tensor_scalar(spot[:, 1:2], spot[:, 1:2], float(NE * REG), None, ALU.min))
            assert links[0] == PLAN
            dve.wait_ge(table_full, 1)
            nc.vector.tensor_copy(table[:, :, :].rearrange("p a s -> p (a s)"), pa[0:1, 0:2 * P]).then_inc(table_done, 1)
            nc.vector.tensor_tensor(gtmp[:, 0, :], top_all[:, :, 1], top_all[:, :, 0], ALU.subtract).then_inc(gate_st, 1)
            dve.wait_ge(table_done, 1)

            def take_tile(t):
                wait(dve, tT_full, t.n + 1)
                nc.vector.tensor_copy(tT[t.pair], tps[t.pair][:, 0:P]).then_inc(tT_done, 1)
                wait(dve, tile_out[t.slot], t.round * 16)
                nc.vector.tensor_copy(ridx[t.slot][:, :], tin[t.slot][:, D:D + 1].bitcast(U32)).then_inc(ridx_done, 1)

            def take_weights(t, e):
                wait(dve, y_done, t.n - 3)
                nc.vector.tensor_copy(w1s[t.slot % 4], w1[:, bass.ds(e, 1), :].rearrange("p o f -> p (o f)")).then_inc(w1_done, 1)

            def take_result(t):
                wait(dve, y_full, t.n + 1)
                nc.vector.tensor_tensor(yo[t.slot][:, :], yps[t.pair][:, 0, 0:D], w1s[t.slot % 4][:, DF:DF + D], ALU.add).then_inc(y_done, 1)

            def tile_step(turn, k):
                later, after, before = Tile(turn, k, 2), Tile(turn, k, 1), Tile(turn, k, -1)
                if after.real:
                    take_tile(after)
                if later.real:
                    take_weights(later, expert_of(dve, later))
                if before.real:
                    take_result(before)

            dve.wait_ge(ld_b2, 32)
            dve.wait_ge(ld_w1, 16 * (NB - 4))
            for t in (Tile(0, 0, 0), Tile(0, 0, 1)):
                take_weights(t, expert_of(dve, t))
            take_tile(Tile(0, 0, 0))
            tile_pipeline(dve, tile_step)

            dve.wait_ge(gexp_done, 1)
            nc.vector.tensor_scalar(gtmp[:, 0, :], gtmp[:, 1, :], 1.0, None, ALU.add).then_inc(gate_st, 1)
            dve.wait_ge(gate_st, 2)
            nc.vector.reciprocal(gates[:, :, 0], gtmp[:, 0, :]).then_inc(gate_st, 1)
            dve.wait_ge(gate_st, 3)
            nc.vector.tensor_tensor(gates[:, :, 1], gtmp[:, 1, :], gates[:, :, 0], ALU.mult).then_inc(gate_st, 1)
            dve.wait_ge(gate_st, 4)
            for c in range(NT // CHUNK):
                dve.wait_ge(back[c], 16)
                dve.wait_ge(weighed, c + 1)
                y = chunk(c)
                for i in range(CHUNK):
                    t = c * CHUNK + i
                    last = nc.vector.scalar_tensor_tensor(y[:, i, 0, :], y[:, i, 0, :], gates[:, t, 0:1], y[:, i, 1, :],
                                                          ALU.mult, ALU.add)
                last.then_inc(summed, 1)
                if c % 2 == 1:
                    dve.wait_ge(summed, c + 1)
                    xs = x_all[:, c * CHUNK:(c + 1) * CHUNK, :]
                    nc.vector.tensor_tensor(xs, xs, y[:, :, 0, :], ALU.add).then_inc(final[1], 1)

        @block.gpsimd
        def _(pool):
            def deviation(mv, ve, rstd, done, before):
                n = ve.shape[1]
                nc.gpsimd.tensor_tensor(ve, mv, powers[:, 1, 0:n], ALU.add).then_inc(done, 1)
                wait(pool, done, before + 1)
                nc.gpsimd.tensor_tensor(rstd, ve, powers[:, 0, 0:n], ALU.pow).then_inc(done, 1)

            def deviation_rows(b):
                wait(pool, ln2_st, (b + 1) * 2 * QT)
                deviation(mv2[:, :, 1], ve2[:, :], rstd2[:, :], rstd2_st, b * 2)

            def deviation_x(first, last, before):
                pool.wait_ge(ln1_st, 2 * last)
                deviation(mv1[:, first:last, 1], ve1[:, first:last], rstd1[:, first:last], rstd1_st, before)

            def add_out_bias(b):
                wait_apart(pool, xn_done, b + 1)
                xs = x_all[:, bass.ds(b * QT, QT), :]
                nc.gpsimd.tensor_tensor(xs, xs, brow[:, None, R_O:R_O + D].broadcast_to([P, QT, D]), ALU.add).then_inc(xb_done, 1)

            def add_biases(b):
                wait(pool, r1_done, b + 1)
                nc.gpsimd.tensor_tensor(turn1[:, :], turn1[:, :], biasqk[:, :, :].rearrange("p i s -> p (i s)"),
                                        ALU.add).then_inc(turn_st, 1)

            def sum_turns(b):
                wait(pool, r2_done, b + 1)
                wait(pool, turn_st, b * 2 + 1)
                nc.gpsimd.tensor_tensor(turn1[:, :], turn1[:, :], turn2[:, :], ALU.add).then_inc(turn_st, 1)

            def third_part(b):
                wait(pool, part2_done, b + 1)
                nc.gpsimd.tensor_tensor(qkp[:, :, 2, :], rest[:, :].rearrange("p (z s) -> p z s", z=2),
                                        qkp[:, :, 1, :], ALU.subtract).then_inc(part3_done, 1)

            def normalise_rows(b):
                wait_apart(pool, sent, b * (QT * TOPK * 16))
                tokens = [pay[:, :, k, 0:D] for k in range(TOPK)]
                rstd = rstd2[:, :, None].broadcast_to([P, QT, D])
                wait_apart(pool, rstd2_st, (b + 1) * 2)
                nc.gpsimd.tensor_tensor(tokens[1], x_all[:, bass.ds(b * QT, QT), :], mv2[:, :, 0:1].broadcast_to([P, QT, D]),
                                        ALU.subtract).then_inc(centred, 1)
                wait(pool, centred, b + 1)
                nc.gpsimd.tensor_tensor(tokens[0], tokens[1], rstd, ALU.mult).then_inc(xn2_done, 1)

            def twin_rows(b):
                wait(pool, rstd2_st, (b + 1) * 2)
                second = pay[:, :, 1, 0:D]
                nc.gpsimd.tensor_tensor(second, second, rstd2[:, :, None].broadcast_to([P, QT, D]), ALU.mult).then_inc(twin_done, 1)

            def normalise_x(b):
                if isinstance(b, int) and b < 5:
                    pool.wait_ge(rstd1_st, 8 if b == 4 else 6)
                wait_apart(pool, xT_full, b)
                nc.gpsimd.tensor_tensor(xn[:, :, :], x_all[:, bass.ds(b * QT, QT), :],
                                        mv1[:, bass.ds(b * QT, QT), 0:1].broadcast_to([P, QT, D]), ALU.subtract).then_inc(xc_done, 1)
                wait_apart(pool, xc_done, b - 2)
                nc.gpsimd.tensor_tensor(xn[:, :, :], xn[:, :, :], rstd1[:, bass.ds(b * QT, QT), None].broadcast_to([P, QT, D]),
                                        ALU.mult).then_inc(xn_done, 1)

            def give_values(b, s):
                wait(pool, vst_done, b + 1)
                wait_apart(pool, pv_full, (b - 1) * H)
                nc.gpsimd.tensor_copy(own_columns(s, 0),
                                      vst[:, :, :].rearrange("p t (j g d) -> p (t j) g d", j=NQ, g=NG)).then_inc(v_done, 1)

            def send(b, s):
                wait(pool, twin_done, b + 1)
                nc.gpsimd.tensor_copy(pay[:, :, :, D].bitcast(U32),
                                      rows[:, bass.ds(b * QT, QT), :]).then_inc(idx_done, 1)
                wait(pool, idx_done, b + 1)
                if isinstance(b, int) and b == NB - 1:
                    pool.wait_ge(pads_out, 16 * (NE + 1))
                wait_apart(pool, pos_st, (b + 1) * 3)
                for t in range(QT):
                    for k in range(TOPK):
                        n = t * TOPK + k
                        nc.gpsimd.indirect_dma_start(
                            dispatched, bass.IndirectOffsetOnAxis(ap=pos[:, n:n + 1], axis=0),
                            pay[:, t, k, :], None).then_inc(sent, 16)

            def step(b, s):
                held = Held(b)
                if isinstance(b, int) and b == 1:
                    deviation_x(10 * QT, NT, 6)
                if held.project:
                    add_out_bias(b + 2)
                if held.normalise:
                    normalise_x(b + 3)
                if held.lead:
                    give_values(b + 1, 1 - s)
                if held.project:
                    add_biases(b + 2)
                if held.send:
                    send(b - 2, s)
                if held.project:
                    sum_turns(b + 2)
                if held.route:
                    deviation_rows(b - 1)
                    normalise_rows(b - 1)
                if held.project:
                    third_part(b + 2)
                if held.route:
                    twin_rows(b - 1)

            def minus_one(i):
                nc.gpsimd.memset(spread[64:96, i, 1, :, :].rearrange("p h s -> p (h s)"), -1.0).then_inc(neg_st, 1)

            nc.gpsimd.memset(powers[:, 0, :], -0.5).then_inc(set_p, 1)
            nc.gpsimd.memset(powers[:, 1, :], EPS).then_inc(set_p, 1)
            pool.wait_ge(set_p, 2)
            minus_one(0)
            pool.wait_ge(neg_st, 1)
            deviation_x(0, 2 * QT, 0)
            pool.wait_ge(rstd1_st, 2)
            minus_one(1)
            pool.wait_ge(neg_st, 2)
            pool.wait_ge(set_v, 7)
            pool.wait_ge(ld_r, 16)
            pool.wait_ge(bias_st, 4)
            for m in range(2):
                add_out_bias(m)
                add_biases(m)
                sum_turns(m)
                if m == 0:
                    deviation_x(2 * QT, 4 * QT, 2)
                third_part(m)
                if m == 0:
                    give_values(0, 0)
            deviation_x(4 * QT, 10 * QT, 4)
            pool.wait_ge(ld_x, 32)
            pipeline(pool, step)

            def tile_step(turn, k):
                t = Tile(turn, k, -1)
                if not t.real:
                    return
                wait_apart(pool, y_done, t.n + 1)
                nc.gpsimd.indirect_dma_start(results, bass.IndirectOffsetOnAxis(ap=ridx[t.slot][:, 0:1], axis=0),
                                             yo[t.slot][:, :], None, bounds_check=TOPK * T - 1,
                                             oob_is_err=False).then_inc(tile_out[t.slot], 16)

            tile_pipeline(pool, tile_step)
            for c in range(0, NT // CHUNK, 2):
                pool.wait_ge(summed, c + 1)
                xs = x_all[:, c * CHUNK:(c + 1) * CHUNK, :]
                nc.gpsimd.tensor_tensor(xs, xs, chunk(c)[:, :, 0, :], ALU.add).then_inc(final[0], 1)


def kernel(**inputs):
    import concourse.bacc as bacc
    from concourse.bass_utils import run_bass_kernel_spmd

    a = {k.split("_", 1)[1]: np.ascontiguousarray(v) for k, v in inputs.items()}
    x = a["attn_x"].reshape(NT, P, D).transpose(1, 0, 2).reshape(P, NT * D)

    def turned(w):
        return w.reshape(*w.shape[:-1], D // 2, 2)[..., ::-1].reshape(w.shape)

    def col(v):
        return v.reshape(-1, 1)

    def heads(w):
        return w[..., by_dimension()]

    upper = np.concatenate([heads(a["attn_Wu_q_w"]), heads(a["attn_Wq_r_w"]), heads(turned(a["attn_Wq_r_w"]))], 1)
    lower = np.concatenate([heads(a["attn_Wu_k_w"]), a["attn_Wu_v_w"][:, by_half()]], 1)
    b1 = a["ffn_b1"].reshape(NE, FC, P).transpose(2, 0, 1).reshape(P, NE * FC)
    weights = np.concatenate([
        a["attn_Wd_q_w"], a["attn_Wd_kv_w"], np.pad(upper, ((0, DQ), (0, 0))), np.pad(lower, ((DQ, 0), (0, 0))),
        heads(a["attn_Wk_r_w"]), heads(turned(a["attn_Wk_r_w"])), a["attn_Wo_w"][by_half()], a["ffn_gate_w"], b1,
        col(np.concatenate([a["attn_Wd_q_b"], a["attn_Wd_kv_b"]])),
        col(heads(a["attn_Wu_q_b"])), col(heads(a["attn_Wq_r_b"])), col(heads(turned(a["attn_Wq_r_b"]))),
        col(heads(a["attn_Wu_k_b"])), col(heads(a["attn_Wk_r_b"])), col(heads(turned(a["attn_Wk_r_b"])))], 1)
    bias_rows = np.concatenate([a["attn_Wu_v_b"][by_half()], a["attn_Wo_b"], a["ffn_gate_b"]])
    w1 = a["ffn_w1"].transpose(1, 0, 2).reshape(P, NE * DF)
    w2 = a["ffn_w2"].reshape(NE, FC, P, D).transpose(2, 0, 1, 3).reshape(P, NE * FC * D)
    arrays = {"x": x, "weights": weights, "bias_rows": bias_rows, "second_bias": a["ffn_b2"].reshape(-1), "w1": w1, "w2": w2,
              "constants": shape_constants(), "rows": result_rows()}
    arrays = {k: np.ascontiguousarray(v) for k, v in arrays.items()}

    nc = bacc.Bacc("TRN2", target_bir_lowering=False, num_devices=1)
    aps = [nc.dram_tensor("in_" + k, v.shape, mybir.dt.from_np(v.dtype), kind="ExternalInput").ap() for k, v in arrays.items()]
    out = nc.dram_tensor("out", (P, NT * D), F32, kind="ExternalOutput").ap()
    build(nc, *aps, out)
    r = run_bass_kernel_spmd(nc, [{"in_" + k: v for k, v in arrays.items()}], core_ids=[0])
    got = r.results[0]["out"]
    return got.reshape(P, NT, D).transpose(1, 0, 2).reshape(NB, S, D)
```
